# Optimizing a Trainium2 kernel written in Bass

```python
import numpy as np
import jax
import jax.numpy as jnp

def _softmax(x, axis=-1):
    return jax.nn.softmax(x, axis=axis)

def _gelu(x):
    return jax.nn.gelu(x, approximate=True)

def _silu(x):
    return jax.nn.silu(x)

def _sigmoid(x):
    return jax.nn.sigmoid(x)

def _layernorm(x, axis=-1, eps=1e-05):
    m = jnp.mean(x, axis=axis, keepdims=True)
    v = jnp.var(x, axis=axis, keepdims=True)
    return (x - m) / jnp.sqrt(v + eps)

def _scatter_add(tgt, idx, src, axis=0):
    return tgt.at[idx].add(src)

def _segment_sum(src, seg, n):
    return jax.ops.segment_sum(src, seg, n)
kernel_name = 'mk_gnn_preln_d4_gnn_r8_ebe85a'

def setup_inputs(seed: int=0):
    np.random.seed(seed)
    _w = jnp.asarray

    def _rec_inputs():
        import jax
        import jax.numpy as jnp
        _gk = jax.random.key(seed)
        x = -0.0003713 + 1 * jax.random.normal(jax.random.fold_in(_gk, 1), (6250, 128), jnp.float32)
        _s = jax.random.randint(jax.random.fold_in(_gk, 2), (50000,), 0, 6250, jnp.int32)
        _d = jax.random.randint(jax.random.fold_in(_gk, 3), (50000,), 0, 6250, jnp.int32)
        _loop = jnp.arange(6250, dtype=jnp.int32)
        src = jnp.concatenate([_s, _d, _loop])
        dst = jnp.concatenate([_d, _s, _loop])
        _o = jnp.argsort(dst, stable=True)
        src = src[_o]
        dst = dst[_o]
        edge_type_5 = jax.random.randint(jax.random.fold_in(_gk, 13), (106250,), 0, 5, jnp.int32)
        return (x, src, dst, edge_type_5)
    x, src, dst, edge_type_5 = _rec_inputs()

    def _L0_gnn_setup():
        import jax, jax.numpy as jnp
        import numpy as np
        N_NODES = 12500
        N_EDGES = 75000
        D_FEAT = 128
        key = jax.random.key(seed)
        k1, k2, k3 = jax.random.split(key, 3)
        x = jax.random.normal(k1, (N_NODES, D_FEAT), dtype=jnp.float32)
        edge_index = jax.random.randint(k2, (2, N_EDGES), 0, N_NODES, dtype=jnp.int32)
        z_agg_hard = jax.random.uniform(k3, (1, 3), dtype=jnp.float32)
        return {'x': x, 'edge_index': edge_index, 'z_agg_hard': z_agg_hard}
    _L0_gnn_all = _L0_gnn_setup()
    _L0_gnn_in = {k: v for k, v in _L0_gnn_all.items() if k in ('z_agg_hard',)}
    del _L0_gnn_all

    def _L1_gnn_setup():
        import jax, jax.numpy as jnp
        import numpy as np
        N_NODES = 6250
        N_EDGES = 100000
        D_FEAT = 128
        D_OUT = 128
        key = jax.random.key(seed)
        k1, k2, k3, k4, k5 = jax.random.split(key, 5)
        features = jax.random.normal(k1, (N_NODES, D_FEAT), dtype=jnp.float32)
        src = jax.random.randint(k2, (N_EDGES,), 0, N_NODES, dtype=jnp.int32)
        dst = jax.random.randint(k3, (N_EDGES,), 0, N_NODES, dtype=jnp.int32)
        W = jax.random.normal(k4, (2 * D_FEAT, D_OUT), dtype=jnp.float32) / np.sqrt(2.0 * D_FEAT)
        b = jax.random.normal(k5, (D_OUT,), dtype=jnp.float32) * 0.01
        return {'features': features, 'src': src, 'dst': dst, 'W': W, 'b': b}
    _L1_gnn_all = _L1_gnn_setup()
    _L1_gnn_in = {k: v for k, v in _L1_gnn_all.items() if k in ('W', 'b')}
    del _L1_gnn_all

    def _L2_gnn_setup():
        import jax, jax.numpy as jnp
        import numpy as np
        N = 6250
        E = 80000
        HIDDEN = 128
        R = 5
        HEADS = 8
        HEAD_DIM = HIDDEN // HEADS
        LN_EPS = 1e-05

        def _fused_forward(node_embeddings, W_Q, W_K, W_V, attn_bias, out_proj_w, out_proj_b, ln_gamma, ln_beta, edge_index, edge_types):
            src, dst = (edge_index[0], edge_index[1])
            n = node_embeddings.shape[0]
            x_src = node_embeddings[src]
            x_dst = node_embeddings[dst]
            scale = HEAD_DIM ** 0.5
            NEG = jnp.float32(-1000000000.0)
            out = jnp.zeros((n, HEADS, HEAD_DIM), dtype=node_embeddings.dtype)
            for r in range(R):
                mask = edge_types == r
                q = jnp.einsum('eh,khd->ekd', x_dst, W_Q[r])
                k = jnp.einsum('eh,khd->ekd', x_src, W_K[r])
                v = jnp.einsum('eh,khd->ekd', x_src, W_V[r])
                logits = (q * k).sum(-1) / scale + attn_bias[r][None, :]
                masked_logits = jnp.where(mask[:, None], logits, NEG)
                max_v = jax.ops.segment_max(masked_logits, dst, num_segments=n)
                max_v = jnp.maximum(max_v, NEG)
                exp_l = jnp.where(mask[:, None], jnp.exp(masked_logits - max_v[dst]), 0.0)
                sum_exp = jax.ops.segment_sum(exp_l, dst, num_segments=n)
                attn = exp_l / (sum_exp[dst] + 1e-12)
                out = out + jax.ops.segment_sum(attn[:, :, None] * v, dst, num_segments=n)
            out = out.reshape(n, HIDDEN)
            out = out @ out_proj_w.T + out_proj_b
            h = out + node_embeddings
            mu = h.mean(-1, keepdims=True)
            var = ((h - mu) ** 2).mean(-1, keepdims=True)
            return (h - mu) / jnp.sqrt(var + LN_EPS) * ln_gamma + ln_beta
        key = jax.random.key(seed)
        ks = jax.random.split(key, 10)
        bound = float(np.sqrt(6.0 / (HIDDEN + HEAD_DIM)))
        pbound = float(np.sqrt(1.0 / HIDDEN))
        return {'node_embeddings': jax.random.normal(ks[0], (N, HIDDEN), dtype=jnp.float32), 'edge_index': jax.random.randint(ks[1], (2, E), 0, N, dtype=jnp.int64), 'edge_types': jax.random.randint(ks[2], (E,), 0, R, dtype=jnp.int64), 'W_Q': jax.random.uniform(ks[3], (R, HEADS, HIDDEN, HEAD_DIM), minval=-bound, maxval=bound, dtype=jnp.float32), 'W_K': jax.random.uniform(ks[4], (R, HEADS, HIDDEN, HEAD_DIM), minval=-bound, maxval=bound, dtype=jnp.float32), 'W_V': jax.random.uniform(ks[5], (R, HEADS, HIDDEN, HEAD_DIM), minval=-bound, maxval=bound, dtype=jnp.float32), 'attn_bias': jnp.zeros((R, HEADS), dtype=jnp.float32), 'out_proj_w': jax.random.uniform(ks[6], (HIDDEN, HIDDEN), minval=-pbound, maxval=pbound, dtype=jnp.float32), 'out_proj_b': jax.random.uniform(ks[7], (HIDDEN,), minval=-pbound, maxval=pbound, dtype=jnp.float32), 'ln_gamma': jnp.ones((HIDDEN,), dtype=jnp.float32), 'ln_beta': jnp.zeros((HIDDEN,), dtype=jnp.float32)}
    _L2_gnn_all = _L2_gnn_setup()
    _L2_gnn_in = {k: v for k, v in _L2_gnn_all.items() if k in ('W_Q', 'W_K', 'W_V', 'attn_bias', 'out_proj_w', 'out_proj_b', 'ln_gamma', 'ln_beta')}
    del _L2_gnn_all

    def _L3_gnn_setup():
        import jax, jax.numpy as jnp
        import numpy as np
        N = 12500
        E = 200000
        IN = 128
        OUT = 128
        H = 4
        FH = OUT // H
        EPS = 1e-05
        NEG_SLOPE = 0.2

        def _gat(x, src, dst, W, a_src, a_dst, b):
            n = x.shape[0]
            xw = (x @ W).reshape(n, H, FH)
            al_s = jnp.einsum('nhf,hf->nh', xw, a_src)
            al_d = jnp.einsum('nhf,hf->nh', xw, a_dst)
            e = jax.nn.leaky_relu(al_s[src] + al_d[dst], NEG_SLOPE)
            m = jax.ops.segment_max(e, dst, num_segments=n)
            ee = jnp.exp(e - m[dst])
            den = jax.ops.segment_sum(ee, dst, num_segments=n)
            alpha = ee / den[dst]
            out = jax.ops.segment_sum(alpha[:, :, None] * xw[src], dst, num_segments=n)
            return out.reshape(n, H * FH) + b

        def _bn(x, gamma, beta):
            mu = x.mean(0)
            var = x.var(0)
            return gamma * (x - mu) * jax.lax.rsqrt(var + EPS) + beta
        key = jax.random.key(seed)
        ks = jax.random.split(key, 10)
        x = jax.random.normal(ks[0], (N, IN), jnp.float32)
        edge_index = jax.random.randint(ks[1], (2, E), 0, N, dtype=jnp.int32)
        W1 = jax.random.normal(ks[2], (IN, OUT), jnp.float32) / np.float32(np.sqrt(IN))
        a1_src = jax.random.normal(ks[3], (H, FH), jnp.float32) * 0.1
        a1_dst = jax.random.normal(ks[4], (H, FH), jnp.float32) * 0.1
        b1 = jnp.zeros((OUT,), jnp.float32)
        g1 = jnp.ones((OUT,), jnp.float32)
        beta1 = jnp.zeros((OUT,), jnp.float32)
        W2 = jax.random.normal(ks[5], (OUT, OUT), jnp.float32) / np.float32(np.sqrt(OUT))
        a2_src = jax.random.normal(ks[6], (H, FH), jnp.float32) * 0.1
        a2_dst = jax.random.normal(ks[7], (H, FH), jnp.float32) * 0.1
        b2 = jnp.zeros((OUT,), jnp.float32)
        g2 = jnp.ones((OUT,), jnp.float32)
        beta2 = jnp.zeros((OUT,), jnp.float32)
        return dict(x=x, edge_index=edge_index, W1=W1, a1_src=a1_src, a1_dst=a1_dst, b1=b1, g1=g1, beta1=beta1, W2=W2, a2_src=a2_src, a2_dst=a2_dst, b2=b2, g2=g2, beta2=beta2)
    _L3_gnn_all = _L3_gnn_setup()
    _L3_gnn_in = {k: v for k, v in _L3_gnn_all.items() if k in ('W1', 'a1_src', 'a1_dst', 'b1', 'g1', 'beta1', 'W2', 'a2_src', 'a2_dst', 'b2', 'g2', 'beta2')}
    del _L3_gnn_all
    return {'x': x, 'src': src, 'dst': dst, 'edge_type_5': edge_type_5, 'L0_gnn_z_agg_hard': _L0_gnn_in['z_agg_hard'], 'L1_gnn_W': _L1_gnn_in['W'], 'L1_gnn_b': _L1_gnn_in['b'], 'L2_gnn_W_Q': _L2_gnn_in['W_Q'], 'L2_gnn_W_K': _L2_gnn_in['W_K'], 'L2_gnn_W_V': _L2_gnn_in['W_V'], 'L2_gnn_attn_bias': _L2_gnn_in['attn_bias'], 'L2_gnn_out_proj_w': _L2_gnn_in['out_proj_w'], 'L2_gnn_out_proj_b': _L2_gnn_in['out_proj_b'], 'L2_gnn_ln_gamma': _L2_gnn_in['ln_gamma'], 'L2_gnn_ln_beta': _L2_gnn_in['ln_beta'], 'L3_gnn_W1': _L3_gnn_in['W1'], 'L3_gnn_a1_src': _L3_gnn_in['a1_src'], 'L3_gnn_a1_dst': _L3_gnn_in['a1_dst'], 'L3_gnn_b1': _L3_gnn_in['b1'], 'L3_gnn_g1': _L3_gnn_in['g1'], 'L3_gnn_beta1': _L3_gnn_in['beta1'], 'L3_gnn_W2': _L3_gnn_in['W2'], 'L3_gnn_a2_src': _L3_gnn_in['a2_src'], 'L3_gnn_a2_dst': _L3_gnn_in['a2_dst'], 'L3_gnn_b2': _L3_gnn_in['b2'], 'L3_gnn_g2': _L3_gnn_in['g2'], 'L3_gnn_beta2': _L3_gnn_in['beta2']}

def reference(x, src, dst, edge_type_5, L0_gnn_z_agg_hard, L1_gnn_W, L1_gnn_b, L2_gnn_W_Q, L2_gnn_W_K, L2_gnn_W_V, L2_gnn_attn_bias, L2_gnn_out_proj_w, L2_gnn_out_proj_b, L2_gnn_ln_gamma, L2_gnn_ln_beta, L3_gnn_W1, L3_gnn_a1_src, L3_gnn_a1_dst, L3_gnn_b1, L3_gnn_g1, L3_gnn_beta1, L3_gnn_W2, L3_gnn_a2_src, L3_gnn_a2_dst, L3_gnn_b2, L3_gnn_g2, L3_gnn_beta2):
    import jax
    import jax.numpy as jnp

    def _L0_gnn_ref(x, edge_index, z_agg_hard):
        import jax, jax.numpy as jnp
        import numpy as np
        N_NODES = 12500
        N_EDGES = 75000
        D_FEAT = 128
        N = x.shape[0]
        dst = edge_index[0]
        src = edge_index[1]
        msg = x[src]
        s_add = jax.ops.segment_sum(msg, dst, num_segments=N)
        cnt = jax.ops.segment_sum(jnp.ones((msg.shape[0],), dtype=x.dtype), dst, num_segments=N)
        s_mean = s_add / jnp.maximum(cnt, 1.0)[:, None]
        s_max = jax.ops.segment_max(msg, dst, num_segments=N)
        s_max = jnp.where(cnt[:, None] > 0, s_max, jnp.zeros_like(s_max))
        stacked = jnp.stack([s_add, s_mean, s_max], axis=0)
        out = jnp.einsum('ij,jkl->ikl', z_agg_hard, stacked)[0]
        return out

    def _L1_gnn_ref(features, src, dst, W, b):
        import jax, jax.numpy as jnp
        import numpy as np
        N_NODES = 6250
        N_EDGES = 100000
        D_FEAT = 128
        D_OUT = 128
        n = features.shape[0]
        msg_sum = jax.ops.segment_sum(features[src], dst, num_segments=n)
        deg = jax.ops.segment_sum(jnp.ones_like(dst, dtype=features.dtype), dst, num_segments=n)
        h = msg_sum / jnp.maximum(deg, 1.0)[:, None]
        h_concat = jnp.concatenate([features, h], axis=1)
        return h_concat @ W + b

    def _L2_gnn_ref(node_embeddings, edge_index, edge_types, W_Q, W_K, W_V, attn_bias, out_proj_w, out_proj_b, ln_gamma, ln_beta):
        import jax, jax.numpy as jnp
        import numpy as np
        N = 6250
        E = 80000
        HIDDEN = 128
        R = 5
        HEADS = 8
        HEAD_DIM = HIDDEN // HEADS
        LN_EPS = 1e-05

        def _fused_forward(node_embeddings, W_Q, W_K, W_V, attn_bias, out_proj_w, out_proj_b, ln_gamma, ln_beta, edge_index, edge_types):
            src, dst = (edge_index[0], edge_index[1])
            n = node_embeddings.shape[0]
            x_src = node_embeddings[src]
            x_dst = node_embeddings[dst]
            scale = HEAD_DIM ** 0.5
            NEG = jnp.float32(-1000000000.0)
            out = jnp.zeros((n, HEADS, HEAD_DIM), dtype=node_embeddings.dtype)
            for r in range(R):
                mask = edge_types == r
                q = jnp.einsum('eh,khd->ekd', x_dst, W_Q[r])
                k = jnp.einsum('eh,khd->ekd', x_src, W_K[r])
                v = jnp.einsum('eh,khd->ekd', x_src, W_V[r])
                logits = (q * k).sum(-1) / scale + attn_bias[r][None, :]
                masked_logits = jnp.where(mask[:, None], logits, NEG)
                max_v = jax.ops.segment_max(masked_logits, dst, num_segments=n)
                max_v = jnp.maximum(max_v, NEG)
                exp_l = jnp.where(mask[:, None], jnp.exp(masked_logits - max_v[dst]), 0.0)
                sum_exp = jax.ops.segment_sum(exp_l, dst, num_segments=n)
                attn = exp_l / (sum_exp[dst] + 1e-12)
                out = out + jax.ops.segment_sum(attn[:, :, None] * v, dst, num_segments=n)
            out = out.reshape(n, HIDDEN)
            out = out @ out_proj_w.T + out_proj_b
            h = out + node_embeddings
            mu = h.mean(-1, keepdims=True)
            var = ((h - mu) ** 2).mean(-1, keepdims=True)
            return (h - mu) / jnp.sqrt(var + LN_EPS) * ln_gamma + ln_beta
        return _fused_forward(node_embeddings, W_Q, W_K, W_V, attn_bias, out_proj_w, out_proj_b, ln_gamma, ln_beta, edge_index, edge_types)

    def _L3_gnn_ref(x, edge_index, W1, a1_src, a1_dst, b1, g1, beta1, W2, a2_src, a2_dst, b2, g2, beta2):
        import jax, jax.numpy as jnp
        import numpy as np
        N = 12500
        E = 200000
        IN = 128
        OUT = 128
        H = 4
        FH = OUT // H
        EPS = 1e-05
        NEG_SLOPE = 0.2

        def _gat(x, src, dst, W, a_src, a_dst, b):
            n = x.shape[0]
            xw = (x @ W).reshape(n, H, FH)
            al_s = jnp.einsum('nhf,hf->nh', xw, a_src)
            al_d = jnp.einsum('nhf,hf->nh', xw, a_dst)
            e = jax.nn.leaky_relu(al_s[src] + al_d[dst], NEG_SLOPE)
            m = jax.ops.segment_max(e, dst, num_segments=n)
            ee = jnp.exp(e - m[dst])
            den = jax.ops.segment_sum(ee, dst, num_segments=n)
            alpha = ee / den[dst]
            out = jax.ops.segment_sum(alpha[:, :, None] * xw[src], dst, num_segments=n)
            return out.reshape(n, H * FH) + b

        def _bn(x, gamma, beta):
            mu = x.mean(0)
            var = x.var(0)
            return gamma * (x - mu) * jax.lax.rsqrt(var + EPS) + beta
        n = x.shape[0]
        loops = jnp.arange(n, dtype=edge_index.dtype)
        src = jnp.concatenate([edge_index[0], loops])
        dst = jnp.concatenate([edge_index[1], loops])
        h = jax.nn.elu(_bn(_gat(x, src, dst, W1, a1_src, a1_dst, b1), g1, beta1))
        h = jax.nn.elu(_bn(_gat(h, src, dst, W2, a2_src, a2_dst, b2), g2, beta2))
        return h
    edge_index = jnp.stack([src, dst])
    h = jnp.maximum(_layernorm(x, axis=-1), 0.0)
    x = x + _L0_gnn_ref(h, edge_index, L0_gnn_z_agg_hard)
    h = jnp.maximum(_layernorm(x, axis=-1), 0.0)
    x = x + _L1_gnn_ref(h, src, dst, L1_gnn_W, L1_gnn_b)
    h = jnp.maximum(_layernorm(x, axis=-1), 0.0)
    x = x + _L2_gnn_ref(h, edge_index, edge_type_5, L2_gnn_W_Q, L2_gnn_W_K, L2_gnn_W_V, L2_gnn_attn_bias, L2_gnn_out_proj_w, L2_gnn_out_proj_b, L2_gnn_ln_gamma, L2_gnn_ln_beta)
    h = jnp.maximum(_layernorm(x, axis=-1), 0.0)
    x = x + _L3_gnn_ref(h, edge_index, L3_gnn_W1, L3_gnn_a1_src, L3_gnn_a1_dst, L3_gnn_b1, L3_gnn_g1, L3_gnn_beta1, L3_gnn_W2, L3_gnn_a2_src, L3_gnn_a2_dst, L3_gnn_b2, L3_gnn_g2, L3_gnn_beta2)
    return x

_drawn_inputs = setup_inputs


def setup_inputs(seed=0):
    import zlib

    import numpy as np

    out = dict(_drawn_inputs(seed))
    spreads = {'L2_gnn_attn_bias': (0.0, 2.0),
     'L2_gnn_ln_gamma': (1.0, 0.564),
     'L2_gnn_ln_beta': (0.0, 0.687),
     'L3_gnn_b1': (0.0, 2.0),
     'L3_gnn_g1': (1.0, 0.6),
     'L3_gnn_beta1': (0.0, 0.8),
     'L3_gnn_b2': (0.0, 2.0),
     'L3_gnn_g2': (1.0, 0.6),
     'L3_gnn_beta2': (0.0, 0.8)}
    factors = {'L1_gnn_b': 35.461,
     'L2_gnn_out_proj_b': 8.0,
     'L3_gnn_a1_src': 2.928,
     'L3_gnn_a1_dst': 8.0,
     'L3_gnn_a2_src': 2.936,
     'L3_gnn_a2_dst': 7.562}
    for name, (base, spread) in spreads.items():
        noise = np.random.default_rng([zlib.crc32(name.encode()), seed]).standard_normal(out[name].shape)
        drawn = base * np.exp(spread * noise) if base else spread * noise
        out[name] = jnp.asarray(drawn.astype(out[name].dtype))
    for name, factor in factors.items():
        out[name] = (out[name] * factor).astype(out[name].dtype)
    return out
```

```python
import concourse.bass as bass
from concourse import mybir
from contextlib import ExitStack

F32 = mybir.dt.float32
BF16 = mybir.dt.bfloat16
I32 = mybir.dt.int32
ALU = mybir.AluOpType
ACT = mybir.ActivationFunctionType
AX = mybir.AxisListType

P = 128
N = 6250
E = 106250
D = 128
T = N // 125
PN = N // T
NP = P * T
G = 8
NS = 4
C = -(-E // (P * G * NS)) * G * NS
EP = P * C
TURNS = C // (G * NS)
LAST = E - (P - 1) * C
GN = 5
NG = T // GN
FAR = 1 << 20
NEG = -1.0e9
LOW = -1.0e38
R = 5
K2 = 8
D2 = D // K2
K3 = 4
D3 = D // K3
LN_EPS = 1e-5
WG = D + 2 * K3


class Line:

    def __init__(self, engine, sem):
        self.engine, self.sem, self.n = engine, sem, 0

    def mark(self, instruction):
        self.n = self.n + 1
        instruction.then_inc(self.sem, 1)
        return self.n

    def link(self, instruction):
        self.engine.wait_ge(self.sem, self.mark(instruction))


def over_heads(ap, heads, width):
    return ap.unsqueeze(3).to_broadcast([ap.shape[0], ap.shape[1], heads, width])


def build(nc, x_in, src_in, dst_in, type_in, z_in, w1_in, b1_in, wq_in, wk_in, wv_in, bias_in, ow_in, ob_in,
          lng_in, lnb_in, g3, out):
    ctx = ExitStack()
    with ctx:
        def dram(name, shape):
            return nc.dram_tensor(name, shape, F32, kind="Internal").ap()

        class Stage(ExitStack):
            def __init__(self, name):
                super().__init__()
                self.name = name + "_"
                stage_names.append(name)
                assert len(set(stage_names)) == len(stage_names)

        stage_names = []

        def getname(at):
            return at.name if isinstance(at, Stage) else ""

        def sb(name, shape, dt=F32, at=ctx):
            return at.enter_context(nc.sbuf_tensor(getname(at) + name, shape, dt))

        def pb(name, shape, at=ctx):
            free = 1
            for n in shape[1:]:
                free *= n
            bank = nc.PSUM_BANK_SIZE_BYTES // 4
            whole = at.enter_context(nc.psum_tensor(getname(at) + name, [shape[0], -(-free // bank) * bank], F32))
            view = whole[:, 0:free]
            return view if len(shape) == 2 else view.rearrange("p (a b) -> p a b", a=shape[1])

        def sem(name, at=ctx):
            return at.enter_context(nc.semaphore(getname(at) + name))

        dst_d = dram("dst_d", [P, C])
        start_d = dram("start_d", [NP + 1])
        run_d = dram("run_d", [NP + 1])
        h0_d = dram("h0_d", [NP, D])
        h1_d = dram("h1_d", [NP, D])
        s0_d = dram("s0_d", [EP, 2 * D])
        s1_d = dram("s1_d", [EP, D])
        kv_d = dram("kv_d", [NP * R, 2 * D])
        q_d = dram("q_d", [NP * R, D + K2])
        v_d = dram("v_d", [EP, D])
        s2_d = dram("s2_d", [EP, D])
        xw_d = dram("xw_d", [NP, D + K3])
        self_d = dram("self_d", [NP, 2 * K3])
        start_rows_d = dram("start_rows_d", [EP, 2 * K3])
        xe_d = dram("xe_d", [EP, D])
        s3_d = dram("s3_d", [EP, WG])

        x = sb("x", [P, T, D])
        h = sb("h", [P, T, D])
        ident = sb("ident", [P, P])
        lane = sb("lane", [P, 1])
        src_i = sb("src_i", [P, C], I32)
        cont = sb("cont", [P, C])
        in_first = sb("in_first", [P, C])
        in_last = sb("in_last", [P, C])
        kv_i = sb("kv_i", [P, C], I32)
        q_i = sb("q_i", [P, C], I32)
        type_f = sb("type_f", [P, C])
        single_row = sb("single_row", [P, P])
        link_row = sb("link_row", [P, P])
        run_rows = sb("run_rows", [P, T, P], BF16)
        end_i = sb("end_i", [P, T], I32)
        start_i = sb("start_i", [P, T], I32)
        dst0_i = sb("dst0_i", [P, 1], I32)
        has = sb("has", [P, T])
        hasnt = sb("hasnt", [P, T])
        rdeg = sb("rdeg", [P, T])
        carry = sb("carry", [P, 2 * D])

        gathered = [sem(f"gathered{s}") for s in range(NS)]
        gathered_count = [0] * NS

        def gathered_before(slots, dmas):
            before = list(gathered_count)
            for s in range(slots):
                gathered_count[s] += 16 * dmas
            return before

        pool_gate, sp_gate, act_gate, pe_gate = sem("pool_gate"), sem("sp_gate"), sem("act_gate"), sem("pe_gate")

        def renew_semaphores():
            nc.all_engine_barrier(sems_to_clear=range(pe_gate.num + 1, 256))

        def rows_of_edges(flat, first, count):
            return flat[first:first + count * C].rearrange("(p c) -> p c", c=C)

        def setup():
            st = Stage("setup")
            with st:
                dst_i = sb("dst_i", [P, C], I32, st)
                prev_i = sb("prev_i", [P, C], I32, st)
                next_i = sb("next_i", [P, 1], I32, st)
                type_i = sb("type_i", [P, C], I32, st)
                dst_f = sb("dst_f", [P, C], F32, st)
                prev_f = sb("prev_f", [P, C], F32, st)
                next_f = sb("next_f", [P, 1], F32, st)
                src_f = sb("src_f", [P, C], F32, st)
                tmp = sb("tmp", [P, C], F32, st)
                ids = sb("ids", [P, T], F32, st)
                wide = sb("wide", [P, GN, P], F32, st)
                below = sb("below", [P, GN, P], F32, st)
                first_row = sb("first_row", [P, P], F32, st)
                runs = sb("runs", [P, T], F32, st)
                run_i = sb("run_i", [P, T], I32, st)
                ids_slot = sb("ids_slot", [P, GN], F32, st)
                cnt_slot = sb("cnt_slot", [P, GN], F32, st)
                cnt = sb("cnt", [P, T], F32, st)
                start = sb("start", [P, T], F32, st)
                after = sb("after", [P, T], F32, st)
                run_after = sb("run_after", [P, T], F32, st)
                ends = sb("ends", [P, 2], F32, st)
                t0 = sb("t0", [P, T], F32, st)
                t1 = sb("t1", [P, T], F32, st)
                deg = sb("deg", [P, T], F32, st)
                run_sel = sb("run_sel", [P, T], F32, st)
                dst_rows = sb("dst_rows", [P, 2, GN, C], F32, st)
                idx_slot = sb("idx_slot", [P, 2, GN], I32, st)
                row_ps = pb("row_ps", [P, GN, P], st)

                cleared, loaded, iotas = sem("cleared", st), sem("loaded", st), sem("iotas", st)
                dst_saved, nodes_saved, nodes_back = (sem("dst_saved", st), sem("nodes_saved", st),
                                                      sem("nodes_back", st))
                dve_steps, wide_ready, rows_ready = sem("dve_steps", st), sem("wide_ready", st), sem("rows_ready", st)
                runs_ready, idx_ready, dst_ready = sem("runs_ready", st), sem("idx_ready", st), sem("dst_ready", st)
                starts_ready, rows_copied = sem("starts_ready", st), sem("rows_copied", st)
                got, g0 = gathered, gathered_before(2, GN * NG // 2)
                counted = sem("counted", st)

                with nc.Block() as block:
                    @block.sync
                    def _(sp):
                        sp.wait_ge(cleared, 6)
                        parts = [(0, 112), (112, P - 1)]
                        for tile, flat in ((dst_i, dst_in), (src_i, src_in), (type_i, type_in)):
                            for a, b in parts:
                                sp.dma_start(tile[a:b, :], rows_of_edges(flat, a * C, b - a)).then_inc(loaded, 16)
                            sp.dma_start(tile[P - 1:P, 0:LAST],
                                         flat[(P - 1) * C:E].rearrange("(a c) -> a c", a=1)).then_inc(loaded, 16)
                        for a, b in ((1, 113), (113, P - 1)):
                            sp.dma_start(prev_i[a:b, :], rows_of_edges(dst_in, a * C - 1, b - a)).then_inc(loaded, 16)
                        sp.dma_start(prev_i[P - 1:P, 0:LAST],
                                     dst_in[(P - 1) * C - 1:E - 1].rearrange("(a c) -> a c", a=1)).then_inc(loaded, 16)
                        sp.dma_start(prev_i[0:1, 1:C], dst_in[0:C - 1].rearrange("(a c) -> a c", a=1)).then_inc(loaded, 16)
                        sp.dma_start(next_i[0:P - 2, :], rows_of_edges(dst_in, C, P - 2)[:, 0:1],
                                     allow_slow_non_contiguous=True).then_inc(loaded, 16)
                        sp.dma_start(next_i[P - 2:P - 1, :],
                                     dst_in[(P - 1) * C:(P - 1) * C + 1].rearrange("(a c) -> a c", a=1)).then_inc(loaded, 16)
                        xv = x_in.rearrange("(p t) f -> p t f", t=T)
                        sp.dma_start(x[0:112, :, :], xv[0:112]).then_inc(loaded, 16)
                        sp.dma_start(x[112:PN, :, :], xv[112:PN]).then_inc(loaded, 16)
                        sp.wait_ge(dst_ready, 1)
                        sp.dma_start(dst_d, dst_f[:]).then_inc(dst_saved, 16)
                        sp.wait_ge(starts_ready, 1)
                        sp.dma_start(start_d[0:NP].rearrange("(p t) -> p t", t=T), start[:]).then_inc(nodes_saved, 16)
                        sp.dma_start(run_d[0:NP].rearrange("(p t) -> p t", t=T), runs[:]).then_inc(nodes_saved, 16)
                        sp.dma_start(start_d[NP:NP + 1].rearrange("(a c) -> a c", a=1), ends[0:1, 0:1]).then_inc(nodes_saved, 16)
                        sp.dma_start(run_d[NP:NP + 1].rearrange("(a c) -> a c", a=1), ends[0:1, 1:2]).then_inc(nodes_saved, 16)
                        sp.wait_ge(nodes_saved, 64)
                        sp.dma_start(after[:], start_d[1:NP + 1].rearrange("(p t) -> p t", t=T)).then_inc(nodes_back, 16)
                        sp.dma_start(run_after[:], run_d[1:NP + 1].rearrange("(p t) -> p t", t=T)).then_inc(nodes_back, 16)
                        sp.wait_ge(nodes_back, 32)

                    @block.gpsimd
                    def _(pool):
                        nc.gpsimd.memset(ident[:], 0.0).then_inc(iotas, 1)
                        pool.wait_ge(iotas, 1)
                        nc.gpsimd.affine_select(out=ident[:], in_=ident[:], compare_op=ALU.not_equal, fill=1.0,
                                                base=0, pattern=[[-1, P]], channel_multiplier=1).then_inc(iotas, 1)
                        nc.gpsimd.iota(lane[:], pattern=[[0, 1]], base=0, channel_multiplier=1,
                                       allow_small_or_imprecise_dtypes=True).then_inc(iotas, 1)
                        nc.gpsimd.iota(ids[:], pattern=[[1, T]], base=0, channel_multiplier=T,
                                       allow_small_or_imprecise_dtypes=True).then_inc(iotas, 1)
                        pool.wait_ge(dst_saved, 16)

                        def gathers(i, s):
                            pool.wait_ge(idx_ready, i * 2 + s + 1)
                            pool.sem_inc(pool_gate, 1)
                            for j in range(GN):
                                nc.gpsimd.indirect_dma_start(
                                    out=dst_rows[:, s, j, :], out_offset=None, in_=dst_d,
                                    in_offset=bass.IndirectOffsetOnAxis(ap=idx_slot[:, s, j:j + 1], axis=0)
                                ).then_inc(got[s], 16)
                        with pool.Fori(0, NG // 2) as i:
                            for s in range(2):
                                gathers(i, s)

                    @block.scalar
                    def _(act):
                        act.wait_ge(runs_ready, 1)
                        act.activation(idx_slot[:], run_i[:, 0:2 * GN].rearrange("p (s g) -> p s g", s=2),
                                       ACT.Copy).then_inc(idx_ready, 2)
                        with act.Fori(1, NG // 2) as i:
                            for s in range(2):
                                act.wait_ge(counted, (i - 1) * 2 + s + 1)
                                act.sem_inc(act_gate, 1)
                                act.activation(idx_slot[:, s, :], run_i[:, bass.ds((i * 2 + s) * GN, GN)],
                                               ACT.Copy).then_inc(idx_ready, 1)
                        with act.Fori(0, NG) as i:
                            act.wait_ge(rows_ready, i + 4)
                            act.sem_inc(act_gate, 1)
                            act.activation(run_rows[:, bass.ds(i * GN, GN), :], row_ps[:], ACT.Copy).then_inc(rows_copied, 1)

                    @block.tensor
                    def _(pe):
                        pe.wait_ge(iotas, 2)
                        for k in range(3):
                            pe.wait_ge(wide_ready, k + 1)
                            nc.tensor.transpose(row_ps[:, 0, :], wide[:, 0, :], ident[:]).then_inc(rows_ready, 1)
                        with pe.Fori(0, NG) as i:
                            pe.wait_ge(wide_ready, i + 4)
                            for j in range(GN):
                                ins = nc.tensor.transpose(row_ps[:, j, :], wide[:, j, :], ident[:])
                            ins.then_inc(rows_ready, 1)

                    @block.vector
                    def _(dve):
                        line = Line(dve, dve_steps)
                        for tile, value in ((dst_i, FAR), (src_i, 0), (type_i, 0), (prev_i, -1), (next_i, -2)):
                            nc.vector.memset(tile[:], value).then_inc(cleared, 1)
                        nc.vector.memset(x[:], 0.0).then_inc(cleared, 1)
                        nc.vector.memset(ends[:, 0:1], float(E))
                        line.link(nc.vector.memset(ends[:, 1:2], float(P - 1)))
                        dve.wait_ge(loaded, 17 * 16)
                        nc.vector.tensor_copy(dst_f[:], dst_i[:]).then_inc(dst_ready, 1)
                        nc.vector.tensor_copy(src_f[:], src_i[:])
                        nc.vector.tensor_copy(type_f[:], type_i[:])
                        nc.vector.tensor_copy(next_f[:], next_i[:])
                        line.link(nc.vector.tensor_copy(prev_f[:], prev_i[:]))
                        nc.vector.tensor_tensor(cont[:], dst_f[:], prev_f[:], ALU.is_equal)
                        nc.vector.tensor_scalar(in_first[:], dst_f[:], prev_f[:, 0:1], None, ALU.is_equal)
                        nc.vector.tensor_scalar(in_last[:], dst_f[:], next_f[:, 0:1], None, ALU.is_equal)
                        line.link(nc.vector.scalar_tensor_tensor(out=tmp[:], in0=src_f[:], scalar=float(R), in1=type_f[:],
                                                                 op0=ALU.mult, op1=ALU.add))
                        line.link(nc.vector.tensor_copy(kv_i[:], tmp[:]))
                        line.link(nc.vector.tensor_scalar(tmp[:], dst_f[:], float(N - 1), float(R), ALU.min, ALU.mult))
                        line.link(nc.vector.tensor_tensor(tmp[:], tmp[:], type_f[:], ALU.add))
                        line.link(nc.vector.tensor_copy(q_i[:], tmp[:]))
                        line.link(nc.vector.tensor_scalar(tmp[:, 0:1], dst_f[:, 0:1], float(N - 1), None, ALU.min))
                        line.link(nc.vector.tensor_copy(dst0_i[:], tmp[:, 0:1]))

                        def spread(column):
                            nc.vector.tensor_copy(wide[:, 0, :], column.to_broadcast([P, P])).then_inc(wide_ready, 1)

                        spread(dst_f[:, 0:1])
                        dve.wait_ge(rows_ready, 1)
                        line.link(nc.vector.tensor_copy(first_row[:], row_ps[:, 0, :]))
                        line.link(nc.vector.tensor_tensor(tmp[:, 0:1], prev_f[:, 0:1], dst_f[:, C - 1:C], ALU.is_equal))
                        spread(tmp[:, 0:1])
                        dve.wait_ge(rows_ready, 2)
                        line.link(nc.vector.tensor_copy(single_row[:], row_ps[:, 0, :]))
                        line.link(nc.vector.tensor_tensor(tmp[:, 0:1], dst_f[:, 0:1], next_f[:, 0:1], ALU.is_equal))
                        spread(tmp[:, 0:1])
                        dve.wait_ge(rows_ready, 3)
                        line.link(nc.vector.tensor_copy(link_row[:], row_ps[:, 0, :]))

                        dve.wait_ge(iotas, 4)
                        base, per = line.n, 3
                        with dve.Fori(0, NG) as i:
                            line.n = i * per + base
                            line.link(nc.vector.tensor_copy(ids_slot[:], ids[:, bass.ds(i * GN, GN)]))
                            line.link(nc.vector.tensor_tensor(
                                below[:], first_row[:].unsqueeze(1).to_broadcast([P, GN, P]),
                                ids_slot[:].unsqueeze(2).to_broadcast([P, GN, P]), ALU.is_lt))
                            line.link(nc.vector.tensor_reduce(cnt_slot[:], below[:], AX.X, ALU.add))
                            nc.vector.tensor_copy(runs[:, bass.ds(i * GN, GN)], cnt_slot[:])
                        line.n = base + NG * per
                        line.link(nc.vector.memset(tmp[:, 0:1], 0.0))
                        line.link(nc.vector.tensor_scalar(runs[:], runs[:], -1.0, 0.0, ALU.add, ALU.max))
                        nc.vector.tensor_copy(run_i[:], runs[:]).then_inc(runs_ready, 1)

                        base, per = line.n, 2
                        with dve.Fori(0, NG // 2) as i:
                            line.n = i * (2 * per) + base
                            for s in range(2):
                                line.link(nc.vector.tensor_copy(ids_slot[:], ids[:, bass.ds((i * 2 + s) * GN, GN)]))
                                dve.wait_ge(got[s], i * (16 * GN) + (g0[s] + 16 * GN))
                                for j in range(GN):
                                    ins = nc.vector.tensor_scalar(dst_rows[:, s, j, :], dst_rows[:, s, j, :],
                                                                  ids_slot[:, j:j + 1], 0.0, ALU.is_lt, ALU.add,
                                                                  accum_out=cnt_slot[:, j:j + 1])
                                line.link(ins)
                                nc.vector.tensor_copy(cnt[:, bass.ds((i * 2 + s) * GN, GN)], cnt_slot[:]).then_inc(counted, 1)
                        line.n = base + NG * per
                        dve.wait_ge(counted, NG)
                        nc.vector.scalar_tensor_tensor(out=start[:], in0=runs[:], scalar=float(C), in1=cnt[:],
                                                       op0=ALU.mult, op1=ALU.add).then_inc(starts_ready, 1)
                        dve.wait_ge(nodes_back, 32)
                        line.link(nc.vector.tensor_tensor(deg[:], after[:], start[:], ALU.subtract))
                        line.link(nc.vector.tensor_scalar(has[:], deg[:], 0.0, None, ALU.is_gt))
                        line.link(nc.vector.tensor_scalar(hasnt[:], has[:], -1.0, 1.0, ALU.mult, ALU.add))
                        line.link(nc.vector.tensor_scalar(deg[:], deg[:], 1.0, None, ALU.max))
                        line.link(nc.vector.reciprocal(rdeg[:], deg[:]))
                        line.link(nc.vector.tensor_scalar(t0[:], after[:], -1.0, 0.0, ALU.add, ALU.max))
                        line.link(nc.vector.tensor_copy(end_i[:], t0[:]))
                        line.link(nc.vector.tensor_scalar(t0[:], start[:], float(-FAR), None, ALU.add))
                        line.link(nc.vector.tensor_tensor(t0[:], t0[:], has[:], ALU.mult))
                        line.link(nc.vector.tensor_scalar(t0[:], t0[:], float(FAR), None, ALU.add))
                        line.link(nc.vector.tensor_copy(start_i[:], t0[:]))
                        line.link(nc.vector.tensor_scalar(t0[:], run_after[:], float(C), None, ALU.mult))
                        line.link(nc.vector.tensor_tensor(t0[:], start[:], t0[:], ALU.is_lt))
                        line.link(nc.vector.tensor_scalar(t1[:], run_after[:], 1.0, None, ALU.add))
                        line.link(nc.vector.tensor_tensor(t1[:], t1[:], t0[:], ALU.mult))
                        line.link(nc.vector.tensor_scalar(run_sel[:], t1[:], -1.0, None, ALU.add))
                        nc.vector.tensor_copy(wide[:], run_sel[:, 0:GN].unsqueeze(2)
                                              .to_broadcast([P, GN, P])).then_inc(wide_ready, 1)
                        with dve.Fori(1, NG) as i:
                            dve.wait_ge(rows_copied, i)
                            nc.vector.tensor_copy(wide[:], run_sel[:, bass.ds(i * GN, GN)].unsqueeze(2)
                                                  .to_broadcast([P, GN, P])).then_inc(wide_ready, 1)

        def norm_relu(name, table):
            st = Stage(name)
            with st:
                stats = sb("stats", [P, T, 6], F32, st)
                half = sb("half", [P, T], F32, st)
                stats_done = sem("stats_done", st)
                rstd = sb("rstd", [P, T], F32, st)
                shift = sb("shift", [P, T], F32, st)
                eps = sb("eps", [P, 1], F32, st)
                dve_steps, var_ready, std_ready = sem("dve_steps", st), sem("var_ready", st), sem("std_ready", st)
                coef_ready, h_ready, saved = sem("coef_ready", st), sem("h_ready", st), sem("saved", st)
                with nc.Block() as block:
                    @block.vector
                    def _(dve):
                        line = Line(dve, dve_steps)
                        line.link(nc.vector.memset(eps[:], LN_EPS))
                        with dve.Fori(0, T // 2) as i:
                            for s in range(2):
                                t = bass.ds(i * 2 + s, 1)
                                nc.vector.bn_stats(stats[:, t, :].rearrange("p a f -> p (a f)"),
                                                   x[:, t, :].rearrange("p a f -> p (a f)")).then_inc(stats_done, 1)
                        dve.wait_ge(stats_done, T)
                        line.link(nc.vector.tensor_tensor(shift[:], stats[:, :, 1], stats[:, :, 4], ALU.add))
                        line.link(nc.vector.tensor_tensor(rstd[:], stats[:, :, 1], stats[:, :, 4], ALU.subtract))
                        line.link(nc.vector.scalar_tensor_tensor(out=rstd[:], in0=rstd[:], scalar=0.25, in1=rstd[:],
                                                                 op0=ALU.mult, op1=ALU.mult))
                        line.link(nc.vector.tensor_tensor(half[:], stats[:, :, 2], stats[:, :, 5], ALU.add))
                        nc.vector.scalar_tensor_tensor(out=rstd[:], in0=half[:], scalar=1.0 / D, in1=rstd[:],
                                                       op0=ALU.mult, op1=ALU.add).then_inc(var_ready, 1)
                        dve.wait_ge(std_ready, 1)
                        line.link(nc.vector.reciprocal(rstd[:], rstd[:]))
                        nc.vector.scalar_tensor_tensor(out=shift[:], in0=shift[:], scalar=-0.5, in1=rstd[:],
                                                       op0=ALU.mult, op1=ALU.mult).then_inc(coef_ready, 1)

                    @block.scalar
                    def _(act):
                        act.wait_ge(var_ready, 1)
                        act.activation(rstd[:], rstd[:], ACT.Sqrt, bias=eps[:, 0:1]).then_inc(std_ready, 1)
                        act.wait_ge(coef_ready, 1)
                        with act.Fori(0, T // 2) as i:
                            for s in range(2):
                                t = bass.ds(i * 2 + s, 1)
                                act.activation(h[:, t, :].rearrange("p a f -> p (a f)"), x[:, t, :].rearrange("p a f -> p (a f)"),
                                               ACT.Relu, bias=shift[:, t], scale=rstd[:, t]).then_inc(h_ready, 1)

                    @block.sync
                    def _(sp):
                        if table is not None:
                            sp.wait_ge(h_ready, T)
                            sp.dma_start(table.rearrange("(p t) f -> p t f", t=T), h[:]).then_inc(saved, 16)
                            sp.wait_ge(saved, 16)

        def gather_sum(name, table, sums_d, with_max):
            W = 2 * D if with_max else D
            ops = 2 if with_max else 1
            st = Stage(name)
            with st:
                idx_slot = sb("idx_slot", [P, NS, G], I32, st)
                rows = sb("rows", [P, NS, G, D], F32, st)
                sums = sb("sums", [P, NS, G, W], F32, st)
                idx_ready, summed, cleared = sem("idx_ready", st), sem("summed", st), sem("cleared", st)
                got, g0 = gathered, gathered_before(NS, C // NS)
                stored = [sem(f"stored{s}", st) for s in range(NS)]
                with nc.Block() as block:
                    @block.gpsimd
                    def _(pool):
                        def turn(i, first):
                            for s in range(NS):
                                pool.wait_ge(idx_ready, i * NS + s + 1)
                                if not first:
                                    pool.wait_ge(summed, (i * NS + s + 1 - NS) * (G * ops))
                                pool.sem_inc(pool_gate, 1)
                                for j in range(G):
                                    nc.gpsimd.indirect_dma_start(
                                        out=rows[:, s, j, :], out_offset=None, in_=table,
                                        in_offset=bass.IndirectOffsetOnAxis(ap=idx_slot[:, s, j:j + 1], axis=0)
                                    ).then_inc(got[s], 16)
                        turn(0, True)
                        with pool.Fori(1, TURNS) as i:
                            turn(i, False)

                    @block.scalar
                    def _(act):
                        act.activation(idx_slot[:], src_i[:, 0:NS * G].rearrange("p (s g) -> p s g", s=NS),
                                       ACT.Copy).then_inc(idx_ready, NS)
                        with act.Fori(1, TURNS) as i:
                            for s in range(NS):
                                act.wait_ge(got[s], i * (16 * G) + g0[s])
                                act.sem_inc(act_gate, 1)
                                act.activation(idx_slot[:, s, :], src_i[:, bass.ds((i * NS + s) * G, G)],
                                               ACT.Copy).then_inc(idx_ready, 1)

                    @block.vector
                    def _(dve):
                        nc.vector.memset(sums[:, NS - 1, G - 1, :], 0.0).then_inc(cleared, 1)
                        dve.wait_ge(cleared, 1)

                        def turn(i, first):
                            for s in range(NS):
                                dve.wait_ge(got[s], i * (16 * G) + (g0[s] + 16 * G))
                                if not first:
                                    dve.wait_ge(stored[s], i * 16)
                                for j in range(G):
                                    ps, pj = (s, j - 1) if j else ((s - 1) % NS, G - 1)
                                    for m in range(ops):
                                        k = (s * G + j) * ops + m
                                        if not (first and k < ops):
                                            dve.wait_ge(summed, i * (NS * G * ops) + (k - ops + 1))
                                        nc.vector.scalar_tensor_tensor(
                                            out=sums[:, s, j, m * D:m * D + D], in0=sums[:, ps, pj, m * D:m * D + D],
                                            scalar=cont[:, bass.ds((i * NS + s) * G + j, 1)], in1=rows[:, s, j, :],
                                            op0=ALU.mult, op1=(ALU.add, ALU.max)[m]).then_inc(summed, 1)
                        turn(0, True)
                        with dve.Fori(1, TURNS) as i:
                            turn(i, False)
                        dve.wait_ge(summed, C * ops)
                        nc.vector.tensor_copy(carry[:, 0:W], sums[:, NS - 1, G - 1, :])

                    @block.sync
                    def _(sp):
                        view = sums_d.rearrange("(p c) f -> p c f", c=C)
                        with sp.Fori(0, TURNS) as i:
                            for s in range(NS):
                                c0 = sp.snap((i * NS + s) * G)
                                sp.wait_ge(summed, (i * NS + s + 1) * (G * ops))
                                sp.sem_inc(sp_gate, 1)
                                sp.dma_start(view[:, bass.ds(c0, G), :], sums[:, s, :, :]).then_inc(stored[s], 16)
                        for s in range(NS):
                            sp.wait_ge(stored[s], 16 * TURNS)

        def chain_runs(name, parts):
            st = Stage(name)
            with st:
                turned = sb("turned", [P, P + 1], F32, st)
                last_t = pb("last_t", [P, P], st)
                back_t = pb("back_t", [P, P], st)
                dve_steps, turned_ready, pe_done = sem("dve_steps", st), sem("turned_ready", st), sem("pe_done", st)
                with nc.Block() as block:
                    @block.tensor
                    def _(pe):
                        for n, (a, w, _m) in enumerate(parts):
                            if n:
                                pe.wait_ge(turned_ready, 2 * n)
                            nc.tensor.transpose(last_t[0:w, :], carry[:, a:a + w], ident[:]).then_inc(pe_done, 1)
                            pe.wait_ge(turned_ready, 2 * n + 1)
                            nc.tensor.transpose(back_t[:, 0:w], turned[0:w, 0:P], ident[0:w, 0:w]).then_inc(pe_done, 1)

                    @block.vector
                    def _(dve):
                        for n, (a, w, is_max) in enumerate(parts):
                            if not n:
                                nc.vector.memset(turned[:, 0:1], 0.0).then_inc(dve_steps, 1)
                                dve.wait_ge(dve_steps, 1)
                            dve.wait_ge(pe_done, 2 * n + 1)
                            nc.vector.tensor_tensor_scan(turned[0:w, 1:P + 1], single_row[0:w, :], last_t[0:w, :], 0.0,
                                                         ALU.mult, ALU.max if is_max else ALU.add).then_inc(turned_ready, 1)
                            dve.wait_ge(pe_done, 2 * n + 2)
                            nc.vector.tensor_copy(carry[:, a:a + w], back_t[:, 0:w]).then_inc(turned_ready, 1)

        def node_totals(name, sums_d, W, WC, pre, per, scratch, consts, body, act_body=None, pe_body=None, pe_start=None):
            st = Stage(name)
            with st:
                idx_slot = sb("idx_slot", [P, 2, GN], I32, st)
                totals = sb("totals", [P, 2, GN, W], F32, st)
                pick = sb("pick", [P, GN, P], F32, st)
                reach = pb("reach", [P, GN, 2 * D], st)
                idx_ready, picked, reached = sem("idx_ready", st), sem("picked", st), sem("reached", st)
                got, g0 = gathered, gathered_before(2, GN * NG // 2)
                dve_steps = sem("dve_steps", st)
                extra = scratch(st)
                with nc.Block() as block:
                    @block.gpsimd
                    def _(pool):
                        with pool.Fori(0, NG // 2) as i:
                            for s in range(2):
                                pool.wait_ge(idx_ready, i * 2 + s + 1)
                                pool.sem_inc(pool_gate, 1)
                                for j in range(GN):
                                    nc.gpsimd.indirect_dma_start(
                                        out=totals[:, s, j, :], out_offset=None, in_=sums_d,
                                        in_offset=bass.IndirectOffsetOnAxis(ap=idx_slot[:, s, j:j + 1], axis=0)
                                    ).then_inc(got[s], 16)

                    @block.sync
                    def _(sp):
                        consts(sp, extra)

                    @block.scalar
                    def _(act):
                        act.activation(idx_slot[:], end_i[:, 0:2 * GN].rearrange("p (s g) -> p s g", s=2),
                                       ACT.Copy).then_inc(idx_ready, 2)

                        def group(k, first):
                            if act_body:
                                act_body(act, k, first, extra)

                        for s in range(2):
                            group(s, s == 0)
                        with act.Fori(1, NG // 2) as i:
                            for s in range(2):
                                act.wait_ge(dve_steps, i * (2 * per) + (pre + (s - 1) * per))
                                act.sem_inc(act_gate, 1)
                                act.activation(idx_slot[:, s, :], end_i[:, bass.ds((i * 2 + s) * GN, GN)],
                                               ACT.Copy).then_inc(idx_ready, 1)
                                group(i * 2 + s, False)

                    @block.tensor
                    def _(pe):
                        if pe_start:
                            pe_start(pe, extra)
                        with pe.Fori(0, NG) as i:
                            pe.wait_ge(picked, i + 1)
                            for j in range(GN):
                                ins = nc.tensor.matmul(reach[:, j, 0:WC], pick[:, j, :], carry[:, 0:WC], start=True, stop=True)
                            ins.then_inc(reached, 1)
                            if pe_body:
                                pe_body(pe, i, extra)

                    @block.vector
                    def _(dve):
                        line = Line(dve, dve_steps)
                        if "prepare" in extra:
                            extra["prepare"](dve, line)
                        assert line.n == pre
                        with dve.Fori(0, NG // 2) as i:
                            for s in range(2):
                                k = i * 2 + s
                                line.n = i * (2 * per) + (pre + s * per)
                                nc.vector.tensor_scalar(pick[:], run_rows[:, bass.ds(k * GN, GN), :], lane[:, 0:1], None,
                                                        ALU.is_equal).then_inc(picked, 1)
                                dve.wait_ge(got[s], i * (16 * GN) + (g0[s] + 16 * GN))
                                dve.wait_ge(reached, k + 1)
                                body(dve, line, k, totals[:, s, :, :], reach, extra)

        def linear_scratch(st, e, sources):
            e["sources"] = sources
            e["left"] = sb("left", [P, sources, GN, D], F32, st)
            e["left_t"] = sb("left_t", [P, sources, GN, D], F32, st)
            e["w"] = sb("w", [P, sources, D], F32, st)
            e["turn_ps"] = pb("turn_ps", [P, sources * GN, D], st)
            e["lin_ps"] = pb("lin_ps", [P, GN, D], st)
            for k in ("left_ready", "h_copied", "turned", "evacuated", "multiplied", "loaded"):
                e[k] = sem(k, st)

        def linear_act(act, k, first, e):
            if e["sources"] == 2:
                if not first:
                    act.wait_ge(e["turned"], k)
                    act.sem_inc(act_gate, 1)
                act.activation(e["left"][:, 1, :, :], h[:, bass.ds(k * GN, GN), :], ACT.Copy).then_inc(e["h_copied"], 1)
            act.wait_ge(e["turned"], k + 1)
            act.activation(e["left_t"][:].rearrange("p a g f -> p (a g) f"), e["turn_ps"][:], ACT.Copy).then_inc(e["evacuated"], 1)

        def linear_pe(pe, i, e):
            pe.wait_ge(e["left_ready"], i + 1)
            if e["sources"] == 2:
                pe.wait_ge(e["h_copied"], i + 1)
            for a in range(e["sources"]):
                for j in range(GN):
                    ins = nc.tensor.transpose(e["turn_ps"][:, a * GN + j, :], e["left"][:, a, j, :], ident[:])
            ins.then_inc(e["turned"], 1)
            pe.wait_ge(e["evacuated"], i + 1)
            for j in range(GN):
                for a in range(e["sources"]):
                    ins = nc.tensor.matmul(e["lin_ps"][:, j, :], e["left_t"][:, a, j, :], e["w"][:, a, :],
                                           start=a == 0, stop=a == e["sources"] - 1)
            ins.then_inc(e["multiplied"], 1)

        def layer0_nodes():
            def scratch(st):
                e = {k: sb(k, [P, T], F32, st) for k in ("sum_w", "max_w")}
                e["z"] = sb("z", [P, 3], F32, st)
                e["a"] = sb("part_a", [P, GN, D], F32, st)
                e["b"] = sb("part_b", [P, GN, D], F32, st)
                e["loaded"] = sem("loaded", st)

                def prepare(dve, line):
                    z = e["z"]
                    dve.wait_ge(e["loaded"], 16)
                    line.link(nc.vector.tensor_scalar(e["sum_w"][:], rdeg[:], z[:, 1:2], z[:, 0:1], ALU.mult, ALU.add))
                    line.link(nc.vector.tensor_tensor(e["sum_w"][:], e["sum_w"][:], has[:], ALU.mult))
                    line.link(nc.vector.tensor_scalar(e["max_w"][:], has[:], z[:, 2:3], None, ALU.mult))
                e["prepare"] = prepare
                return e

            def consts(sp, e):
                sp.dma_start(e["z"][:], z_in.to_broadcast([P, 3])).then_inc(e["loaded"], 16)
                sp.wait_ge(e["loaded"], 16)

            def body(dve, line, k, total, reach, e):
                tiles = bass.ds(k * GN, GN)
                a, b = e["a"], e["b"]
                line.link(nc.vector.tensor_tensor(a[:], total[:, :, 0:D], reach[:, :, 0:D], ALU.add))
                line.link(nc.vector.tensor_tensor(b[:], total[:, :, D:2 * D], reach[:, :, D:2 * D], ALU.max))
                line.link(nc.vector.tensor_tensor(a[:], a[:], e["sum_w"][:, tiles].unsqueeze(2).to_broadcast([P, GN, D]), ALU.mult))
                line.link(nc.vector.tensor_tensor(b[:], b[:], e["max_w"][:, tiles].unsqueeze(2).to_broadcast([P, GN, D]), ALU.mult))
                line.link(nc.vector.tensor_tensor(a[:], a[:], b[:], ALU.add))
                line.link(nc.vector.tensor_tensor(x[:, tiles, :], x[:, tiles, :], a[:], ALU.add))

            node_totals("nodes0", s0_d, 2 * D, 2 * D, 3, 6, scratch, consts, body)

        def layer1_nodes():
            def scratch(st):
                e = {}
                linear_scratch(st, e, 2)
                e["bias"] = sb("bias", [P, D], F32, st)
                e["mean_w"] = sb("mean_w", [P, T], F32, st)

                def prepare(dve, line):
                    line.link(nc.vector.tensor_tensor(e["mean_w"][:], rdeg[:], has[:], ALU.mult))
                    dve.wait_ge(e["loaded"], 48)
                e["prepare"] = prepare
                return e

            def consts(sp, e):
                sp.dma_start(e["w"][:, 0, :], w1_in[D:2 * D, :]).then_inc(e["loaded"], 16)
                sp.dma_start(e["w"][:, 1, :], w1_in[0:D, :]).then_inc(e["loaded"], 16)
                sp.dma_start(e["bias"][:], b1_in.rearrange("(a f) -> a f", a=1).to_broadcast([P, D])).then_inc(e["loaded"], 16)
                sp.wait_ge(e["loaded"], 48)

            def body(dve, line, k, total, reach, e):
                tiles = bass.ds(k * GN, GN)
                m = e["left"][:, 0, :, :]
                line.link(nc.vector.tensor_tensor(m, total[:, :, 0:D], reach[:, :, 0:D], ALU.add))
                nc.vector.tensor_tensor(m, m, e["mean_w"][:, tiles].unsqueeze(2).to_broadcast([P, GN, D]),
                                        ALU.mult).then_inc(e["left_ready"], 1)
                dve.wait_ge(e["multiplied"], k + 1)
                line.link(nc.vector.tensor_tensor(m, e["lin_ps"][:], e["bias"][:].unsqueeze(1).to_broadcast([P, GN, D]), ALU.add))
                line.link(nc.vector.tensor_tensor(x[:, tiles, :], x[:, tiles, :], m, ALU.add))

            def pe_body(pe, i, e):
                linear_pe(pe, i, e)

            node_totals("nodes1", s1_d, D, D, 1, 3, scratch, consts, body, linear_act, pe_body)

        def relation_tables():
            BANK = 512
            KV = R * 2 * D
            st = Stage("tables2")
            with st:
                w = sb("w", [P, KV + R * D], F32, st)
                left = sb("left", [P, 2, D], F32, st)
                left_t = sb("left_t", [P, 2, D], F32, st)
                kv_slot = sb("kv_slot", [P, 2, KV], F32, st)
                q_slot = sb("q_slot", [P, 2, R, D + K2], F32, st)
                bias = sb("bias", [P, R, K2], F32, st)
                turn_ps = pb("turn_ps", [P, BANK], st)
                out_ps = pb("out_ps", [P, 4, BANK], st)
                loaded, copied, turned, evacuated = sem("loaded", st), sem("copied", st), sem("turned", st), sem("evacuated", st)
                multiplied, dve_out, act_out = sem("multiplied", st), sem("dve_out", st), sem("act_out", st)
                bias_in_place = sem("bias_in_place", st)
                saved = [sem(f"saved{s}", st) for s in range(2)]
                with nc.Block() as block:
                    @block.sync
                    def _(sp):
                        for r in range(R):
                            for a, src in ((r * 2 * D, wk_in), (r * 2 * D + D, wv_in), (KV + r * D, wq_in)):
                                sp.dma_start(w[:, a:a + D].rearrange("h (k d) -> h k d", k=K2),
                                             src[r].rearrange("k h d -> h k d")).then_inc(loaded, 16)
                        sp.dma_start(bias[:].rearrange("p r k -> p (r k)"),
                                     bias_in.rearrange("(a r) k -> a (r k)", a=1).to_broadcast([P, R * K2])).then_inc(loaded, 16)
                        kv_v = kv_d.rearrange("(p t r) w -> p t (r w)", t=T, r=R)
                        q_v = q_d.rearrange("(p t r) w -> p t (r w)", t=T, r=R)
                        with sp.Fori(0, T // 2) as i:
                            for s in range(2):
                                t = sp.snap(i * 2 + s)
                                sp.wait_ge(dve_out, i * 2 + s + 1)
                                sp.sem_inc(sp_gate, 1)
                                sp.wait_ge(act_out, i * 2 + s + 1)
                                sp.sem_inc(sp_gate, 1)
                                sp.dma_start(kv_v[:, bass.ds(t, 1), :], kv_slot[:, s:s + 1, :]).then_inc(saved[s], 16)
                                sp.dma_start(q_v[:, bass.ds(t, 1), :],
                                             q_slot[:, s:s + 1, :, :].rearrange("p a r w -> p a (r w)")).then_inc(saved[s], 16)
                        for s in range(2):
                            sp.wait_ge(saved[s], 32 * (T // 2))

                    @block.scalar
                    def _(act):
                        def tile(i, s, first):
                            k = i * 2 + s
                            if not (first and s < 1):
                                act.wait_ge(turned, k)
                                act.sem_inc(act_gate, 1)
                            act.activation(left[:, s:s + 1, :], h[:, bass.ds(k, 1), :], ACT.Copy).then_inc(copied, 1)
                            act.wait_ge(turned, k + 1)
                            act.activation(left_t[:, s, :], turn_ps[:, 0:D], ACT.Copy).then_inc(evacuated, 1)
                            if not first:
                                act.wait_ge(saved[s], i * 32)
                            act.wait_ge(multiplied, k * 4 + 3)
                            act.activation(kv_slot[:, s, 2 * BANK:KV], out_ps[:, 2, 0:256], ACT.Copy)
                            act.activation(q_slot[:, s, 0:2, 0:D], out_ps[:, 2, 256:512].rearrange("p (r f) -> p r f", r=2), ACT.Copy)
                            act.wait_ge(multiplied, k * 4 + 4)
                            act.activation(q_slot[:, s, 2:5, 0:D], out_ps[:, 3, 0:384].rearrange("p (r f) -> p r f", r=3),
                                           ACT.Copy).then_inc(act_out, 1)
                        for s in range(2):
                            tile(0, s, True)
                        with act.Fori(1, T // 2) as i:
                            for s in range(2):
                                tile(i, s, False)

                    @block.tensor
                    def _(pe):
                        pe.wait_ge(loaded, 16 * (3 * R + 1))

                        def tile(i, s, first):
                            k = i * 2 + s
                            pe.wait_ge(copied, k + 1)
                            nc.tensor.transpose(turn_ps[:, 0:D], left[:, s, :], ident[:]).then_inc(turned, 1)
                            pe.wait_ge(evacuated, k + 1)
                            for b in range(4):
                                if b == 0 and not first:
                                    pe.wait_ge(dve_out, k)
                                if b == 2 and not first:
                                    pe.wait_ge(act_out, k)
                                cols = min(BANK, KV + R * D - b * BANK)
                                nc.tensor.matmul(out_ps[:, b, 0:cols], left_t[:, s, :], w[:, b * BANK:b * BANK + cols],
                                                 start=True, stop=True).then_inc(multiplied, 1)
                        tile(0, 0, True)
                        tile(0, 1, False)
                        with pe.Fori(1, T // 2) as i:
                            for s in range(2):
                                tile(i, s, False)

                    @block.vector
                    def _(dve):
                        dve.wait_ge(loaded, 16 * (3 * R + 1))
                        for s in range(2):
                            nc.vector.tensor_copy(q_slot[:, s, :, D:D + K2], bias[:]).then_inc(bias_in_place, 1)
                        dve.wait_ge(bias_in_place, 2)

                        def tile(i, s, first):
                            k = i * 2 + s
                            if not first:
                                dve.wait_ge(saved[s], i * 32)
                            dve.wait_ge(multiplied, k * 4 + 2)
                            nc.vector.tensor_copy(kv_slot[:, s, 0:2 * BANK], out_ps[:, 0:2, :].rearrange("p b f -> p (b f)")).then_inc(dve_out, 1)
                        for s in range(2):
                            tile(0, s, True)
                        with dve.Fori(1, T // 2) as i:
                            for s in range(2):
                                tile(i, s, False)

        def relation_logits(logits):
            st = Stage("logits2")
            with st:
                kv_idx = sb("kv_idx", [P, NS, G], I32, st)
                q_idx = sb("q_idx", [P, NS, G], I32, st)
                kv_rows = sb("kv_rows", [P, NS, G, 2 * D], F32, st)
                q_rows = sb("q_rows", [P, NS, G, D + K2], F32, st)
                prod = sb("prod", [P, 2, G, D], F32, st)
                dots = sb("dots", [P, 2, G, K2], F32, st)
                idx_ready, multiplied, reduced, scored = (sem("idx_ready", st), sem("multiplied", st), sem("reduced", st),
                                                          sem("scored", st))
                got, g0 = gathered, gathered_before(NS, 2 * C // NS)
                stored = [sem(f"stored{s}", st) for s in range(NS)]
                with nc.Block() as block:
                    @block.gpsimd
                    def _(pool):
                        def turn(i, first):
                            for s in range(NS):
                                pool.wait_ge(idx_ready, i * NS + s + 1)
                                if not first:
                                    pool.wait_ge(scored, i * NS + s + 1 - NS)
                                    pool.sem_inc(pool_gate, 1)
                                    pool.wait_ge(stored[s], i * 16)
                                pool.sem_inc(pool_gate, 1)
                                for j in range(G):
                                    nc.gpsimd.indirect_dma_start(
                                        out=kv_rows[:, s, j, :], out_offset=None, in_=kv_d,
                                        in_offset=bass.IndirectOffsetOnAxis(ap=kv_idx[:, s, j:j + 1], axis=0)).then_inc(got[s], 16)
                                    nc.gpsimd.indirect_dma_start(
                                        out=q_rows[:, s, j, :], out_offset=None, in_=q_d,
                                        in_offset=bass.IndirectOffsetOnAxis(ap=q_idx[:, s, j:j + 1], axis=0)).then_inc(got[s], 16)
                        turn(0, True)
                        with pool.Fori(1, TURNS) as i:
                            turn(i, False)

                    @block.scalar
                    def _(act):
                        act.activation(kv_idx[:], kv_i[:, 0:NS * G].rearrange("p (s g) -> p s g", s=NS), ACT.Copy)
                        act.activation(q_idx[:], q_i[:, 0:NS * G].rearrange("p (s g) -> p s g", s=NS), ACT.Copy).then_inc(idx_ready, NS)
                        with act.Fori(1, TURNS) as i:
                            for s in range(NS):
                                act.wait_ge(got[s], i * (32 * G) + g0[s])
                                act.sem_inc(act_gate, 1)
                                cols = bass.ds((i * NS + s) * G, G)
                                act.activation(kv_idx[:, s, :], kv_i[:, cols], ACT.Copy)
                                act.activation(q_idx[:, s, :], q_i[:, cols], ACT.Copy).then_inc(idx_ready, 1)

                    @block.vector
                    def _(dve):
                        with dve.Fori(0, TURNS) as i:
                            for s in range(NS):
                                k = i * NS + s
                                dve.wait_ge(got[s], i * (32 * G) + (g0[s] + 32 * G))
                                nc.vector.tensor_tensor(prod[:, s % 2, :, :], kv_rows[:, s, :, 0:D], q_rows[:, s, :, 0:D],
                                                        ALU.mult).then_inc(multiplied, 1)
                                dve.wait_ge(multiplied, k + 1)
                                nc.vector.tensor_reduce(dots[:, s % 2, :, :].rearrange("p j k -> p (j k)"),
                                                        prod[:, s % 2, :, :].rearrange("p j (k d) -> p (j k) d", k=K2),
                                                        AX.X, ALU.add).then_inc(reduced, 1)
                                dve.wait_ge(reduced, k + 1)
                                nc.vector.scalar_tensor_tensor(
                                    out=logits[:, :, bass.ds(k * G, G)].rearrange("p k j -> p j k"), in0=dots[:, s % 2, :, :],
                                    scalar=1.0 / float(D2) ** 0.5, in1=q_rows[:, s, :, D:D + K2], op0=ALU.mult,
                                    op1=ALU.add).then_inc(scored, 1)

                    @block.sync
                    def _(sp):
                        view = v_d.rearrange("(p c) f -> p c f", c=C)
                        with sp.Fori(0, TURNS) as i:
                            for s in range(NS):
                                c0 = sp.snap((i * NS + s) * G)
                                sp.wait_ge(got[s], i * (32 * G) + (g0[s] + 32 * G))
                                sp.sem_inc(sp_gate, 1)
                                sp.dma_start(view[:, bass.ds(c0, G), :], kv_rows[:, s, :, D:2 * D]).then_inc(stored[s], 16)
                        for s in range(NS):
                            sp.wait_ge(stored[s], 16 * TURNS)

        def spread_scratch(st, heads):
            e = {"heads": heads}
            e["stay"] = sb("stay", [P, C + 1], F32, st)
            e["pen_first"] = sb("pen_first", [P, C], F32, st)
            e["pen_last"] = sb("pen_last", [P, C], F32, st)
            e["pen_single"] = sb("pen_single", [P, P], F32, st)
            e["pen_link"] = sb("pen_link", [P, P], F32, st)
            e["ends"] = sb("ends", [P, 2, heads], F32, st)
            e["left"] = sb("left", [K2, P + 1], F32, st)
            e["right"] = sb("right", [K2, P + 1], F32, st)
            e["reach"] = sb("reach", [P, 2, heads], F32, st)
            e["ends_ps"] = pb("ends_ps", [P, 2, P], st)
            e["reach_ps"] = pb("reach_ps", [P, 2, K2], st)
            e["dve_turns"], e["pe_turns"] = sem("dve_turns", st), sem("pe_turns", st)
            return e

        def spread_prepare(line, e):
            for tile, mask in ((e["stay"][:, 0:C], cont), (e["pen_first"][:], in_first), (e["pen_last"][:], in_last),
                               (e["pen_single"][:], single_row), (e["pen_link"][:], link_row)):
                line.link(nc.vector.tensor_scalar(tile, mask[:], -1.0, -LOW, ALU.add, ALU.mult))
            line.link(nc.vector.memset(e["stay"][:, C:C + 1], LOW))
        PREPARES = 6

        def spread(dve, line, lanes, is_max, call, e):
            n, least = e["heads"], LOW if is_max else 0.0
            for k in range(n):
                ins = nc.vector.tensor_tensor_scan(lanes[:, k, :], e["stay"][:, 0:C] if is_max else cont[:], lanes[:, k, :], least,
                                                   ALU.add if is_max else ALU.mult, ALU.max if is_max else ALU.add)
                line.mark(ins)
            dve.wait_ge(line.sem, line.n)
            line.link(nc.vector.tensor_copy(e["ends"][:, 0, :], lanes[:, :, C - 1]))
            for k in range(n):
                ins = nc.vector.tensor_tensor_scan(lanes[:, k, ::-1], e["stay"][:, 1:C + 1][:, ::-1], lanes[:, k, ::-1], least,
                                                   ALU.add, ALU.max)
                line.mark(ins)
            dve.wait_ge(line.sem, line.n)
            nc.vector.tensor_copy(e["ends"][:, 1, :], lanes[:, :, 0]).then_inc(e["dve_turns"], 1)
            nc.vector.memset(e["left"][:, 0:1], least)
            line.link(nc.vector.memset(e["right"][:, P:P + 1], least))
            dve.wait_ge(e["pe_turns"], call * 2 + 1)
            op0, op1 = (ALU.add, ALU.max) if is_max else (ALU.mult, ALU.add)
            line.link(nc.vector.tensor_tensor_scan(e["left"][0:n, 1:P + 1], (e["pen_single"] if is_max else single_row)[0:n, :],
                                                   e["ends_ps"][0:n, 0, :], least, op0, op1))
            nc.vector.tensor_tensor_scan(e["right"][0:n, 0:P][:, ::-1], (e["pen_link"] if is_max else link_row)[0:n, ::-1],
                                         e["ends_ps"][0:n, 1, ::-1], least, op0, op1).then_inc(e["dve_turns"], 1)
            dve.wait_ge(e["pe_turns"], call * 2 + 2)
            line.link(nc.vector.tensor_copy(e["reach"][:], e["reach_ps"][:, :, 0:n]))
            for side, mask in ((0, e["pen_first"] if is_max else in_first), (1, e["pen_last"] if is_max else in_last)):
                for k in range(n):
                    line.mark(nc.vector.scalar_tensor_tensor(out=lanes[:, k, :], in0=mask[:], scalar=e["reach"][:, side, k:k + 1],
                                                             in1=lanes[:, k, :], op0=op0 if is_max else ALU.mult, op1=op1))
                dve.wait_ge(line.sem, line.n)

        def spread_pe(pe, call, e):
            n = e["heads"]
            pe.wait_ge(e["dve_turns"], call * 2 + 1)
            nc.tensor.transpose(e["ends_ps"][0:n, 0, :], e["ends"][:, 0, :], ident[:])
            nc.tensor.transpose(e["ends_ps"][0:n, 1, :], e["ends"][:, 1, :], ident[:]).then_inc(e["pe_turns"], 1)
            pe.wait_ge(e["dve_turns"], call * 2 + 2)
            pe.sem_inc(pe_gate, 1)
            nc.tensor.transpose(e["reach_ps"][:, 0, 0:n], e["left"][0:n, 0:P], ident[0:n, 0:n])
            nc.tensor.transpose(e["reach_ps"][:, 1, 0:n], e["right"][0:n, 1:P + 1], ident[0:n, 0:n]).then_inc(e["pe_turns"], 1)

        def spread_steps(heads):
            return 4 * heads + 4

        def relation_softmax(logits, weights):
            st = Stage("softmax2")
            with st:
                e = spread_scratch(st, K2)
                lanes = sb("lanes", [P, K2, C], F32, st)
                mask = sb("mask", [P, C], F32, st)
                number = sb("number", [P, R], F32, st)
                rel = sb("rel", [P, 1], F32, st)
                dve_steps, numbered, shifted, exped = sem("dve_steps", st), sem("numbered", st), sem("shifted", st), sem("exped", st)

                def all_heads(ap):
                    return ap.unsqueeze(1).to_broadcast([P, K2, C])

                with nc.Block() as block:
                    @block.gpsimd
                    def _(pool):
                        nc.gpsimd.iota(number[:], pattern=[[1, R]], base=0, channel_multiplier=0,
                                       allow_small_or_imprecise_dtypes=True).then_inc(numbered, 1)

                    @block.tensor
                    def _(pe):
                        with pe.Fori(0, 2 * R) as i:
                            spread_pe(pe, i, e)

                    @block.scalar
                    def _(act):
                        act.wait_ge(shifted, 1)
                        act.activation(logits[:], logits[:], ACT.Exp).then_inc(exped, 1)

                    @block.vector
                    def _(dve):
                        line = Line(dve, dve_steps)
                        spread_prepare(line, e)
                        line.link(nc.vector.memset(weights[:], NEG))
                        dve.wait_ge(numbered, 1)
                        base, per = line.n, spread_steps(K2) + 6
                        with dve.Fori(0, R) as r:
                            line.n = r * per + base
                            line.link(nc.vector.tensor_copy(rel[:], number[:, bass.ds(r, 1)]))
                            line.link(nc.vector.tensor_scalar(mask[:], type_f[:], rel[:, 0:1], 1.0e30, ALU.is_equal, ALU.mult))
                            line.link(nc.vector.tensor_scalar(mask[:], mask[:], NEG, None, ALU.add))
                            line.link(nc.vector.tensor_tensor(lanes[:], logits[:], all_heads(mask[:]), ALU.min))
                            spread(dve, line, lanes, True, r, e)
                            line.link(nc.vector.tensor_tensor(lanes[:], lanes[:], all_heads(mask[:]), ALU.min))
                            line.link(nc.vector.tensor_tensor(weights[:], weights[:], lanes[:], ALU.max))
                        line.n = base + R * per
                        nc.vector.tensor_tensor(logits[:], logits[:], weights[:], ALU.subtract).then_inc(shifted, 1)
                        dve.wait_ge(exped, 1)
                        line.link(nc.vector.memset(weights[:], 0.0))
                        base, per = line.n, spread_steps(K2) + 5
                        with dve.Fori(0, R) as r:
                            line.n = r * per + base
                            line.link(nc.vector.tensor_copy(rel[:], number[:, bass.ds(r, 1)]))
                            line.link(nc.vector.tensor_scalar(mask[:], type_f[:], rel[:, 0:1], None, ALU.is_equal))
                            line.link(nc.vector.tensor_tensor(lanes[:], logits[:], all_heads(mask[:]), ALU.mult))
                            spread(dve, line, lanes, False, r + R, e)
                            line.link(nc.vector.tensor_tensor(lanes[:], lanes[:], all_heads(mask[:]), ALU.mult))
                            line.link(nc.vector.tensor_tensor(weights[:], weights[:], lanes[:], ALU.add))
                        line.n = base + R * per
                        line.link(nc.vector.tensor_scalar(weights[:], weights[:], 1e-12, None, ALU.add))
                        line.link(nc.vector.reciprocal(weights[:], weights[:]))
                        line.link(nc.vector.tensor_tensor(weights[:], weights[:], logits[:], ALU.mult))

        def weighted_sum(name, rows_d, sums_d, weights, heads, top=None):
            W = D + heads if top is not None else D
            WS = W + heads if top is not None else D
            ops = 2 if top is not None else 1
            st = Stage(name)
            with st:
                rows = sb("rows", [P, NS, G, D], F32, st)
                prod = sb("prod", [P, 2, G, W], F32, st)
                sums = sb("sums", [P, NS, G, WS], F32, st)
                cleared, multiplied, summed, topped = (sem("cleared", st), sem("multiplied", st), sem("summed", st), sem("topped", st))
                got = [sem(f"got{s}", st) for s in range(NS)]
                stored = [sem(f"stored{s}", st) for s in range(NS)]
                with nc.Block() as block:
                    @block.sync
                    def _(sp):
                        view = rows_d.rearrange("(p c) f -> p c f", c=C)

                        def turn(i, first):
                            for s in range(NS):
                                c0 = (i * NS + s) * G if first else sp.snap((i * NS + s) * G)
                                if not first:
                                    sp.wait_ge(multiplied, (i * NS + s + 1 - NS) * ops)
                                    sp.sem_inc(sp_gate, 1)
                                sp.dma_start(rows[:, s, :, :], view[:, bass.ds(c0, G), :]).then_inc(got[s], 16)
                        turn(0, True)
                        with sp.Fori(1, TURNS) as i:
                            turn(i, False)

                    @block.vector
                    def _(dve):
                        nc.vector.memset(sums[:, NS - 1, G - 1, :], 0.0).then_inc(cleared, 1)
                        dve.wait_ge(cleared, 1)

                        def turn(i, first):
                            for s in range(NS):
                                k = i * NS + s
                                cols = bass.ds(k * G, G)
                                w_jk = weights[:, :, cols].rearrange("p k j -> p j k")
                                dve.wait_ge(got[s], i * 16 + 16)
                                nc.vector.tensor_tensor(
                                    prod[:, s % 2, :, 0:D].rearrange("p j (k d) -> p j k d", k=heads),
                                    rows[:, s, :, :].rearrange("p j (k d) -> p j k d", k=heads),
                                    over_heads(w_jk, heads, D // heads), ALU.mult).then_inc(multiplied, 1)
                                if top is not None:
                                    nc.vector.tensor_copy(prod[:, s % 2, :, D:W], w_jk).then_inc(multiplied, 1)
                                if not first:
                                    dve.wait_ge(stored[s], i * 16)
                                dve.wait_ge(multiplied, (k + 1) * ops)
                                for j in range(G):
                                    ps, pj = (s, j - 1) if j else ((s - 1) % NS, G - 1)
                                    if not (first and s == 0 and j == 0):
                                        dve.wait_ge(summed, i * (NS * G) + (s * G + j))
                                    nc.vector.scalar_tensor_tensor(
                                        out=sums[:, s, j, 0:W], in0=sums[:, ps, pj, 0:W],
                                        scalar=cont[:, bass.ds((i * NS + s) * G + j, 1)], in1=prod[:, s % 2, j, :],
                                        op0=ALU.mult, op1=ALU.add).then_inc(summed, 1)
                        turn(0, True)
                        with dve.Fori(1, TURNS) as i:
                            turn(i, False)
                        dve.wait_ge(summed, C)
                        nc.vector.tensor_copy(carry[:, 0:W], sums[:, NS - 1, G - 1, 0:W])

                    @block.scalar
                    def _(act):
                        view = sums_d.rearrange("(p c) f -> p c f", c=C)

                        def turn(i, first):
                            for s in range(NS):
                                k = i * NS + s
                                if top is not None:
                                    if not first:
                                        act.wait_ge(stored[s], i * 16)
                                        act.sem_inc(act_gate, 1)
                                    act.activation(sums[:, s, :, W:WS], top[:, :, bass.ds(k * G, G)].rearrange("p k j -> p j k"),
                                                   ACT.Copy).then_inc(topped, 1)
                                    act.wait_ge(topped, k + 1)
                                act.wait_ge(summed, (k + 1) * G)
                                act.dma_start(view[:, bass.ds(k * G, G), :], sums[:, s, :, :]).then_inc(stored[s], 16)
                        turn(0, True)
                        with act.Fori(1, TURNS) as i:
                            turn(i, False)
                        for s in range(NS):
                            act.wait_ge(stored[s], 16 * TURNS)

        def layer2_nodes():
            def scratch(st):
                e = {}
                linear_scratch(st, e, 1)
                for k in ("bias", "gamma", "beta", "wo"):
                    e[k] = sb(k, [P, D], F32, st)
                e["stats"] = sb("stats", [P, GN, 6], F32, st)
                for k in ("mean", "dev", "std"):
                    e[k] = sb(k, [P, GN], F32, st)
                e["eps"] = sb("eps", [P, 1], F32, st)
                for k in ("w_turned", "w_ready", "var_ready", "std_ready"):
                    e[k] = sem(k, st)

                def prepare(dve, line):
                    line.link(nc.vector.memset(e["eps"][:], LN_EPS))
                    dve.wait_ge(e["w_turned"], 1)
                    nc.vector.tensor_copy(e["w"][:, 0, :], e["lin_ps"][:, 0, :]).then_inc(e["w_ready"], 1)
                e["prepare"] = prepare
                return e

            def consts(sp, e):
                sp.dma_start(e["wo"][:], ow_in).then_inc(e["loaded"], 16)
                for k, src in (("bias", ob_in), ("gamma", lng_in), ("beta", lnb_in)):
                    sp.dma_start(e[k][:], src.rearrange("(a f) -> a f", a=1).to_broadcast([P, D])).then_inc(e["loaded"], 16)
                sp.wait_ge(e["loaded"], 64)

            def body(dve, line, k, total, reach, e):
                tiles = bass.ds(k * GN, GN)
                m = e["left"][:, 0, :, :]

                def tiled(ap):
                    return ap.unsqueeze(2).to_broadcast([P, GN, D])

                def rowed(ap):
                    return ap.unsqueeze(1).to_broadcast([P, GN, D])

                line.link(nc.vector.tensor_tensor(m, total[:, :, 0:D], reach[:, :, 0:D], ALU.add))
                nc.vector.tensor_tensor(m, m, tiled(has[:, tiles]), ALU.mult).then_inc(e["left_ready"], 1)
                dve.wait_ge(e["multiplied"], k + 1)
                line.link(nc.vector.tensor_tensor(m, e["lin_ps"][:], rowed(e["bias"][:]), ALU.add))
                line.link(nc.vector.tensor_tensor(m, m, h[:, tiles, :], ALU.add))
                for j in range(GN):
                    line.mark(nc.vector.bn_stats(e["stats"][:, j, :], e["left"][:, 0, j, :]))
                dve.wait_ge(line.sem, line.n)
                stats = e["stats"]
                line.link(nc.vector.tensor_tensor(e["mean"][:], stats[:, :, 1], stats[:, :, 4], ALU.add))
                line.link(nc.vector.tensor_scalar(e["mean"][:], e["mean"][:], 0.5, None, ALU.mult))
                line.link(nc.vector.tensor_tensor(e["dev"][:], stats[:, :, 1], stats[:, :, 4], ALU.subtract))
                line.link(nc.vector.scalar_tensor_tensor(out=e["dev"][:], in0=e["dev"][:], scalar=0.25, in1=e["dev"][:],
                                                         op0=ALU.mult, op1=ALU.mult))
                line.link(nc.vector.tensor_tensor(e["std"][:], stats[:, :, 2], stats[:, :, 5], ALU.add))
                nc.vector.scalar_tensor_tensor(out=e["dev"][:], in0=e["std"][:], scalar=1.0 / D, in1=e["dev"][:],
                                               op0=ALU.mult, op1=ALU.add).then_inc(e["var_ready"], 1)
                line.link(nc.vector.tensor_tensor(m, m, tiled(e["mean"][:]), ALU.subtract))
                dve.wait_ge(e["std_ready"], k + 1)
                line.link(nc.vector.reciprocal(e["std"][:], e["std"][:]))
                line.link(nc.vector.tensor_tensor(m, m, tiled(e["std"][:]), ALU.mult))
                line.link(nc.vector.tensor_tensor(m, m, rowed(e["gamma"][:]), ALU.mult))
                line.link(nc.vector.tensor_tensor(m, m, rowed(e["beta"][:]), ALU.add))
                line.link(nc.vector.tensor_tensor(x[:, tiles, :], x[:, tiles, :], m, ALU.add))

            def act_body(act, k, first, e):
                linear_act(act, k, first, e)
                act.wait_ge(e["var_ready"], k + 1)
                act.activation(e["std"][:], e["dev"][:], ACT.Sqrt, bias=e["eps"][:, 0:1]).then_inc(e["std_ready"], 1)

            def pe_start(pe, e):
                pe.wait_ge(e["loaded"], 64)
                nc.tensor.transpose(e["lin_ps"][:, 0, :], e["wo"][:], ident[:]).then_inc(e["w_turned"], 1)
                pe.wait_ge(e["w_ready"], 1)

            node_totals("nodes2", s2_d, D, D, 1, 3 + 5 + 5 + 6, scratch, consts, body, act_body, linear_pe, pe_start)

        def gat_tables(name, g, xw, selfs, first):
            w_in, a_src_in, a_dst_in = g[0], g[1], g[2]
            st = Stage(name)
            with st:
                w = sb("w", [P, D], F32, st)
                a_src = sb("a_src", [P, D], F32, st)
                a_dst = sb("a_dst", [P, D], F32, st)
                left = sb("left", [P, GN, D], F32, st)
                left_t = sb("left_t", [P, GN, D], F32, st)
                made = sb("made", [P, 2, GN, D + K3], F32, st)
                prod = sb("prod", [P, 2, GN, D], F32, st)
                pair = sb("pair", [P, GN, 2 * K3], F32, st)
                zeros = sb("zeros", [P, C, 2 * K3], F32, st) if first else None
                start_slot = sb("start_slot", [P, 2, GN], I32, st)
                self_slot = sb("self_slot", [P, 2, GN, 2 * K3], F32, st)
                turn_ps = pb("turn_ps", [P, GN, D], st)
                lin_ps = pb("lin_ps", [P, GN, D], st)
                loaded, copied, turned, evacuated = sem("loaded", st), sem("copied", st), sem("turned", st), sem("evacuated", st)
                multiplied, made_ready, dve_steps, all_made = (sem("multiplied", st), sem("made_ready", st), sem("dve_steps", st),
                                                               sem("all_made", st))
                zeroed, zeros_out, staged, selfs_saved = sem("zeroed", st), sem("zeros_out", st), sem("staged", st), sem("selfs_saved", st)
                saved = [sem(f"saved{s}", st) for s in range(2)]
                put, g0 = gathered, gathered_before(2, GN * NG // 2)
                per = 8
                with nc.Block() as block:
                    @block.sync
                    def _(sp):
                        sp.dma_start(w[:], w_in).then_inc(loaded, 16)
                        for tile, src in ((a_src, a_src_in), (a_dst, a_dst_in)):
                            sp.dma_start(tile[:], src.rearrange("(a k) d -> a (k d)", a=1).to_broadcast([P, D])).then_inc(loaded, 16)
                        if first:
                            sp.wait_ge(zeroed, 1)
                            sp.dma_start(start_rows_d.rearrange("(p c) f -> p (c f)", c=C),
                                         zeros[:].rearrange("p c f -> p (c f)")).then_inc(zeros_out, 16)
                            sp.wait_ge(zeros_out, 16)
                        view = xw_d.rearrange("(p t) f -> p t f", t=T)
                        with sp.Fori(0, NG // 2) as i:
                            for s in range(2):
                                t0 = sp.snap((i * 2 + s) * GN)
                                sp.wait_ge(made_ready, i * 2 + s + 1)
                                sp.sem_inc(sp_gate, 1)
                                sp.dma_start(view[:, bass.ds(t0, GN), :], made[:, s, :, :]).then_inc(saved[s], 16)
                        sp.wait_ge(all_made, 1)
                        sp.dma_start(self_d.rearrange("(p t) f -> p t f", t=T), selfs[:]).then_inc(selfs_saved, 16)
                        for s in range(2):
                            sp.wait_ge(saved[s], 16 * (NG // 2))
                        sp.wait_ge(selfs_saved, 16)

                    @block.scalar
                    def _(act):
                        def group(k, begin):
                            if not begin:
                                act.wait_ge(turned, k)
                                act.sem_inc(act_gate, 1)
                            act.activation(left[:], h[:, bass.ds(k * GN, GN), :], ACT.Copy).then_inc(copied, 1)
                            act.wait_ge(turned, k + 1)
                            if not begin:
                                act.wait_ge(multiplied, k)
                            act.activation(left_t[:], turn_ps[:], ACT.Copy).then_inc(evacuated, 1)
                        group(0, True)
                        with act.Fori(1, NG) as i:
                            group(i, False)
                        act.wait_ge(all_made, 1)

                        def stage(i, s, begin):
                            if not begin:
                                act.wait_ge(put[s], i * (16 * GN) + g0[s])
                                act.sem_inc(act_gate, 1)
                            tiles = bass.ds((i * 2 + s) * GN, GN)
                            act.activation(start_slot[:, s, :], start_i[:, tiles], ACT.Copy).then_inc(staged, 1)
                            act.activation(self_slot[:, s, :, :], selfs[:, tiles, :], ACT.Copy).then_inc(staged, 1)
                        for s in range(2):
                            stage(0, s, True)
                        with act.Fori(1, NG // 2) as i:
                            for s in range(2):
                                stage(i, s, False)

                    @block.gpsimd
                    def _(pool):
                        if first:
                            pool.wait_ge(zeros_out, 16)
                        with pool.Fori(0, NG // 2) as i:
                            for s in range(2):
                                pool.wait_ge(staged, i * 4 + (2 * s + 2))
                                pool.sem_inc(pool_gate, 1)
                                for j in range(GN):
                                    nc.gpsimd.indirect_dma_start(
                                        out=start_rows_d, in_=self_slot[:, s, j, :], in_offset=None,
                                        out_offset=bass.IndirectOffsetOnAxis(ap=start_slot[:, s, j:j + 1], axis=0),
                                        bounds_check=EP - 1, oob_is_err=False).then_inc(put[s], 16)
                        for s in range(2):
                            pool.wait_ge(put[s], g0[s] + 16 * GN * (NG // 2))

                    @block.tensor
                    def _(pe):
                        pe.wait_ge(loaded, 48)

                        def group(k, begin):
                            pe.wait_ge(copied, k + 1)
                            for j in range(GN):
                                ins = nc.tensor.transpose(turn_ps[:, j, :], left[:, j, :], ident[:])
                            ins.then_inc(turned, 1)
                            pe.wait_ge(evacuated, k + 1)
                            if not begin:
                                pe.wait_ge(made_ready, k)
                            for j in range(GN):
                                ins = nc.tensor.matmul(lin_ps[:, j, :], left_t[:, j, :], w[:], start=True, stop=True)
                            ins.then_inc(multiplied, 1)
                        group(0, True)
                        with pe.Fori(1, NG) as i:
                            group(i, False)

                    @block.vector
                    def _(dve):
                        line = Line(dve, dve_steps)
                        if first:
                            nc.vector.memset(zeros[:], 0.0).then_inc(zeroed, 1)
                        dve.wait_ge(loaded, 48)

                        def group(i, s, begin):
                            k = i * 2 + s
                            tiles = bass.ds(k * GN, GN)
                            m = made[:, s, :, 0:D]
                            line.n = k * per
                            if not begin:
                                dve.wait_ge(saved[s], i * 16)
                            dve.wait_ge(multiplied, k + 1)
                            line.link(nc.vector.tensor_copy(m, lin_ps[:]))
                            line.link(nc.vector.tensor_copy(xw[:, tiles, :], m))
                            for n, a in ((0, a_src), (1, a_dst)):
                                line.mark(nc.vector.tensor_tensor(prod[:, n, :, :], m, a[:].unsqueeze(1).to_broadcast([P, GN, D]), ALU.mult))
                            dve.wait_ge(line.sem, line.n)
                            for n, o in ((0, made[:, s, :, D:D + K3]), (1, pair[:, :, 0:K3])):
                                line.mark(nc.vector.tensor_reduce(o, prod[:, n, :, :].rearrange("p j (k d) -> p j k d", k=K3), AX.X, ALU.add))
                            dve.wait_ge(line.sem, line.n)
                            line.link(nc.vector.tensor_tensor(pair[:, :, K3:2 * K3], made[:, s, :, D:D + K3], pair[:, :, 0:K3], ALU.add))
                            line.link(nc.vector.scalar_tensor_tensor(out=pair[:, :, K3:2 * K3], in0=pair[:, :, K3:2 * K3], scalar=0.2,
                                                                     in1=pair[:, :, K3:2 * K3], op0=ALU.mult, op1=ALU.max))
                            nc.vector.tensor_copy(selfs[:, tiles, :], pair[:]).then_inc(made_ready, 1)
                        for s in range(2):
                            group(0, s, True)
                        with dve.Fori(1, NG // 2) as i:
                            for s in range(2):
                                group(i, s, False)
                        dve.wait_ge(made_ready, NG)
                        nc.vector.memset(prod[:, 0, 0, 0:1], 0.0).then_inc(all_made, 1)

        def gat_gather(name, al):
            st = Stage(name)
            with st:
                idx_slot = sb("idx_slot", [P, NS, G], I32, st)
                rows = sb("rows", [P, NS, G, D + K3], F32, st)
                idx_ready, taken = sem("idx_ready", st), sem("taken", st)
                got, g0 = gathered, gathered_before(NS, C // NS)
                stored = [sem(f"stored{s}", st) for s in range(NS)]
                with nc.Block() as block:
                    @block.gpsimd
                    def _(pool):
                        def turn(i, first):
                            for s in range(NS):
                                pool.wait_ge(idx_ready, i * NS + s + 1)
                                if not first:
                                    pool.wait_ge(taken, i * NS + s + 1 - NS)
                                    pool.sem_inc(pool_gate, 1)
                                    pool.wait_ge(stored[s], i * 16)
                                pool.sem_inc(pool_gate, 1)
                                for j in range(G):
                                    nc.gpsimd.indirect_dma_start(
                                        out=rows[:, s, j, :], out_offset=None, in_=xw_d,
                                        in_offset=bass.IndirectOffsetOnAxis(ap=idx_slot[:, s, j:j + 1], axis=0)).then_inc(got[s], 16)
                        turn(0, True)
                        with pool.Fori(1, TURNS) as i:
                            turn(i, False)

                    @block.scalar
                    def _(act):
                        act.activation(idx_slot[:], src_i[:, 0:NS * G].rearrange("p (s g) -> p s g", s=NS),
                                       ACT.Copy).then_inc(idx_ready, NS)
                        with act.Fori(1, TURNS) as i:
                            for s in range(NS):
                                act.wait_ge(got[s], i * (16 * G) + g0[s])
                                act.sem_inc(act_gate, 1)
                                act.activation(idx_slot[:, s, :], src_i[:, bass.ds((i * NS + s) * G, G)],
                                               ACT.Copy).then_inc(idx_ready, 1)

                    @block.vector
                    def _(dve):
                        with dve.Fori(0, TURNS) as i:
                            for s in range(NS):
                                dve.wait_ge(got[s], i * (16 * G) + (g0[s] + 16 * G))
                                nc.vector.tensor_scalar(al[:, :, bass.ds((i * NS + s) * G, G)].rearrange("p k j -> p j k"),
                                                        rows[:, s, :, D:D + K3], 1.0, None, ALU.mult).then_inc(taken, 1)

                    @block.sync
                    def _(sp):
                        view = xe_d.rearrange("(p c) f -> p c f", c=C)
                        with sp.Fori(0, TURNS) as i:
                            for s in range(NS):
                                c0 = sp.snap((i * NS + s) * G)
                                sp.wait_ge(got[s], i * (16 * G) + (g0[s] + 16 * G))
                                sp.sem_inc(sp_gate, 1)
                                sp.dma_start(view[:, bass.ds(c0, G), :], rows[:, s, :, 0:D]).then_inc(stored[s], 16)
                        for s in range(NS):
                            sp.wait_ge(stored[s], 16 * TURNS)

        def gat_weights(name, al, top):
            st = Stage(name)
            with st:
                e = spread_scratch(st, K3)
                at_start = sb("at_start", [P, C, 2 * K3], F32, st)
                held = sb("held", [P, 2 * K3, C], F32, st)
                initial = sb("initial", [P, 2 * K3], F32, st)
                got_start, got_initial, dve_steps = sem("got_start", st), gathered[0], sem("dve_steps", st)
                g0 = gathered_before(1, 1)
                shifted, exped = sem("shifted", st), sem("exped", st)
                with nc.Block() as block:
                    @block.sync
                    def _(sp):
                        sp.dma_start(at_start[:].rearrange("p c f -> p (c f)"),
                                     start_rows_d.rearrange("(p c) f -> p (c f)", c=C)).then_inc(got_start, 16)
                        sp.wait_ge(got_start, 16)

                    @block.gpsimd
                    def _(pool):
                        nc.gpsimd.indirect_dma_start(out=initial[:], out_offset=None, in_=self_d,
                                                     in_offset=bass.IndirectOffsetOnAxis(ap=dst0_i[:], axis=0)).then_inc(got_initial, 16)

                    @block.tensor
                    def _(pe):
                        spread_pe(pe, 0, e)

                    @block.scalar
                    def _(act):
                        act.wait_ge(shifted, 1)
                        act.activation(al[:], al[:], ACT.Exp).then_inc(exped, 1)
                        act.wait_ge(exped, 1)

                    @block.vector
                    def _(dve):
                        line = Line(dve, dve_steps)
                        spread_prepare(line, e)
                        dve.wait_ge(got_start, 16)
                        dve.wait_ge(got_initial, g0[0] + 16)
                        for k in range(2 * K3):
                            line.mark(nc.vector.tensor_tensor_scan(held[:, k, :], cont[:], at_start[:, :, k], initial[:, k:k + 1],
                                                                   ALU.mult, ALU.add))
                        dve.wait_ge(line.sem, line.n)
                        line.link(nc.vector.tensor_tensor(al[:], al[:], held[:, 0:K3, :], ALU.add))
                        line.link(nc.vector.scalar_tensor_tensor(out=al[:], in0=al[:], scalar=0.2, in1=al[:], op0=ALU.mult, op1=ALU.max))
                        line.link(nc.vector.tensor_copy(top[:], al[:]))
                        spread(dve, line, top, True, 0, e)
                        line.link(nc.vector.tensor_tensor(top[:], top[:], held[:, K3:2 * K3, :], ALU.max))
                        nc.vector.tensor_tensor(al[:], al[:], top[:], ALU.subtract).then_inc(shifted, 1)

        def gat_nodes(name, g, xw, selfs):
            def scratch(st):
                e = {"a": sb("a", [P, GN, D], F32, st), "own": sb("own", [P, GN, D], F32, st),
                     "bias": sb("bias", [P, D], F32, st), "loaded": sem("loaded", st),
                     "logit_ready": sem("logit_ready", st), "exped": sem("exped", st)}
                for k in ("den", "top", "alone", "weight"):
                    e[k] = sb(k, [P, GN, K3], F32, st)

                def prepare(dve, line):
                    dve.wait_ge(e["loaded"], 16)
                e["prepare"] = prepare
                return e

            def consts(sp, e):
                sp.dma_start(e["bias"][:], g[3].rearrange("(a f) -> a f", a=1).to_broadcast([P, D])).then_inc(e["loaded"], 16)
                sp.wait_ge(e["loaded"], 16)

            def body(dve, line, k, total, reach, e):
                tiles = bass.ds(k * GN, GN)
                a, den, top, alone, own = e["a"], e["den"], e["top"], e["alone"], e["own"]
                self_logit = selfs[:, tiles, K3:2 * K3]
                has_k = has[:, tiles].unsqueeze(2).to_broadcast([P, GN, K3])
                line.mark(nc.vector.tensor_tensor(top[:], total[:, :, D + K3:D + 2 * K3], has_k, ALU.mult))
                line.link(nc.vector.tensor_tensor(alone[:], self_logit, hasnt[:, tiles].unsqueeze(2).to_broadcast([P, GN, K3]), ALU.mult))
                line.link(nc.vector.tensor_tensor(top[:], top[:], alone[:], ALU.add))
                nc.vector.tensor_tensor(alone[:], self_logit, top[:], ALU.subtract).then_inc(e["logit_ready"], 1)
                line.mark(nc.vector.tensor_tensor(a[:], total[:, :, 0:D], reach[:, :, 0:D], ALU.add))
                line.link(nc.vector.tensor_tensor(den[:], total[:, :, D:D + K3], reach[:, :, D:D + K3], ALU.add))
                line.mark(nc.vector.tensor_tensor(a[:], a[:], has[:, tiles].unsqueeze(2).to_broadcast([P, GN, D]), ALU.mult))
                line.link(nc.vector.tensor_tensor(den[:], den[:], has_k, ALU.mult))
                dve.wait_ge(e["exped"], k + 1)
                weight = e["weight"]
                line.mark(nc.vector.tensor_tensor(den[:], den[:], weight[:], ALU.add))
                line.link(nc.vector.tensor_tensor(own[:].rearrange("p j (k d) -> p j k d", k=K3),
                                                  xw[:, tiles, :].rearrange("p j (k d) -> p j k d", k=K3),
                                                  over_heads(weight[:], K3, D3), ALU.mult))
                line.mark(nc.vector.tensor_tensor(a[:], a[:], own[:], ALU.add))
                line.link(nc.vector.reciprocal(den[:], den[:]))
                av = a[:].rearrange("p j (k d) -> p j k d", k=K3)
                line.link(nc.vector.tensor_tensor(av, av, over_heads(den[:], K3, D3), ALU.mult))
                line.link(nc.vector.tensor_tensor(h[:, tiles, :], a[:], e["bias"][:].unsqueeze(1).to_broadcast([P, GN, D]), ALU.add))

            def act_body(act, k, first, e):
                act.wait_ge(e["logit_ready"], k + 1)
                act.activation(e["weight"][:], e["alone"][:], ACT.Exp).then_inc(e["exped"], 1)

            node_totals(name, s3_d, WG, D + K3, 0, 13, scratch, consts, body, act_body)

        def batch_norm_elu(name, g, last):
            st = Stage(name)
            with st:
                squares = sb("squares", [P, T, D], F32, st)
                part = sb("part", [P, D], F32, st)
                valid = sb("valid", [P, P], F32, st)
                mean = sb("mean", [P, D], F32, st)
                std = sb("std", [P, D], F32, st)
                gamma = sb("gamma", [P, D], F32, st)
                beta = sb("beta", [P, D], F32, st)
                eps = sb("eps", [P, 1], F32, st)
                real = sb("real", [P, 1], F32, st)
                tot_ps = pb("tot_ps", [P, D], st)
                loaded, part_ready, totalled, dve_steps = sem("loaded", st), sem("part_ready", st), sem("totalled", st), sem("dve_steps", st)
                std_ready, low_ready, exped = sem("std_ready", st), sem("low_ready", st), sem("exped", st)

                def all_tiles(ap):
                    return ap.unsqueeze(1).to_broadcast([P, T, D])

                with nc.Block() as block:
                    @block.sync
                    def _(sp):
                        for tile, src in ((gamma, g[4]), (beta, g[5])):
                            sp.dma_start(tile[:], src.rearrange("(a f) -> a f", a=1).to_broadcast([P, D])).then_inc(loaded, 16)
                        sp.wait_ge(loaded, 32)

                    @block.tensor
                    def _(pe):
                        for n in range(2):
                            pe.wait_ge(part_ready, n + 1)
                            nc.tensor.matmul(tot_ps[:], valid[:], part[:], start=True, stop=True).then_inc(totalled, 1)

                    @block.scalar
                    def _(act):
                        act.wait_ge(totalled, 2)
                        act.activation(std[:], tot_ps[:], ACT.Sqrt, bias=eps[:, 0:1], scale=1.0 / N).then_inc(std_ready, 1)
                        act.wait_ge(low_ready, 1)
                        act.activation(squares[:], squares[:], ACT.Exp).then_inc(exped, 1)

                    @block.vector
                    def _(dve):
                        line = Line(dve, dve_steps)
                        line.link(nc.vector.memset(eps[:], LN_EPS))
                        line.link(nc.vector.tensor_scalar(real[:], lane[:], float(PN), None, ALU.is_lt))
                        line.link(nc.vector.tensor_copy(valid[:], real[:].to_broadcast([P, P])))
                        nc.vector.tensor_reduce(part[:], h[:].rearrange("p t f -> p f t"), AX.X, ALU.add).then_inc(part_ready, 1)
                        dve.wait_ge(totalled, 1)
                        line.link(nc.vector.tensor_scalar(mean[:], tot_ps[:], 1.0 / N, None, ALU.mult))
                        line.link(nc.vector.tensor_tensor(h[:], h[:], all_tiles(mean[:]), ALU.subtract))
                        line.link(nc.vector.tensor_tensor(squares[:], h[:], h[:], ALU.mult))
                        nc.vector.tensor_reduce(part[:], squares[:].rearrange("p t f -> p f t"), AX.X, ALU.add).then_inc(part_ready, 1)
                        dve.wait_ge(std_ready, 1)
                        line.link(nc.vector.reciprocal(std[:], std[:]))
                        dve.wait_ge(loaded, 32)
                        line.link(nc.vector.tensor_tensor(std[:], std[:], gamma[:], ALU.mult))
                        line.link(nc.vector.tensor_tensor(h[:], h[:], all_tiles(std[:]), ALU.mult))
                        line.link(nc.vector.tensor_tensor(h[:], h[:], all_tiles(beta[:]), ALU.add))
                        nc.vector.tensor_scalar(squares[:], h[:], 0.0, None, ALU.min).then_inc(low_ready, 1)
                        line.link(nc.vector.tensor_scalar(h[:], h[:], 0.0, None, ALU.max))
                        dve.wait_ge(exped, 1)
                        line.link(nc.vector.scalar_tensor_tensor(out=h[:], in0=squares[:], scalar=-1.0, in1=h[:], op0=ALU.add, op1=ALU.add))
                        if last:
                            line.link(nc.vector.tensor_tensor(x[:], x[:], h[:], ALU.add))

        def finish():
            st = Stage("finish")
            with st:
                written = sem("written", st)
                with nc.Block() as block:
                    @block.sync
                    def _(sp):
                        ov = out.rearrange("(p t) f -> p t f", t=T)
                        sp.dma_start(ov[0:112], x[0:112, :, :]).then_inc(written, 16)
                        sp.dma_start(ov[112:PN], x[112:PN, :, :]).then_inc(written, 16)
                        sp.wait_ge(written, 32)

        setup()
        norm_relu("norm0", h0_d)
        gather_sum("sum0", h0_d, s0_d, True)
        chain_runs("chain0", [(0, D, False), (D, D, True)])
        layer0_nodes()
        norm_relu("norm1", h1_d)
        gather_sum("sum1", h1_d, s1_d, False)
        chain_runs("chain1", [(0, D, False)])
        layer1_nodes()
        norm_relu("norm2", None)
        relation_tables()
        with ExitStack() as keep:
            weights = sb("weights2", [P, K2, C], F32, keep)
            with ExitStack() as short:
                logits = sb("logits2", [P, K2, C], F32, short)
                relation_logits(logits)
                relation_softmax(logits, weights)
            weighted_sum("sum2", v_d, s2_d, weights, K2)
        chain_runs("chain2", [(0, D, False)])
        layer2_nodes()
        renew_semaphores()
        norm_relu("norm3", None)
        with ExitStack() as keep:
            xw = sb("xw", [P, T, D], F32, keep)
            selfs = sb("selfs", [P, T, 2 * K3], F32, keep)
            for n, g in enumerate(g3):
                if n:
                    renew_semaphores()
                gat_tables(f"tables3{n}", g, xw, selfs, n == 0)
                with ExitStack() as edges:
                    al = sb(f"al{n}", [P, K3, C], F32, edges)
                    top = sb(f"top{n}", [P, K3, C], F32, edges)
                    gat_gather(f"gather3{n}", al)
                    gat_weights(f"weights3{n}", al, top)
                    weighted_sum(f"sum3{n}", xe_d, s3_d, al, K3, top)
                chain_runs(f"chain3{n}", [(0, D, False), (D, K3, False)])
                gat_nodes(f"nodes3{n}", g, xw, selfs)
                batch_norm_elu(f"bn3{n}", g, n == 1)
        finish()


_INS = ['x', 'src', 'dst', 'edge_type_5', 'L0_gnn_z_agg_hard', 'L1_gnn_W', 'L1_gnn_b', 'L2_gnn_W_Q', 'L2_gnn_W_K',
        'L2_gnn_W_V', 'L2_gnn_attn_bias', 'L2_gnn_out_proj_w', 'L2_gnn_out_proj_b', 'L2_gnn_ln_gamma',
        'L2_gnn_ln_beta', 'L3_gnn_W1', 'L3_gnn_a1_src', 'L3_gnn_a1_dst', 'L3_gnn_b1', 'L3_gnn_g1', 'L3_gnn_beta1',
        'L3_gnn_W2', 'L3_gnn_a2_src', 'L3_gnn_a2_dst', 'L3_gnn_b2', 'L3_gnn_g2', 'L3_gnn_beta2']


def kernel(**inputs):
    import numpy as _np
    import concourse.bacc as _bacc
    from concourse import mybir as _mybir
    from concourse.bass_utils import run_bass_kernel_spmd as _run

    nc = _bacc.Bacc("TRN2", target_bir_lowering=False, num_devices=1)
    arrays, args = {}, []
    for name in _INS:
        a = _np.ascontiguousarray(inputs[name])
        arrays[f"in_{name}_dram"] = a
        args.append(nc.dram_tensor(f"in_{name}_dram", a.shape, _mybir.dt.from_np(a.dtype), kind="ExternalInput").ap())
    result = nc.dram_tensor("out_0_dram", (N, D), _mybir.dt.float32, kind="ExternalOutput").ap()
    build(nc, *args[:15], [args[15:21], args[21:27]], result)
    r = _run(nc, [arrays], core_ids=[0])
    return r.results[0]["out_0_dram"]
```

```python
import concourse.bass as bass
from concourse import mybir
from contextlib import ExitStack

F32 = mybir.dt.float32
BF16 = mybir.dt.bfloat16
I32 = mybir.dt.int32
ALU = mybir.AluOpType
ACT = mybir.ActivationFunctionType
AX = mybir.AxisListType

P = 128
N = 6250
E = 106250
D = 128
T = N // 125
PN = N // T
NP = P * T
G = 8
NS = 4
C = -(-E // (P * G * NS)) * G * NS
EP = P * C
TURNS = C // (G * NS)
LAST = E - (P - 1) * C
GN = 5
NG = T // GN
FAR = 1 << 20
NEG = -1.0e9
LOW = -1.0e38
R = 5
K2 = 8
D2 = D // K2
K3 = 4
D3 = D // K3
LN_EPS = 1e-5
WH = D3 + 1
WS3 = K3 * WH
WG = WS3 + K3
BW = G * NS
BS = 2
BTURNS = C // (BW * BS)
assert BTURNS * BW * BS == C


class Line:

    def __init__(self, engine, sem):
        self.engine, self.sem, self.n = engine, sem, 0

    def mark(self, instruction):
        self.n = self.n + 1
        instruction.then_inc(self.sem, 1)
        return self.n

    def link(self, instruction):
        self.engine.wait_ge(self.sem, self.mark(instruction))


def over_heads(ap, heads, width):
    return ap.unsqueeze(3).to_broadcast([ap.shape[0], ap.shape[1], heads, width])


def build(nc, x_in, src_in, dst_in, type_in, z_in, w1_in, b1_in, wq_in, wk_in, wv_in, bias_in, ow_in, ob_in,
          lng_in, lnb_in, g3, out):
    ctx = ExitStack()
    with ctx:
        def dram(name, shape):
            return nc.dram_tensor(name, shape, F32, kind="Internal").ap()

        class Stage(ExitStack):
            def __init__(self, name):
                super().__init__()
                self.name = name + "_"
                stage_names.append(name)
                assert len(set(stage_names)) == len(stage_names)

        stage_names = []

        def getname(at):
            return at.name if isinstance(at, Stage) else ""

        def sb(name, shape, dt=F32, at=ctx):
            return at.enter_context(nc.sbuf_tensor(getname(at) + name, shape, dt))

        def pb(name, shape, at=ctx):
            free = 1
            for n in shape[1:]:
                free *= n
            bank = nc.PSUM_BANK_SIZE_BYTES // 4
            whole = at.enter_context(nc.psum_tensor(getname(at) + name, [shape[0], -(-free // bank) * bank], F32))
            view = whole[:, 0:free]
            return view if len(shape) == 2 else view.rearrange("p (a b) -> p a b", a=shape[1])

        def sem(name, at=ctx):
            return at.enter_context(nc.semaphore(getname(at) + name))

        dst_d = dram("dst_d", [P, C])
        start_d = dram("start_d", [NP + 1])
        run_d = dram("run_d", [NP + 1])
        h0_d = dram("h0_d", [NP, D])
        h1_d = dram("h1_d", [NP, D])
        s0_d = dram("s0_d", [EP, 2 * D])
        s1_d = dram("s1_d", [EP, D])
        kv_d = dram("kv_d", [NP * R, 2 * D])
        q_d = dram("q_d", [NP * R, D + K2])
        v_d = dram("v_d", [EP, D])
        s2_d = dram("s2_d", [EP, D])
        xw_d = dram("xw_d", [NP, WG])
        self_d = dram("self_d", [NP, 2 * K3])
        start_rows_d = dram("start_rows_d", [EP, K3])
        s3_d = dram("s3_d", [EP, WG])

        x = sb("x", [P, T, D])
        h = sb("h", [P, T, D])
        ident = sb("ident", [P, P])
        lane = sb("lane", [P, 1])
        src_i = sb("src_i", [P, C], I32)
        cont = sb("cont", [P, C])
        in_first = sb("in_first", [P, C])
        in_last = sb("in_last", [P, C])
        kv_i = sb("kv_i", [P, C], I32)
        q_i = sb("q_i", [P, C], I32)
        type_f = sb("type_f", [P, C])
        single_row = sb("single_row", [P, P])
        link_row = sb("link_row", [P, P])
        run_rows = sb("run_rows", [P, T, P], BF16)
        end_i = sb("end_i", [P, T], I32)
        start_i = sb("start_i", [P, T], I32)
        dst0_i = sb("dst0_i", [P, 1], I32)
        has = sb("has", [P, T])
        low_without = sb("low_without", [P, T])
        low_unreached = sb("low_unreached", [P, T])
        rdeg = sb("rdeg", [P, T])
        carry = sb("carry", [P, 2 * D])

        gathered = [sem(f"gathered{s}") for s in range(BS * NS)]
        gathered_count = [0] * (BS * NS)

        def gathered_before(slots, dmas):
            before = list(gathered_count)
            for s in range(slots):
                gathered_count[s] += 16 * dmas
            return before

        initial_gathered = sem("initial_gathered")

        pool_gate, sp_gate, act_gate, pe_gate = sem("pool_gate"), sem("sp_gate"), sem("act_gate"), sem("pe_gate")

        def renew_semaphores():
            nc.all_engine_barrier(sems_to_clear=range(pe_gate.num + 1, 256))

        def rows_of_edges(flat, first, count):
            return flat[first:first + count * C].rearrange("(p c) -> p c", c=C)

        def setup():
            st = Stage("setup")
            with st:
                dst_i = sb("dst_i", [P, C], I32, st)
                prev_i = sb("prev_i", [P, C], I32, st)
                next_i = sb("next_i", [P, 1], I32, st)
                type_i = sb("type_i", [P, C], I32, st)
                dst_f = sb("dst_f", [P, C], F32, st)
                prev_f = sb("prev_f", [P, C], F32, st)
                next_f = sb("next_f", [P, 1], F32, st)
                src_f = sb("src_f", [P, C], F32, st)
                tmp = sb("tmp", [P, C], F32, st)
                ids = sb("ids", [P, T], F32, st)
                wide = sb("wide", [P, GN, P], F32, st)
                below = sb("below", [P, GN, P], F32, st)
                first_row = sb("first_row", [P, P], F32, st)
                runs = sb("runs", [P, T], F32, st)
                run_i = sb("run_i", [P, T], I32, st)
                ids_slot = sb("ids_slot", [P, GN], F32, st)
                cnt_slot = sb("cnt_slot", [P, GN], F32, st)
                cnt = sb("cnt", [P, T], F32, st)
                start = sb("start", [P, T], F32, st)
                after = sb("after", [P, T], F32, st)
                run_after = sb("run_after", [P, T], F32, st)
                ends = sb("ends", [P, 2], F32, st)
                t0 = sb("t0", [P, T], F32, st)
                t1 = sb("t1", [P, T], F32, st)
                deg = sb("deg", [P, T], F32, st)
                run_sel = sb("run_sel", [P, T], F32, st)
                dst_rows = sb("dst_rows", [P, 2, GN, C], F32, st)
                idx_slot = sb("idx_slot", [P, 2, GN], I32, st)
                row_ps = pb("row_ps", [P, GN, P], st)

                cleared, loaded, iotas = sem("cleared", st), sem("loaded", st), sem("iotas", st)
                dst_saved, nodes_saved, nodes_back = (sem("dst_saved", st), sem("nodes_saved", st),
                                                      sem("nodes_back", st))
                dve_steps, wide_ready, rows_ready = sem("dve_steps", st), sem("wide_ready", st), sem("rows_ready", st)
                runs_ready, idx_ready, dst_ready = sem("runs_ready", st), sem("idx_ready", st), sem("dst_ready", st)
                starts_ready, rows_copied = sem("starts_ready", st), sem("rows_copied", st)
                got, g0 = gathered, gathered_before(2, GN * NG // 2)
                counted = sem("counted", st)

                with nc.Block() as block:
                    @block.sync
                    def _(sp):
                        sp.wait_ge(cleared, 6)
                        parts = [(0, 112), (112, P - 1)]
                        for tile, flat in ((dst_i, dst_in), (src_i, src_in), (type_i, type_in)):
                            for a, b in parts:
                                sp.dma_start(tile[a:b, :], rows_of_edges(flat, a * C, b - a)).then_inc(loaded, 16)
                            sp.dma_start(tile[P - 1:P, 0:LAST],
                                         flat[(P - 1) * C:E].rearrange("(a c) -> a c", a=1)).then_inc(loaded, 16)
                        for a, b in ((1, 113), (113, P - 1)):
                            sp.dma_start(prev_i[a:b, :], rows_of_edges(dst_in, a * C - 1, b - a)).then_inc(loaded, 16)
                        sp.dma_start(prev_i[P - 1:P, 0:LAST],
                                     dst_in[(P - 1) * C - 1:E - 1].rearrange("(a c) -> a c", a=1)).then_inc(loaded, 16)
                        sp.dma_start(prev_i[0:1, 1:C], dst_in[0:C - 1].rearrange("(a c) -> a c", a=1)).then_inc(loaded, 16)
                        sp.dma_start(next_i[0:P - 2, :], rows_of_edges(dst_in, C, P - 2)[:, 0:1],
                                     allow_slow_non_contiguous=True).then_inc(loaded, 16)
                        sp.dma_start(next_i[P - 2:P - 1, :],
                                     dst_in[(P - 1) * C:(P - 1) * C + 1].rearrange("(a c) -> a c", a=1)).then_inc(loaded, 16)
                        xv = x_in.rearrange("(p t) f -> p t f", t=T)
                        sp.dma_start(x[0:112, :, :], xv[0:112]).then_inc(loaded, 16)
                        sp.dma_start(x[112:PN, :, :], xv[112:PN]).then_inc(loaded, 16)
                        sp.wait_ge(dst_ready, 1)
                        sp.dma_start(dst_d, dst_f[:]).then_inc(dst_saved, 16)
                        sp.wait_ge(starts_ready, 1)
                        sp.dma_start(start_d[0:NP].rearrange("(p t) -> p t", t=T), start[:]).then_inc(nodes_saved, 16)
                        sp.dma_start(run_d[0:NP].rearrange("(p t) -> p t", t=T), runs[:]).then_inc(nodes_saved, 16)
                        sp.dma_start(start_d[NP:NP + 1].rearrange("(a c) -> a c", a=1), ends[0:1, 0:1]).then_inc(nodes_saved, 16)
                        sp.dma_start(run_d[NP:NP + 1].rearrange("(a c) -> a c", a=1), ends[0:1, 1:2]).then_inc(nodes_saved, 16)
                        sp.wait_ge(nodes_saved, 64)
                        sp.dma_start(after[:], start_d[1:NP + 1].rearrange("(p t) -> p t", t=T)).then_inc(nodes_back, 16)
                        sp.dma_start(run_after[:], run_d[1:NP + 1].rearrange("(p t) -> p t", t=T)).then_inc(nodes_back, 16)
                        sp.wait_ge(nodes_back, 32)

                    @block.gpsimd
                    def _(pool):
                        nc.gpsimd.memset(ident[:], 0.0).then_inc(iotas, 1)
                        pool.wait_ge(iotas, 1)
                        nc.gpsimd.affine_select(out=ident[:], in_=ident[:], compare_op=ALU.not_equal, fill=1.0,
                                                base=0, pattern=[[-1, P]], channel_multiplier=1).then_inc(iotas, 1)
                        nc.gpsimd.iota(lane[:], pattern=[[0, 1]], base=0, channel_multiplier=1,
                                       allow_small_or_imprecise_dtypes=True).then_inc(iotas, 1)
                        nc.gpsimd.iota(ids[:], pattern=[[1, T]], base=0, channel_multiplier=T,
                                       allow_small_or_imprecise_dtypes=True).then_inc(iotas, 1)
                        pool.wait_ge(dst_saved, 16)

                        def gathers(i, s):
                            pool.wait_ge(idx_ready, i * 2 + s + 1)
                            pool.sem_inc(pool_gate, 1)
                            for j in range(GN):
                                nc.gpsimd.indirect_dma_start(
                                    out=dst_rows[:, s, j, :], out_offset=None, in_=dst_d,
                                    in_offset=bass.IndirectOffsetOnAxis(ap=idx_slot[:, s, j:j + 1], axis=0)
                                ).then_inc(got[s], 16)
                        with pool.Fori(0, NG // 2) as i:
                            for s in range(2):
                                gathers(i, s)

                    @block.scalar
                    def _(act):
                        act.wait_ge(runs_ready, 1)
                        act.activation(idx_slot[:], run_i[:, 0:2 * GN].rearrange("p (s g) -> p s g", s=2),
                                       ACT.Copy).then_inc(idx_ready, 2)
                        with act.Fori(1, NG // 2) as i:
                            for s in range(2):
                                act.wait_ge(counted, (i - 1) * 2 + s + 1)
                                act.sem_inc(act_gate, 1)
                                act.activation(idx_slot[:, s, :], run_i[:, bass.ds((i * 2 + s) * GN, GN)],
                                               ACT.Copy).then_inc(idx_ready, 1)
                        with act.Fori(0, NG) as i:
                            act.wait_ge(rows_ready, i + 4)
                            act.sem_inc(act_gate, 1)
                            act.activation(run_rows[:, bass.ds(i * GN, GN), :], row_ps[:], ACT.Copy).then_inc(rows_copied, 1)

                    @block.tensor
                    def _(pe):
                        pe.wait_ge(iotas, 2)
                        for k in range(3):
                            pe.wait_ge(wide_ready, k + 1)
                            nc.tensor.transpose(row_ps[:, 0, :], wide[:, 0, :], ident[:]).then_inc(rows_ready, 1)
                        with pe.Fori(0, NG) as i:
                            pe.wait_ge(wide_ready, i + 4)
                            for j in range(GN):
                                ins = nc.tensor.transpose(row_ps[:, j, :], wide[:, j, :], ident[:])
                            ins.then_inc(rows_ready, 1)

                    @block.vector
                    def _(dve):
                        line = Line(dve, dve_steps)
                        for tile, value in ((dst_i, FAR), (src_i, 0), (type_i, 0), (prev_i, -1), (next_i, -2)):
                            nc.vector.memset(tile[:], value).then_inc(cleared, 1)
                        nc.vector.memset(x[:], 0.0).then_inc(cleared, 1)
                        nc.vector.memset(ends[:, 0:1], float(E))
                        line.link(nc.vector.memset(ends[:, 1:2], float(P - 1)))
                        dve.wait_ge(loaded, 17 * 16)
                        nc.vector.tensor_copy(dst_f[:], dst_i[:]).then_inc(dst_ready, 1)
                        nc.vector.tensor_copy(src_f[:], src_i[:])
                        nc.vector.tensor_copy(type_f[:], type_i[:])
                        nc.vector.tensor_copy(next_f[:], next_i[:])
                        line.link(nc.vector.tensor_copy(prev_f[:], prev_i[:]))
                        nc.vector.tensor_tensor(cont[:], dst_f[:], prev_f[:], ALU.is_equal)
                        nc.vector.tensor_scalar(in_first[:], dst_f[:], prev_f[:, 0:1], None, ALU.is_equal)
                        nc.vector.tensor_scalar(in_last[:], dst_f[:], next_f[:, 0:1], None, ALU.is_equal)
                        line.link(nc.vector.scalar_tensor_tensor(out=tmp[:], in0=src_f[:], scalar=float(R), in1=type_f[:],
                                                                 op0=ALU.mult, op1=ALU.add))
                        line.link(nc.vector.tensor_copy(kv_i[:], tmp[:]))
                        line.link(nc.vector.tensor_scalar(tmp[:], dst_f[:], float(N - 1), float(R), ALU.min, ALU.mult))
                        line.link(nc.vector.tensor_tensor(tmp[:], tmp[:], type_f[:], ALU.add))
                        line.link(nc.vector.tensor_copy(q_i[:], tmp[:]))
                        line.link(nc.vector.tensor_scalar(tmp[:, 0:1], dst_f[:, 0:1], float(N - 1), None, ALU.min))
                        line.link(nc.vector.tensor_copy(dst0_i[:], tmp[:, 0:1]))

                        def spread(column):
                            nc.vector.tensor_copy(wide[:, 0, :], column.to_broadcast([P, P])).then_inc(wide_ready, 1)

                        spread(dst_f[:, 0:1])
                        dve.wait_ge(rows_ready, 1)
                        line.link(nc.vector.tensor_copy(first_row[:], row_ps[:, 0, :]))
                        line.link(nc.vector.tensor_tensor(tmp[:, 0:1], prev_f[:, 0:1], dst_f[:, C - 1:C], ALU.is_equal))
                        spread(tmp[:, 0:1])
                        dve.wait_ge(rows_ready, 2)
                        line.link(nc.vector.tensor_copy(single_row[:], row_ps[:, 0, :]))
                        line.link(nc.vector.tensor_tensor(tmp[:, 0:1], dst_f[:, 0:1], next_f[:, 0:1], ALU.is_equal))
                        spread(tmp[:, 0:1])
                        dve.wait_ge(rows_ready, 3)
                        line.link(nc.vector.tensor_copy(link_row[:], row_ps[:, 0, :]))

                        dve.wait_ge(iotas, 4)
                        base, per = line.n, 3
                        with dve.Fori(0, NG) as i:
                            line.n = i * per + base
                            line.link(nc.vector.tensor_copy(ids_slot[:], ids[:, bass.ds(i * GN, GN)]))
                            line.link(nc.vector.tensor_tensor(
                                below[:], first_row[:].unsqueeze(1).to_broadcast([P, GN, P]),
                                ids_slot[:].unsqueeze(2).to_broadcast([P, GN, P]), ALU.is_lt))
                            line.link(nc.vector.tensor_reduce(cnt_slot[:], below[:], AX.X, ALU.add))
                            nc.vector.tensor_copy(runs[:, bass.ds(i * GN, GN)], cnt_slot[:])
                        line.n = base + NG * per
                        line.link(nc.vector.memset(tmp[:, 0:1], 0.0))
                        line.link(nc.vector.tensor_scalar(runs[:], runs[:], -1.0, 0.0, ALU.add, ALU.max))
                        nc.vector.tensor_copy(run_i[:], runs[:]).then_inc(runs_ready, 1)

                        base, per = line.n, 2
                        with dve.Fori(0, NG // 2) as i:
                            line.n = i * (2 * per) + base
                            for s in range(2):
                                line.link(nc.vector.tensor_copy(ids_slot[:], ids[:, bass.ds((i * 2 + s) * GN, GN)]))
                                dve.wait_ge(got[s], i * (16 * GN) + (g0[s] + 16 * GN))
                                for j in range(GN):
                                    ins = nc.vector.tensor_scalar(dst_rows[:, s, j, :], dst_rows[:, s, j, :],
                                                                  ids_slot[:, j:j + 1], 0.0, ALU.is_lt, ALU.add,
                                                                  accum_out=cnt_slot[:, j:j + 1])
                                line.link(ins)
                                nc.vector.tensor_copy(cnt[:, bass.ds((i * 2 + s) * GN, GN)], cnt_slot[:]).then_inc(counted, 1)
                        line.n = base + NG * per
                        dve.wait_ge(counted, NG)
                        nc.vector.scalar_tensor_tensor(out=start[:], in0=runs[:], scalar=float(C), in1=cnt[:],
                                                       op0=ALU.mult, op1=ALU.add).then_inc(starts_ready, 1)
                        dve.wait_ge(nodes_back, 32)
                        line.link(nc.vector.tensor_tensor(deg[:], after[:], start[:], ALU.subtract))
                        line.link(nc.vector.tensor_scalar(has[:], deg[:], 0.0, None, ALU.is_gt))
                        line.link(nc.vector.tensor_scalar(low_without[:], has[:], -1.0, -LOW, ALU.add, ALU.mult))
                        line.link(nc.vector.tensor_scalar(deg[:], deg[:], 1.0, None, ALU.max))
                        line.link(nc.vector.reciprocal(rdeg[:], deg[:]))
                        line.link(nc.vector.tensor_scalar(t0[:], after[:], -1.0, 0.0, ALU.add, ALU.max))
                        line.link(nc.vector.tensor_copy(end_i[:], t0[:]))
                        line.link(nc.vector.tensor_scalar(t0[:], start[:], float(-FAR), None, ALU.add))
                        line.link(nc.vector.tensor_tensor(t0[:], t0[:], has[:], ALU.mult))
                        line.link(nc.vector.tensor_scalar(t0[:], t0[:], float(FAR), None, ALU.add))
                        line.link(nc.vector.tensor_copy(start_i[:], t0[:]))
                        line.link(nc.vector.tensor_scalar(t0[:], run_after[:], float(C), None, ALU.mult))
                        line.link(nc.vector.tensor_tensor(t0[:], start[:], t0[:], ALU.is_lt))
                        line.link(nc.vector.tensor_scalar(low_unreached[:], t0[:], -1.0, -LOW, ALU.add, ALU.mult))
                        line.link(nc.vector.tensor_scalar(t1[:], run_after[:], 1.0, None, ALU.add))
                        line.link(nc.vector.tensor_tensor(t1[:], t1[:], t0[:], ALU.mult))
                        line.link(nc.vector.tensor_scalar(run_sel[:], t1[:], -1.0, None, ALU.add))
                        nc.vector.tensor_copy(wide[:], run_sel[:, 0:GN].unsqueeze(2)
                                              .to_broadcast([P, GN, P])).then_inc(wide_ready, 1)
                        with dve.Fori(1, NG) as i:
                            dve.wait_ge(rows_copied, i)
                            nc.vector.tensor_copy(wide[:], run_sel[:, bass.ds(i * GN, GN)].unsqueeze(2)
                                                  .to_broadcast([P, GN, P])).then_inc(wide_ready, 1)

        def norm_relu(name, table):
            st = Stage(name)
            with st:
                stats = sb("stats", [P, T, 6], F32, st)
                half = sb("half", [P, T], F32, st)
                stats_done = sem("stats_done", st)
                rstd = sb("rstd", [P, T], F32, st)
                shift = sb("shift", [P, T], F32, st)
                eps = sb("eps", [P, 1], F32, st)
                dve_steps, var_ready, std_ready = sem("dve_steps", st), sem("var_ready", st), sem("std_ready", st)
                coef_ready, h_ready, saved = sem("coef_ready", st), sem("h_ready", st), sem("saved", st)
                with nc.Block() as block:
                    @block.vector
                    def _(dve):
                        line = Line(dve, dve_steps)
                        line.link(nc.vector.memset(eps[:], LN_EPS))
                        with dve.Fori(0, T // 2) as i:
                            for s in range(2):
                                t = bass.ds(i * 2 + s, 1)
                                nc.vector.bn_stats(stats[:, t, :].rearrange("p a f -> p (a f)"),
                                                   x[:, t, :].rearrange("p a f -> p (a f)")).then_inc(stats_done, 1)
                        dve.wait_ge(stats_done, T)
                        line.link(nc.vector.tensor_tensor(shift[:], stats[:, :, 1], stats[:, :, 4], ALU.add))
                        line.link(nc.vector.tensor_tensor(rstd[:], stats[:, :, 1], stats[:, :, 4], ALU.subtract))
                        line.link(nc.vector.scalar_tensor_tensor(out=rstd[:], in0=rstd[:], scalar=0.25, in1=rstd[:],
                                                                 op0=ALU.mult, op1=ALU.mult))
                        line.link(nc.vector.tensor_tensor(half[:], stats[:, :, 2], stats[:, :, 5], ALU.add))
                        nc.vector.scalar_tensor_tensor(out=rstd[:], in0=half[:], scalar=1.0 / D, in1=rstd[:],
                                                       op0=ALU.mult, op1=ALU.add).then_inc(var_ready, 1)
                        dve.wait_ge(std_ready, 1)
                        line.link(nc.vector.reciprocal(rstd[:], rstd[:]))
                        nc.vector.scalar_tensor_tensor(out=shift[:], in0=shift[:], scalar=-0.5, in1=rstd[:],
                                                       op0=ALU.mult, op1=ALU.mult).then_inc(coef_ready, 1)

                    @block.scalar
                    def _(act):
                        act.wait_ge(var_ready, 1)
                        act.activation(rstd[:], rstd[:], ACT.Sqrt, bias=eps[:, 0:1]).then_inc(std_ready, 1)
                        act.wait_ge(coef_ready, 1)
                        with act.Fori(0, T // 2) as i:
                            for s in range(2):
                                t = bass.ds(i * 2 + s, 1)
                                act.activation(h[:, t, :].rearrange("p a f -> p (a f)"), x[:, t, :].rearrange("p a f -> p (a f)"),
                                               ACT.Relu, bias=shift[:, t], scale=rstd[:, t]).then_inc(h_ready, 1)

                    @block.sync
                    def _(sp):
                        if table is not None:
                            sp.wait_ge(h_ready, T)
                            sp.dma_start(table.rearrange("(p t) f -> p t f", t=T), h[:]).then_inc(saved, 16)
                            sp.wait_ge(saved, 16)

        def gather_sum(name, table, sums_d, with_max):
            W = 2 * D if with_max else D
            ops = 2 if with_max else 1
            st = Stage(name)
            with st:
                idx_slot = sb("idx_slot", [P, NS, G], I32, st)
                rows = sb("rows", [P, NS, G, D], F32, st)
                sums = sb("sums", [P, NS, G, W], F32, st)
                idx_ready, summed, cleared = sem("idx_ready", st), sem("summed", st), sem("cleared", st)
                got, g0 = gathered, gathered_before(NS, C // NS)
                stored = [sem(f"stored{s}", st) for s in range(NS)]
                with nc.Block() as block:
                    @block.gpsimd
                    def _(pool):
                        def turn(i, first):
                            for s in range(NS):
                                pool.wait_ge(idx_ready, i * NS + s + 1)
                                if not first:
                                    pool.wait_ge(summed, (i * NS + s + 1 - NS) * (G * ops))
                                pool.sem_inc(pool_gate, 1)
                                for j in range(G):
                                    nc.gpsimd.indirect_dma_start(
                                        out=rows[:, s, j, :], out_offset=None, in_=table,
                                        in_offset=bass.IndirectOffsetOnAxis(ap=idx_slot[:, s, j:j + 1], axis=0)
                                    ).then_inc(got[s], 16)
                        turn(0, True)
                        with pool.Fori(1, TURNS) as i:
                            turn(i, False)

                    @block.scalar
                    def _(act):
                        act.activation(idx_slot[:], src_i[:, 0:NS * G].rearrange("p (s g) -> p s g", s=NS),
                                       ACT.Copy).then_inc(idx_ready, NS)
                        with act.Fori(1, TURNS) as i:
                            for s in range(NS):
                                act.wait_ge(got[s], i * (16 * G) + g0[s])
                                act.sem_inc(act_gate, 1)
                                act.activation(idx_slot[:, s, :], src_i[:, bass.ds((i * NS + s) * G, G)],
                                               ACT.Copy).then_inc(idx_ready, 1)

                    @block.vector
                    def _(dve):
                        nc.vector.memset(sums[:, NS - 1, G - 1, :], 0.0).then_inc(cleared, 1)
                        dve.wait_ge(cleared, 1)

                        def turn(i, first):
                            for s in range(NS):
                                dve.wait_ge(got[s], i * (16 * G) + (g0[s] + 16 * G))
                                if not first:
                                    dve.wait_ge(stored[s], i * 16)
                                for j in range(G):
                                    ps, pj = (s, j - 1) if j else ((s - 1) % NS, G - 1)
                                    for m in range(ops):
                                        k = (s * G + j) * ops + m
                                        if not (first and k < ops):
                                            dve.wait_ge(summed, i * (NS * G * ops) + (k - ops + 1))
                                        nc.vector.scalar_tensor_tensor(
                                            out=sums[:, s, j, m * D:m * D + D], in0=sums[:, ps, pj, m * D:m * D + D],
                                            scalar=cont[:, bass.ds((i * NS + s) * G + j, 1)], in1=rows[:, s, j, :],
                                            op0=ALU.mult, op1=(ALU.add, ALU.max)[m]).then_inc(summed, 1)
                        turn(0, True)
                        with dve.Fori(1, TURNS) as i:
                            turn(i, False)
                        dve.wait_ge(summed, C * ops)
                        nc.vector.tensor_copy(carry[:, 0:W], sums[:, NS - 1, G - 1, :])

                    @block.sync
                    def _(sp):
                        view = sums_d.rearrange("(p c) f -> p c f", c=C)
                        with sp.Fori(0, TURNS) as i:
                            for s in range(NS):
                                c0 = sp.snap((i * NS + s) * G)
                                sp.wait_ge(summed, (i * NS + s + 1) * (G * ops))
                                sp.sem_inc(sp_gate, 1)
                                sp.dma_start(view[:, bass.ds(c0, G), :], sums[:, s, :, :]).then_inc(stored[s], 16)
                        for s in range(NS):
                            sp.wait_ge(stored[s], 16 * TURNS)

        def chain_runs(name, parts):
            st = Stage(name)
            with st:
                turned = sb("turned", [P, P + 1], F32, st)
                last_t = pb("last_t", [P, P], st)
                back_t = pb("back_t", [P, P], st)
                dve_steps, turned_ready, pe_done = sem("dve_steps", st), sem("turned_ready", st), sem("pe_done", st)
                with nc.Block() as block:
                    @block.tensor
                    def _(pe):
                        for n, (a, w, _m) in enumerate(parts):
                            if n:
                                pe.wait_ge(turned_ready, 2 * n)
                            nc.tensor.transpose(last_t[0:w, :], carry[:, a:a + w], ident[:]).then_inc(pe_done, 1)
                            pe.wait_ge(turned_ready, 2 * n + 1)
                            nc.tensor.transpose(back_t[:, 0:w], turned[0:w, 0:P], ident[0:w, 0:w]).then_inc(pe_done, 1)

                    @block.vector
                    def _(dve):
                        for n, (a, w, is_max) in enumerate(parts):
                            if not n:
                                nc.vector.memset(turned[:, 0:1], 0.0).then_inc(dve_steps, 1)
                                dve.wait_ge(dve_steps, 1)
                            dve.wait_ge(pe_done, 2 * n + 1)
                            nc.vector.tensor_tensor_scan(turned[0:w, 1:P + 1], single_row[0:w, :], last_t[0:w, :], 0.0,
                                                         ALU.mult, ALU.max if is_max else ALU.add).then_inc(turned_ready, 1)
                            dve.wait_ge(pe_done, 2 * n + 2)
                            nc.vector.tensor_copy(carry[:, a:a + w], back_t[:, 0:w]).then_inc(turned_ready, 1)

        def node_totals(name, sums_d, W, WC, pre, per, scratch, consts, body, act_body=None, pe_body=None, pe_start=None):
            st = Stage(name)
            with st:
                idx_slot = sb("idx_slot", [P, 2, GN], I32, st)
                totals = sb("totals", [P, 2, GN, W], F32, st)
                pick = sb("pick", [P, GN, P], F32, st)
                reach = pb("reach", [P, GN, 2 * D], st)
                idx_ready, picked, reached = sem("idx_ready", st), sem("picked", st), sem("reached", st)
                got, g0 = gathered, gathered_before(2, GN * NG // 2)
                dve_steps = sem("dve_steps", st)
                extra = scratch(st)
                with nc.Block() as block:
                    @block.gpsimd
                    def _(pool):
                        with pool.Fori(0, NG // 2) as i:
                            for s in range(2):
                                pool.wait_ge(idx_ready, i * 2 + s + 1)
                                pool.sem_inc(pool_gate, 1)
                                for j in range(GN):
                                    nc.gpsimd.indirect_dma_start(
                                        out=totals[:, s, j, :], out_offset=None, in_=sums_d,
                                        in_offset=bass.IndirectOffsetOnAxis(ap=idx_slot[:, s, j:j + 1], axis=0)
                                    ).then_inc(got[s], 16)

                    @block.sync
                    def _(sp):
                        consts(sp, extra)

                    @block.scalar
                    def _(act):
                        act.activation(idx_slot[:], end_i[:, 0:2 * GN].rearrange("p (s g) -> p s g", s=2),
                                       ACT.Copy).then_inc(idx_ready, 2)

                        def group(k, first):
                            if act_body:
                                act_body(act, k, first, extra)

                        for s in range(2):
                            group(s, s == 0)
                        with act.Fori(1, NG // 2) as i:
                            for s in range(2):
                                act.wait_ge(dve_steps, i * (2 * per) + (pre + (s - 1) * per))
                                act.sem_inc(act_gate, 1)
                                act.activation(idx_slot[:, s, :], end_i[:, bass.ds((i * 2 + s) * GN, GN)],
                                               ACT.Copy).then_inc(idx_ready, 1)
                                group(i * 2 + s, False)

                    @block.tensor
                    def _(pe):
                        if pe_start:
                            pe_start(pe, extra)
                        with pe.Fori(0, NG) as i:
                            pe.wait_ge(picked, i + 1)
                            for j in range(GN):
                                ins = nc.tensor.matmul(reach[:, j, 0:WC], pick[:, j, :], carry[:, 0:WC], start=True, stop=True)
                            ins.then_inc(reached, 1)
                            if pe_body:
                                pe_body(pe, i, extra)

                    @block.vector
                    def _(dve):
                        line = Line(dve, dve_steps)
                        if "prepare" in extra:
                            extra["prepare"](dve, line)
                        assert line.n == pre
                        with dve.Fori(0, NG // 2) as i:
                            for s in range(2):
                                k = i * 2 + s
                                line.n = i * (2 * per) + (pre + s * per)
                                nc.vector.tensor_scalar(pick[:], run_rows[:, bass.ds(k * GN, GN), :], lane[:, 0:1], None,
                                                        ALU.is_equal).then_inc(picked, 1)
                                dve.wait_ge(got[s], i * (16 * GN) + (g0[s] + 16 * GN))
                                dve.wait_ge(reached, k + 1)
                                body(dve, line, k, totals[:, s, :, :], reach, extra)

        def linear_scratch(st, e, sources):
            e["sources"] = sources
            e["left"] = sb("left", [P, sources, GN, D], F32, st)
            e["left_t"] = sb("left_t", [P, sources, GN, D], F32, st)
            e["w"] = sb("w", [P, sources, D], F32, st)
            e["turn_ps"] = pb("turn_ps", [P, sources * GN, D], st)
            e["lin_ps"] = pb("lin_ps", [P, GN, D], st)
            for k in ("left_ready", "h_copied", "turned", "evacuated", "multiplied", "loaded"):
                e[k] = sem(k, st)

        def linear_act(act, k, first, e):
            if e["sources"] == 2:
                if not first:
                    act.wait_ge(e["turned"], k)
                    act.sem_inc(act_gate, 1)
                act.activation(e["left"][:, 1, :, :], h[:, bass.ds(k * GN, GN), :], ACT.Copy).then_inc(e["h_copied"], 1)
            act.wait_ge(e["turned"], k + 1)
            act.activation(e["left_t"][:].rearrange("p a g f -> p (a g) f"), e["turn_ps"][:], ACT.Copy).then_inc(e["evacuated"], 1)

        def linear_pe(pe, i, e):
            pe.wait_ge(e["left_ready"], i + 1)
            if e["sources"] == 2:
                pe.wait_ge(e["h_copied"], i + 1)
            for a in range(e["sources"]):
                for j in range(GN):
                    ins = nc.tensor.transpose(e["turn_ps"][:, a * GN + j, :], e["left"][:, a, j, :], ident[:])
            ins.then_inc(e["turned"], 1)
            pe.wait_ge(e["evacuated"], i + 1)
            for j in range(GN):
                for a in range(e["sources"]):
                    ins = nc.tensor.matmul(e["lin_ps"][:, j, :], e["left_t"][:, a, j, :], e["w"][:, a, :],
                                           start=a == 0, stop=a == e["sources"] - 1)
            ins.then_inc(e["multiplied"], 1)

        def layer0_nodes():
            def scratch(st):
                e = {k: sb(k, [P, T], F32, st) for k in ("sum_w", "max_w")}
                e["z"] = sb("z", [P, 3], F32, st)
                e["a"] = sb("part_a", [P, GN, D], F32, st)
                e["b"] = sb("part_b", [P, GN, D], F32, st)
                e["loaded"] = sem("loaded", st)

                def prepare(dve, line):
                    z = e["z"]
                    dve.wait_ge(e["loaded"], 16)
                    line.link(nc.vector.tensor_scalar(e["sum_w"][:], rdeg[:], z[:, 1:2], z[:, 0:1], ALU.mult, ALU.add))
                    line.link(nc.vector.tensor_tensor(e["sum_w"][:], e["sum_w"][:], has[:], ALU.mult))
                    line.link(nc.vector.tensor_scalar(e["max_w"][:], has[:], z[:, 2:3], None, ALU.mult))
                e["prepare"] = prepare
                return e

            def consts(sp, e):
                sp.dma_start(e["z"][:], z_in.to_broadcast([P, 3])).then_inc(e["loaded"], 16)
                sp.wait_ge(e["loaded"], 16)

            def body(dve, line, k, total, reach, e):
                tiles = bass.ds(k * GN, GN)
                a, b = e["a"], e["b"]
                line.link(nc.vector.tensor_tensor(a[:], total[:, :, 0:D], reach[:, :, 0:D], ALU.add))
                line.link(nc.vector.tensor_tensor(b[:], total[:, :, D:2 * D], reach[:, :, D:2 * D], ALU.max))
                line.link(nc.vector.tensor_tensor(a[:], a[:], e["sum_w"][:, tiles].unsqueeze(2).to_broadcast([P, GN, D]), ALU.mult))
                line.link(nc.vector.tensor_tensor(b[:], b[:], e["max_w"][:, tiles].unsqueeze(2).to_broadcast([P, GN, D]), ALU.mult))
                line.link(nc.vector.tensor_tensor(a[:], a[:], b[:], ALU.add))
                line.link(nc.vector.tensor_tensor(x[:, tiles, :], x[:, tiles, :], a[:], ALU.add))

            node_totals("nodes0", s0_d, 2 * D, 2 * D, 3, 6, scratch, consts, body)

        def layer1_nodes():
            def scratch(st):
                e = {}
                linear_scratch(st, e, 2)
                e["bias"] = sb("bias", [P, D], F32, st)
                e["mean_w"] = sb("mean_w", [P, T], F32, st)

                def prepare(dve, line):
                    line.link(nc.vector.tensor_tensor(e["mean_w"][:], rdeg[:], has[:], ALU.mult))
                    dve.wait_ge(e["loaded"], 48)
                e["prepare"] = prepare
                return e

            def consts(sp, e):
                sp.dma_start(e["w"][:, 0, :], w1_in[D:2 * D, :]).then_inc(e["loaded"], 16)
                sp.dma_start(e["w"][:, 1, :], w1_in[0:D, :]).then_inc(e["loaded"], 16)
                sp.dma_start(e["bias"][:], b1_in.rearrange("(a f) -> a f", a=1).to_broadcast([P, D])).then_inc(e["loaded"], 16)
                sp.wait_ge(e["loaded"], 48)

            def body(dve, line, k, total, reach, e):
                tiles = bass.ds(k * GN, GN)
                m = e["left"][:, 0, :, :]
                line.link(nc.vector.tensor_tensor(m, total[:, :, 0:D], reach[:, :, 0:D], ALU.add))
                nc.vector.tensor_tensor(m, m, e["mean_w"][:, tiles].unsqueeze(2).to_broadcast([P, GN, D]),
                                        ALU.mult).then_inc(e["left_ready"], 1)
                dve.wait_ge(e["multiplied"], k + 1)
                line.link(nc.vector.tensor_tensor(m, e["lin_ps"][:], e["bias"][:].unsqueeze(1).to_broadcast([P, GN, D]), ALU.add))
                line.link(nc.vector.tensor_tensor(x[:, tiles, :], x[:, tiles, :], m, ALU.add))

            def pe_body(pe, i, e):
                linear_pe(pe, i, e)

            node_totals("nodes1", s1_d, D, D, 1, 3, scratch, consts, body, linear_act, pe_body)

        def relation_tables():
            BANK = 512
            KV = R * 2 * D
            st = Stage("tables2")
            with st:
                w = sb("w", [P, KV + R * D], F32, st)
                left = sb("left", [P, 2, D], F32, st)
                left_t = sb("left_t", [P, 2, D], F32, st)
                kv_slot = sb("kv_slot", [P, 2, KV], F32, st)
                q_slot = sb("q_slot", [P, 2, R, D + K2], F32, st)
                bias = sb("bias", [P, R, K2], F32, st)
                turn_ps = pb("turn_ps", [P, BANK], st)
                out_ps = pb("out_ps", [P, 4, BANK], st)
                loaded, copied, turned, evacuated = sem("loaded", st), sem("copied", st), sem("turned", st), sem("evacuated", st)
                multiplied, dve_out, act_out = sem("multiplied", st), sem("dve_out", st), sem("act_out", st)
                bias_in_place = sem("bias_in_place", st)
                saved = [sem(f"saved{s}", st) for s in range(2)]
                with nc.Block() as block:
                    @block.sync
                    def _(sp):
                        for r in range(R):
                            for a, src in ((r * 2 * D, wk_in), (r * 2 * D + D, wv_in), (KV + r * D, wq_in)):
                                sp.dma_start(w[:, a:a + D].rearrange("h (k d) -> h k d", k=K2),
                                             src[r].rearrange("k h d -> h k d")).then_inc(loaded, 16)
                        sp.dma_start(bias[:].rearrange("p r k -> p (r k)"),
                                     bias_in.rearrange("(a r) k -> a (r k)", a=1).to_broadcast([P, R * K2])).then_inc(loaded, 16)
                        kv_v = kv_d.rearrange("(p t r) w -> p t (r w)", t=T, r=R)
                        q_v = q_d.rearrange("(p t r) w -> p t (r w)", t=T, r=R)
                        with sp.Fori(0, T // 2) as i:
                            for s in range(2):
                                t = sp.snap(i * 2 + s)
                                sp.wait_ge(dve_out, i * 2 + s + 1)
                                sp.sem_inc(sp_gate, 1)
                                sp.wait_ge(act_out, i * 2 + s + 1)
                                sp.sem_inc(sp_gate, 1)
                                sp.dma_start(kv_v[:, bass.ds(t, 1), :], kv_slot[:, s:s + 1, :]).then_inc(saved[s], 16)
                                sp.dma_start(q_v[:, bass.ds(t, 1), :],
                                             q_slot[:, s:s + 1, :, :].rearrange("p a r w -> p a (r w)")).then_inc(saved[s], 16)
                        for s in range(2):
                            sp.wait_ge(saved[s], 32 * (T // 2))

                    @block.scalar
                    def _(act):
                        def tile(i, s, first):
                            k = i * 2 + s
                            if not (first and s < 1):
                                act.wait_ge(turned, k)
                                act.sem_inc(act_gate, 1)
                            act.activation(left[:, s:s + 1, :], h[:, bass.ds(k, 1), :], ACT.Copy).then_inc(copied, 1)
                            act.wait_ge(turned, k + 1)
                            act.activation(left_t[:, s, :], turn_ps[:, 0:D], ACT.Copy).then_inc(evacuated, 1)
                            if not first:
                                act.wait_ge(saved[s], i * 32)
                            act.wait_ge(multiplied, k * 4 + 3)
                            act.activation(kv_slot[:, s, 2 * BANK:KV], out_ps[:, 2, 0:256], ACT.Copy)
                            act.activation(q_slot[:, s, 0:2, 0:D], out_ps[:, 2, 256:512].rearrange("p (r f) -> p r f", r=2), ACT.Copy)
                            act.wait_ge(multiplied, k * 4 + 4)
                            act.activation(q_slot[:, s, 2:5, 0:D], out_ps[:, 3, 0:384].rearrange("p (r f) -> p r f", r=3),
                                           ACT.Copy).then_inc(act_out, 1)
                        for s in range(2):
                            tile(0, s, True)
                        with act.Fori(1, T // 2) as i:
                            for s in range(2):
                                tile(i, s, False)

                    @block.tensor
                    def _(pe):
                        pe.wait_ge(loaded, 16 * (3 * R + 1))

                        def tile(i, s, first):
                            k = i * 2 + s
                            pe.wait_ge(copied, k + 1)
                            nc.tensor.transpose(turn_ps[:, 0:D], left[:, s, :], ident[:]).then_inc(turned, 1)
                            pe.wait_ge(evacuated, k + 1)
                            for b in range(4):
                                if b == 0 and not first:
                                    pe.wait_ge(dve_out, k)
                                if b == 2 and not first:
                                    pe.wait_ge(act_out, k)
                                cols = min(BANK, KV + R * D - b * BANK)
                                nc.tensor.matmul(out_ps[:, b, 0:cols], left_t[:, s, :], w[:, b * BANK:b * BANK + cols],
                                                 start=True, stop=True).then_inc(multiplied, 1)
                        tile(0, 0, True)
                        tile(0, 1, False)
                        with pe.Fori(1, T // 2) as i:
                            for s in range(2):
                                tile(i, s, False)

                    @block.vector
                    def _(dve):
                        dve.wait_ge(loaded, 16 * (3 * R + 1))
                        for s in range(2):
                            nc.vector.tensor_copy(q_slot[:, s, :, D:D + K2], bias[:]).then_inc(bias_in_place, 1)
                        dve.wait_ge(bias_in_place, 2)

                        def tile(i, s, first):
                            k = i * 2 + s
                            if not first:
                                dve.wait_ge(saved[s], i * 32)
                            dve.wait_ge(multiplied, k * 4 + 2)
                            nc.vector.tensor_copy(kv_slot[:, s, 0:2 * BANK], out_ps[:, 0:2, :].rearrange("p b f -> p (b f)")).then_inc(dve_out, 1)
                        for s in range(2):
                            tile(0, s, True)
                        with dve.Fori(1, T // 2) as i:
                            for s in range(2):
                                tile(i, s, False)

        def relation_logits(logits):
            st = Stage("logits2")
            with st:
                kv_idx = sb("kv_idx", [P, NS, G], I32, st)
                q_idx = sb("q_idx", [P, NS, G], I32, st)
                kv_rows = sb("kv_rows", [P, NS, G, 2 * D], F32, st)
                q_rows = sb("q_rows", [P, NS, G, D + K2], F32, st)
                prod = sb("prod", [P, 2, G, D], F32, st)
                dots = sb("dots", [P, 2, G, K2], F32, st)
                idx_ready, multiplied, reduced, scored = (sem("idx_ready", st), sem("multiplied", st), sem("reduced", st),
                                                          sem("scored", st))
                got, g0 = gathered, gathered_before(NS, 2 * C // NS)
                stored = [sem(f"stored{s}", st) for s in range(NS)]
                with nc.Block() as block:
                    @block.gpsimd
                    def _(pool):
                        def turn(i, first):
                            for s in range(NS):
                                pool.wait_ge(idx_ready, i * NS + s + 1)
                                if not first:
                                    pool.wait_ge(scored, i * NS + s + 1 - NS)
                                    pool.sem_inc(pool_gate, 1)
                                    pool.wait_ge(stored[s], i * 16)
                                pool.sem_inc(pool_gate, 1)
                                for j in range(G):
                                    nc.gpsimd.indirect_dma_start(
                                        out=kv_rows[:, s, j, :], out_offset=None, in_=kv_d,
                                        in_offset=bass.IndirectOffsetOnAxis(ap=kv_idx[:, s, j:j + 1], axis=0)).then_inc(got[s], 16)
                                    nc.gpsimd.indirect_dma_start(
                                        out=q_rows[:, s, j, :], out_offset=None, in_=q_d,
                                        in_offset=bass.IndirectOffsetOnAxis(ap=q_idx[:, s, j:j + 1], axis=0)).then_inc(got[s], 16)
                        turn(0, True)
                        with pool.Fori(1, TURNS) as i:
                            turn(i, False)

                    @block.scalar
                    def _(act):
                        act.activation(kv_idx[:], kv_i[:, 0:NS * G].rearrange("p (s g) -> p s g", s=NS), ACT.Copy)
                        act.activation(q_idx[:], q_i[:, 0:NS * G].rearrange("p (s g) -> p s g", s=NS), ACT.Copy).then_inc(idx_ready, NS)
                        with act.Fori(1, TURNS) as i:
                            for s in range(NS):
                                act.wait_ge(got[s], i * (32 * G) + g0[s])
                                act.sem_inc(act_gate, 1)
                                cols = bass.ds((i * NS + s) * G, G)
                                act.activation(kv_idx[:, s, :], kv_i[:, cols], ACT.Copy)
                                act.activation(q_idx[:, s, :], q_i[:, cols], ACT.Copy).then_inc(idx_ready, 1)

                    @block.vector
                    def _(dve):
                        with dve.Fori(0, TURNS) as i:
                            for s in range(NS):
                                k = i * NS + s
                                dve.wait_ge(got[s], i * (32 * G) + (g0[s] + 32 * G))
                                nc.vector.tensor_tensor(prod[:, s % 2, :, :], kv_rows[:, s, :, 0:D], q_rows[:, s, :, 0:D],
                                                        ALU.mult).then_inc(multiplied, 1)
                                dve.wait_ge(multiplied, k + 1)
                                nc.vector.tensor_reduce(dots[:, s % 2, :, :].rearrange("p j k -> p (j k)"),
                                                        prod[:, s % 2, :, :].rearrange("p j (k d) -> p (j k) d", k=K2),
                                                        AX.X, ALU.add).then_inc(reduced, 1)
                                dve.wait_ge(reduced, k + 1)
                                nc.vector.scalar_tensor_tensor(
                                    out=logits[:, :, bass.ds(k * G, G)].rearrange("p k j -> p j k"), in0=dots[:, s % 2, :, :],
                                    scalar=1.0 / float(D2) ** 0.5, in1=q_rows[:, s, :, D:D + K2], op0=ALU.mult,
                                    op1=ALU.add).then_inc(scored, 1)

                    @block.sync
                    def _(sp):
                        view = v_d.rearrange("(p c) f -> p c f", c=C)
                        with sp.Fori(0, TURNS) as i:
                            for s in range(NS):
                                c0 = sp.snap((i * NS + s) * G)
                                sp.wait_ge(got[s], i * (32 * G) + (g0[s] + 32 * G))
                                sp.sem_inc(sp_gate, 1)
                                sp.dma_start(view[:, bass.ds(c0, G), :], kv_rows[:, s, :, D:2 * D]).then_inc(stored[s], 16)
                        for s in range(NS):
                            sp.wait_ge(stored[s], 16 * TURNS)

        def spread_scratch(st, heads):
            e = {"heads": heads}
            e["stay"] = sb("stay", [P, C + 1], F32, st)
            e["pen_first"] = sb("pen_first", [P, C], F32, st)
            e["pen_last"] = sb("pen_last", [P, C], F32, st)
            e["pen_single"] = sb("pen_single", [P, P], F32, st)
            e["pen_link"] = sb("pen_link", [P, P], F32, st)
            e["ends"] = sb("ends", [P, 2, heads], F32, st)
            e["left"] = sb("left", [K2, P + 1], F32, st)
            e["right"] = sb("right", [K2, P + 1], F32, st)
            e["reach"] = sb("reach", [P, 2, heads], F32, st)
            e["ends_ps"] = pb("ends_ps", [P, 2, P], st)
            e["reach_ps"] = pb("reach_ps", [P, 2, K2], st)
            e["dve_turns"], e["pe_turns"] = sem("dve_turns", st), sem("pe_turns", st)
            return e

        def spread_prepare(line, e):
            for tile, mask in ((e["stay"][:, 0:C], cont), (e["pen_first"][:], in_first), (e["pen_last"][:], in_last),
                               (e["pen_single"][:], single_row), (e["pen_link"][:], link_row)):
                line.link(nc.vector.tensor_scalar(tile, mask[:], -1.0, -LOW, ALU.add, ALU.mult))
            line.link(nc.vector.memset(e["stay"][:, C:C + 1], LOW))
        PREPARES = 6

        def spread(dve, line, lanes, is_max, call, e):
            n, least = e["heads"], LOW if is_max else 0.0
            for k in range(n):
                ins = nc.vector.tensor_tensor_scan(lanes[:, k, :], e["stay"][:, 0:C] if is_max else cont[:], lanes[:, k, :], least,
                                                   ALU.add if is_max else ALU.mult, ALU.max if is_max else ALU.add)
                line.mark(ins)
            dve.wait_ge(line.sem, line.n)
            line.link(nc.vector.tensor_copy(e["ends"][:, 0, :], lanes[:, :, C - 1]))
            for k in range(n):
                ins = nc.vector.tensor_tensor_scan(lanes[:, k, ::-1], e["stay"][:, 1:C + 1][:, ::-1], lanes[:, k, ::-1], least,
                                                   ALU.add, ALU.max)
                line.mark(ins)
            dve.wait_ge(line.sem, line.n)
            nc.vector.tensor_copy(e["ends"][:, 1, :], lanes[:, :, 0]).then_inc(e["dve_turns"], 1)
            nc.vector.memset(e["left"][:, 0:1], least)
            line.link(nc.vector.memset(e["right"][:, P:P + 1], least))
            dve.wait_ge(e["pe_turns"], call * 2 + 1)
            op0, op1 = (ALU.add, ALU.max) if is_max else (ALU.mult, ALU.add)
            line.link(nc.vector.tensor_tensor_scan(e["left"][0:n, 1:P + 1], (e["pen_single"] if is_max else single_row)[0:n, :],
                                                   e["ends_ps"][0:n, 0, :], least, op0, op1))
            nc.vector.tensor_tensor_scan(e["right"][0:n, 0:P][:, ::-1], (e["pen_link"] if is_max else link_row)[0:n, ::-1],
                                         e["ends_ps"][0:n, 1, ::-1], least, op0, op1).then_inc(e["dve_turns"], 1)
            dve.wait_ge(e["pe_turns"], call * 2 + 2)
            line.link(nc.vector.tensor_copy(e["reach"][:], e["reach_ps"][:, :, 0:n]))
            for side, mask in ((0, e["pen_first"] if is_max else in_first), (1, e["pen_last"] if is_max else in_last)):
                for k in range(n):
                    line.mark(nc.vector.scalar_tensor_tensor(out=lanes[:, k, :], in0=mask[:], scalar=e["reach"][:, side, k:k + 1],
                                                             in1=lanes[:, k, :], op0=op0 if is_max else ALU.mult, op1=op1))
                dve.wait_ge(line.sem, line.n)

        def spread_pe(pe, call, e):
            n = e["heads"]
            pe.wait_ge(e["dve_turns"], call * 2 + 1)
            nc.tensor.transpose(e["ends_ps"][0:n, 0, :], e["ends"][:, 0, :], ident[:])
            nc.tensor.transpose(e["ends_ps"][0:n, 1, :], e["ends"][:, 1, :], ident[:]).then_inc(e["pe_turns"], 1)
            pe.wait_ge(e["dve_turns"], call * 2 + 2)
            pe.sem_inc(pe_gate, 1)
            nc.tensor.transpose(e["reach_ps"][:, 0, 0:n], e["left"][0:n, 0:P], ident[0:n, 0:n])
            nc.tensor.transpose(e["reach_ps"][:, 1, 0:n], e["right"][0:n, 1:P + 1], ident[0:n, 0:n]).then_inc(e["pe_turns"], 1)

        def spread_steps(heads):
            return 4 * heads + 4

        def relation_softmax(logits, weights):
            st = Stage("softmax2")
            with st:
                e = spread_scratch(st, K2)
                lanes = sb("lanes", [P, K2, C], F32, st)
                mask = sb("mask", [P, C], F32, st)
                number = sb("number", [P, R], F32, st)
                rel = sb("rel", [P, 1], F32, st)
                dve_steps, numbered, shifted, exped = sem("dve_steps", st), sem("numbered", st), sem("shifted", st), sem("exped", st)

                def all_heads(ap):
                    return ap.unsqueeze(1).to_broadcast([P, K2, C])

                with nc.Block() as block:
                    @block.gpsimd
                    def _(pool):
                        nc.gpsimd.iota(number[:], pattern=[[1, R]], base=0, channel_multiplier=0,
                                       allow_small_or_imprecise_dtypes=True).then_inc(numbered, 1)

                    @block.tensor
                    def _(pe):
                        with pe.Fori(0, 2 * R) as i:
                            spread_pe(pe, i, e)

                    @block.scalar
                    def _(act):
                        act.wait_ge(shifted, 1)
                        act.activation(logits[:], logits[:], ACT.Exp).then_inc(exped, 1)

                    @block.vector
                    def _(dve):
                        line = Line(dve, dve_steps)
                        spread_prepare(line, e)
                        line.link(nc.vector.memset(weights[:], NEG))
                        dve.wait_ge(numbered, 1)
                        base, per = line.n, spread_steps(K2) + 6
                        with dve.Fori(0, R) as r:
                            line.n = r * per + base
                            line.link(nc.vector.tensor_copy(rel[:], number[:, bass.ds(r, 1)]))
                            line.link(nc.vector.tensor_scalar(mask[:], type_f[:], rel[:, 0:1], 1.0e30, ALU.is_equal, ALU.mult))
                            line.link(nc.vector.tensor_scalar(mask[:], mask[:], NEG, None, ALU.add))
                            line.link(nc.vector.tensor_tensor(lanes[:], logits[:], all_heads(mask[:]), ALU.min))
                            spread(dve, line, lanes, True, r, e)
                            line.link(nc.vector.tensor_tensor(lanes[:], lanes[:], all_heads(mask[:]), ALU.min))
                            line.link(nc.vector.tensor_tensor(weights[:], weights[:], lanes[:], ALU.max))
                        line.n = base + R * per
                        nc.vector.tensor_tensor(logits[:], logits[:], weights[:], ALU.subtract).then_inc(shifted, 1)
                        dve.wait_ge(exped, 1)
                        line.link(nc.vector.memset(weights[:], 0.0))
                        base, per = line.n, spread_steps(K2) + 5
                        with dve.Fori(0, R) as r:
                            line.n = r * per + base
                            line.link(nc.vector.tensor_copy(rel[:], number[:, bass.ds(r, 1)]))
                            line.link(nc.vector.tensor_scalar(mask[:], type_f[:], rel[:, 0:1], None, ALU.is_equal))
                            line.link(nc.vector.tensor_tensor(lanes[:], logits[:], all_heads(mask[:]), ALU.mult))
                            spread(dve, line, lanes, False, r + R, e)
                            line.link(nc.vector.tensor_tensor(lanes[:], lanes[:], all_heads(mask[:]), ALU.mult))
                            line.link(nc.vector.tensor_tensor(weights[:], weights[:], lanes[:], ALU.add))
                        line.n = base + R * per
                        line.link(nc.vector.tensor_scalar(weights[:], weights[:], 1e-12, None, ALU.add))
                        line.link(nc.vector.reciprocal(weights[:], weights[:]))
                        line.link(nc.vector.tensor_tensor(weights[:], weights[:], logits[:], ALU.mult))

        def weighted_sum(name, rows_d, sums_d, weights, heads):
            st = Stage(name)
            with st:
                rows = sb("rows", [P, NS, G, D], F32, st)
                prod = sb("prod", [P, 2, G, D], F32, st)
                sums = sb("sums", [P, NS, G, D], F32, st)
                cleared, multiplied, summed = sem("cleared", st), sem("multiplied", st), sem("summed", st)
                got = [sem(f"got{s}", st) for s in range(NS)]
                stored = [sem(f"stored{s}", st) for s in range(NS)]
                with nc.Block() as block:
                    @block.sync
                    def _(sp):
                        view = rows_d.rearrange("(p c) f -> p c f", c=C)

                        def turn(i, first):
                            for s in range(NS):
                                c0 = (i * NS + s) * G if first else sp.snap((i * NS + s) * G)
                                if not first:
                                    sp.wait_ge(multiplied, i * NS + s + 1 - NS)
                                    sp.sem_inc(sp_gate, 1)
                                sp.dma_start(rows[:, s, :, :], view[:, bass.ds(c0, G), :]).then_inc(got[s], 16)
                        turn(0, True)
                        with sp.Fori(1, TURNS) as i:
                            turn(i, False)

                    @block.vector
                    def _(dve):
                        nc.vector.memset(sums[:, NS - 1, G - 1, :], 0.0).then_inc(cleared, 1)
                        dve.wait_ge(cleared, 1)

                        def turn(i, first):
                            for s in range(NS):
                                k = i * NS + s
                                cols = bass.ds(k * G, G)
                                w_jk = weights[:, :, cols].rearrange("p k j -> p j k")
                                dve.wait_ge(got[s], i * 16 + 16)
                                nc.vector.tensor_tensor(
                                    prod[:, s % 2, :, :].rearrange("p j (k d) -> p j k d", k=heads),
                                    rows[:, s, :, :].rearrange("p j (k d) -> p j k d", k=heads),
                                    over_heads(w_jk, heads, D // heads), ALU.mult).then_inc(multiplied, 1)
                                if not first:
                                    dve.wait_ge(stored[s], i * 16)
                                dve.wait_ge(multiplied, k + 1)
                                for j in range(G):
                                    ps, pj = (s, j - 1) if j else ((s - 1) % NS, G - 1)
                                    if not (first and s == 0 and j == 0):
                                        dve.wait_ge(summed, i * (NS * G) + (s * G + j))
                                    nc.vector.scalar_tensor_tensor(
                                        out=sums[:, s, j, :], in0=sums[:, ps, pj, :],
                                        scalar=cont[:, bass.ds((i * NS + s) * G + j, 1)], in1=prod[:, s % 2, j, :],
                                        op0=ALU.mult, op1=ALU.add).then_inc(summed, 1)
                        turn(0, True)
                        with dve.Fori(1, TURNS) as i:
                            turn(i, False)
                        dve.wait_ge(summed, C)
                        nc.vector.tensor_copy(carry[:, 0:D], sums[:, NS - 1, G - 1, :])

                    @block.scalar
                    def _(act):
                        view = sums_d.rearrange("(p c) f -> p c f", c=C)

                        with act.Fori(0, TURNS) as i:
                            for s in range(NS):
                                act.wait_ge(summed, (i * NS + s + 1) * G)
                                act.dma_start(view[:, bass.ds((i * NS + s) * G, G), :], sums[:, s, :, :]).then_inc(stored[s], 16)
                        for s in range(NS):
                            act.wait_ge(stored[s], 16 * TURNS)

        def layer2_nodes():
            def scratch(st):
                e = {}
                linear_scratch(st, e, 1)
                for k in ("bias", "gamma", "beta", "wo"):
                    e[k] = sb(k, [P, D], F32, st)
                e["stats"] = sb("stats", [P, GN, 6], F32, st)
                for k in ("mean", "dev", "std"):
                    e[k] = sb(k, [P, GN], F32, st)
                e["eps"] = sb("eps", [P, 1], F32, st)
                for k in ("w_turned", "w_ready", "var_ready", "std_ready"):
                    e[k] = sem(k, st)

                def prepare(dve, line):
                    line.link(nc.vector.memset(e["eps"][:], LN_EPS))
                    dve.wait_ge(e["w_turned"], 1)
                    nc.vector.tensor_copy(e["w"][:, 0, :], e["lin_ps"][:, 0, :]).then_inc(e["w_ready"], 1)
                e["prepare"] = prepare
                return e

            def consts(sp, e):
                sp.dma_start(e["wo"][:], ow_in).then_inc(e["loaded"], 16)
                for k, src in (("bias", ob_in), ("gamma", lng_in), ("beta", lnb_in)):
                    sp.dma_start(e[k][:], src.rearrange("(a f) -> a f", a=1).to_broadcast([P, D])).then_inc(e["loaded"], 16)
                sp.wait_ge(e["loaded"], 64)

            def body(dve, line, k, total, reach, e):
                tiles = bass.ds(k * GN, GN)
                m = e["left"][:, 0, :, :]

                def tiled(ap):
                    return ap.unsqueeze(2).to_broadcast([P, GN, D])

                def rowed(ap):
                    return ap.unsqueeze(1).to_broadcast([P, GN, D])

                line.link(nc.vector.tensor_tensor(m, total[:, :, 0:D], reach[:, :, 0:D], ALU.add))
                nc.vector.tensor_tensor(m, m, tiled(has[:, tiles]), ALU.mult).then_inc(e["left_ready"], 1)
                dve.wait_ge(e["multiplied"], k + 1)
                line.link(nc.vector.tensor_tensor(m, e["lin_ps"][:], rowed(e["bias"][:]), ALU.add))
                line.link(nc.vector.tensor_tensor(m, m, h[:, tiles, :], ALU.add))
                for j in range(GN):
                    line.mark(nc.vector.bn_stats(e["stats"][:, j, :], e["left"][:, 0, j, :]))
                dve.wait_ge(line.sem, line.n)
                stats = e["stats"]
                line.link(nc.vector.tensor_tensor(e["mean"][:], stats[:, :, 1], stats[:, :, 4], ALU.add))
                line.link(nc.vector.tensor_scalar(e["mean"][:], e["mean"][:], 0.5, None, ALU.mult))
                line.link(nc.vector.tensor_tensor(e["dev"][:], stats[:, :, 1], stats[:, :, 4], ALU.subtract))
                line.link(nc.vector.scalar_tensor_tensor(out=e["dev"][:], in0=e["dev"][:], scalar=0.25, in1=e["dev"][:],
                                                         op0=ALU.mult, op1=ALU.mult))
                line.link(nc.vector.tensor_tensor(e["std"][:], stats[:, :, 2], stats[:, :, 5], ALU.add))
                nc.vector.scalar_tensor_tensor(out=e["dev"][:], in0=e["std"][:], scalar=1.0 / D, in1=e["dev"][:],
                                               op0=ALU.mult, op1=ALU.add).then_inc(e["var_ready"], 1)
                line.link(nc.vector.tensor_tensor(m, m, tiled(e["mean"][:]), ALU.subtract))
                dve.wait_ge(e["std_ready"], k + 1)
                line.link(nc.vector.reciprocal(e["std"][:], e["std"][:]))
                line.link(nc.vector.tensor_tensor(m, m, tiled(e["std"][:]), ALU.mult))
                line.link(nc.vector.tensor_tensor(m, m, rowed(e["gamma"][:]), ALU.mult))
                line.link(nc.vector.tensor_tensor(m, m, rowed(e["beta"][:]), ALU.add))
                line.link(nc.vector.tensor_tensor(x[:, tiles, :], x[:, tiles, :], m, ALU.add))

            def act_body(act, k, first, e):
                linear_act(act, k, first, e)
                act.wait_ge(e["var_ready"], k + 1)
                act.activation(e["std"][:], e["dev"][:], ACT.Sqrt, bias=e["eps"][:, 0:1]).then_inc(e["std_ready"], 1)

            def pe_start(pe, e):
                pe.wait_ge(e["loaded"], 64)
                nc.tensor.transpose(e["lin_ps"][:, 0, :], e["wo"][:], ident[:]).then_inc(e["w_turned"], 1)
                pe.wait_ge(e["w_ready"], 1)

            node_totals("nodes2", s2_d, D, D, 1, 3 + 5 + 5 + 6, scratch, consts, body, act_body, linear_pe, pe_start)

        def heads_of(ap):
            return ap.rearrange("p j (k d) -> p j k d", k=K3)

        def gat_tables(name, g, xw, selfs, first):
            w_in, a_src_in, a_dst_in = g[0], g[1], g[2]
            st = Stage(name)
            with st:
                w = sb("w", [P, D], F32, st)
                a_src = sb("a_src", [P, D], F32, st)
                a_dst = sb("a_dst", [P, D], F32, st)
                left = sb("left", [P, GN, D], F32, st)
                left_t = sb("left_t", [P, GN, D], F32, st)
                made = sb("made", [P, 2, GN, WG], F32, st)
                prod = sb("prod", [P, 2, GN, D], F32, st)
                zeros = sb("zeros", [P, C, K3], F32, st) if first else None
                start_slot = sb("start_slot", [P, 2, GN], I32, st)
                pair = sb("pair", [P, 2, GN, 2 * K3], F32, st)
                turn_ps = pb("turn_ps", [P, GN, D], st)
                lin_ps = pb("lin_ps", [P, GN, D], st)
                loaded, copied, turned, evacuated = sem("loaded", st), sem("copied", st), sem("turned", st), sem("evacuated", st)
                multiplied, made_ready, dve_steps = sem("multiplied", st), sem("made_ready", st), sem("dve_steps", st)
                zeroed, zeros_out, staged, selfs_saved = sem("zeroed", st), sem("zeros_out", st), sem("staged", st), sem("selfs_saved", st)
                saved = [sem(f"saved{s}", st) for s in range(2)]
                put, g0 = gathered, gathered_before(2, GN * NG // 2)
                per = 7
                with nc.Block() as block:
                    @block.sync
                    def _(sp):
                        sp.dma_start(w[:], w_in).then_inc(loaded, 16)
                        for tile, src in ((a_src, a_src_in), (a_dst, a_dst_in)):
                            sp.dma_start(tile[:], src.rearrange("(a k) d -> a (k d)", a=1).to_broadcast([P, D])).then_inc(loaded, 16)
                        if first:
                            sp.wait_ge(zeroed, 1)
                            sp.dma_start(start_rows_d.rearrange("(p c) f -> p (c f)", c=C),
                                         zeros[:].rearrange("p c f -> p (c f)")).then_inc(zeros_out, 16)
                            sp.wait_ge(zeros_out, 16)
                        view = xw_d.rearrange("(p t) f -> p t f", t=T)
                        with sp.Fori(0, NG // 2) as i:
                            for s in range(2):
                                t0 = sp.snap((i * 2 + s) * GN)
                                sp.wait_ge(made_ready, i * 2 + s + 1)
                                sp.sem_inc(sp_gate, 1)
                                sp.dma_start(view[:, bass.ds(t0, GN), :], made[:, s, :, :]).then_inc(saved[s], 16)
                        sp.wait_ge(made_ready, NG)
                        sp.dma_start(self_d.rearrange("(p t) f -> p t f", t=T), selfs[:]).then_inc(selfs_saved, 16)
                        for s in range(2):
                            sp.wait_ge(saved[s], 16 * (NG // 2))
                        sp.wait_ge(selfs_saved, 16)

                    @block.scalar
                    def _(act):
                        def group(i, s, begin):
                            k = i * 2 + s
                            if not (begin and s == 0):
                                act.wait_ge(turned, k)
                                act.sem_inc(act_gate, 1)
                            act.activation(left[:], h[:, bass.ds(k * GN, GN), :], ACT.Copy).then_inc(copied, 1)
                            if not begin:
                                act.wait_ge(put[s], i * (16 * GN) + g0[s])
                                act.sem_inc(act_gate, 1)
                            act.activation(start_slot[:, s, :], start_i[:, bass.ds(k * GN, GN)], ACT.Copy).then_inc(staged, 1)
                            act.wait_ge(turned, k + 1)
                            if not (begin and s == 0):
                                act.wait_ge(multiplied, k)
                            act.activation(left_t[:], turn_ps[:], ACT.Copy).then_inc(evacuated, 1)
                        for s in range(2):
                            group(0, s, True)
                        with act.Fori(1, NG // 2) as i:
                            for s in range(2):
                                group(i, s, False)

                    @block.gpsimd
                    def _(pool):
                        if first:
                            pool.wait_ge(zeros_out, 16)
                        with pool.Fori(0, NG // 2) as i:
                            for s in range(2):
                                pool.wait_ge(staged, i * 2 + s + 1)
                                pool.sem_inc(pool_gate, 1)
                                pool.wait_ge(made_ready, i * 2 + s + 1)
                                pool.sem_inc(pool_gate, 1)
                                for j in range(GN):
                                    nc.gpsimd.indirect_dma_start(
                                        out=start_rows_d, in_=pair[:, s, j, 0:K3], in_offset=None,
                                        out_offset=bass.IndirectOffsetOnAxis(ap=start_slot[:, s, j:j + 1], axis=0),
                                        bounds_check=EP - 1, oob_is_err=False).then_inc(put[s], 16)
                        for s in range(2):
                            pool.wait_ge(put[s], g0[s] + 16 * GN * (NG // 2))

                    @block.tensor
                    def _(pe):
                        pe.wait_ge(loaded, 48)

                        def group(k, begin):
                            pe.wait_ge(copied, k + 1)
                            for j in range(GN):
                                ins = nc.tensor.transpose(turn_ps[:, j, :], left[:, j, :], ident[:])
                            ins.then_inc(turned, 1)
                            pe.wait_ge(evacuated, k + 1)
                            if not begin:
                                pe.wait_ge(made_ready, k)
                            for j in range(GN):
                                ins = nc.tensor.matmul(lin_ps[:, j, :], left_t[:, j, :], w[:], start=True, stop=True)
                            ins.then_inc(multiplied, 1)
                        group(0, True)
                        with pe.Fori(1, NG) as i:
                            group(i, False)

                    @block.vector
                    def _(dve):
                        line = Line(dve, dve_steps)
                        if first:
                            nc.vector.memset(zeros[:], 0.0).then_inc(zeroed, 1)
                        line.link(nc.vector.memset(made[:], 1.0))
                        base = line.n
                        dve.wait_ge(loaded, 48)

                        def group(i, s, begin):
                            k = i * 2 + s
                            tiles = bass.ds(k * GN, GN)
                            m = heads_of(made[:, s, :, 0:WS3])[:, :, :, 0:D3]
                            line.n = k * per + base
                            if not begin:
                                dve.wait_ge(saved[s], i * 16)
                                dve.wait_ge(put[s], i * (16 * GN) + g0[s])
                            dve.wait_ge(multiplied, k + 1)
                            line.mark(nc.vector.tensor_copy(m, lin_ps[:].rearrange("p j (k d) -> p j k d", k=K3)))
                            for n, a in ((0, a_src), (1, a_dst)):
                                line.mark(nc.vector.tensor_tensor(prod[:, n, :, :], lin_ps[:], a[:].unsqueeze(1).to_broadcast([P, GN, D]), ALU.mult))
                            dve.wait_ge(line.sem, line.n)
                            for n, o in ((0, made[:, s, :, WS3:WG]), (1, pair[:, s, :, 0:K3])):
                                line.mark(nc.vector.tensor_reduce(o, prod[:, n, :, :].rearrange("p j (k d) -> p j k d", k=K3), AX.X, ALU.add))
                            dve.wait_ge(line.sem, line.n)
                            nc.vector.tensor_copy(xw[:, tiles, :], made[:, s, :, 0:WS3])
                            own = pair[:, s, :, K3:2 * K3]
                            line.link(nc.vector.tensor_tensor(own, made[:, s, :, WS3:WG], pair[:, s, :, 0:K3], ALU.add))
                            line.link(nc.vector.scalar_tensor_tensor(out=own, in0=own, scalar=0.2, in1=own, op0=ALU.mult, op1=ALU.max))
                            nc.vector.tensor_copy(selfs[:, tiles, :], pair[:, s, :, :]).then_inc(made_ready, 1)
                        for s in range(2):
                            group(0, s, True)
                        with dve.Fori(1, NG // 2) as i:
                            for s in range(2):
                                group(i, s, False)

        def gat_sum(name, layer):
            st = Stage(name)
            with st:
                idx_slot = sb("idx_slot", [P, BS * NS, G], I32, st)
                rows = sb("rows", [P, BS * NS, G, WG], F32, st)
                sums = sb("sums", [P, BS, BW, WG], F32, st)
                held = sb("held", [P, K3, C], F32, st)
                initial = sb("initial", [P, 2 * K3], F32, st)
                stay = sb("stay", [P, BS, BW + 1], F32, st)
                logit = sb("logit", [P, K3, BW], F32, st)
                top = sb("top", [P, BS, K3, BW], F32, st)
                weight = sb("weight", [P, K3, BW + 1], F32, st)
                before = sb("before", [P, WS3], F32, st)
                got_start, got_initial = sem("got_start", st), initial_gathered
                got, g0 = gathered, gathered_before(BS * NS, C // (BS * NS))
                idx_ready, stay_ready, dve_steps = sem("idx_ready", st), sem("stay_ready", st), sem("dve_steps", st)
                shifted, exped, topped, summed = sem("shifted", st), sem("exped", st), sem("topped", st), sem("summed", st)
                stored = [sem(f"stored{b}", st) for b in range(BS)]
                at_start = sums[:].rearrange("p b c f -> p (b c f)")[:, 0:C * K3]
                with nc.Block() as block:
                    @block.gpsimd
                    def _(pool):
                        nc.gpsimd.indirect_dma_start(out=initial[:], out_offset=None, in_=self_d,
                                                     in_offset=bass.IndirectOffsetOnAxis(ap=dst0_i[:], axis=0)).then_inc(got_initial, 16)

                        def turn(i, first):
                            for s in range(BS * NS):
                                pool.wait_ge(idx_ready, (i * BS + s // NS) * NS + (s % NS + 1))
                                if not first:
                                    pool.sem_inc(pool_gate, 1)
                                    pool.wait_ge(summed, i * (BS * BW) + ((s + 1) * G - BS * BW))
                                pool.sem_inc(pool_gate, 1)
                                for j in range(G):
                                    nc.gpsimd.indirect_dma_start(
                                        out=rows[:, s, j, :], out_offset=None, in_=xw_d,
                                        in_offset=bass.IndirectOffsetOnAxis(ap=idx_slot[:, s, j:j + 1], axis=0)).then_inc(got[s], 16)
                        turn(0, True)
                        with pool.Fori(1, BTURNS) as i:
                            turn(i, False)

                    @block.scalar
                    def _(act):
                        def stage_stay(b, cols):
                            act.activation(stay[:, b, 0:BW], cont[:, cols], ACT.Copy, bias=LOW, scale=-LOW).then_inc(stay_ready, 1)

                        def stage_idx(s, cols):
                            act.activation(idx_slot[:, s, :], src_i[:, cols], ACT.Copy).then_inc(idx_ready, 1)

                        for s in range(BS * NS):
                            stage_idx(s, slice(s * G, (s + 1) * G))
                        for b in range(BS):
                            stage_stay(b, slice(b * BW, (b + 1) * BW))

                        def turn(i, first, last):
                            for b in range(BS):
                                k = i * BS + b
                                if not last:
                                    for s in range(b * NS, (b + 1) * NS):
                                        act.wait_ge(got[s], i * (16 * G) + (g0[s] + 16 * G))
                                        act.sem_inc(act_gate, 1)
                                        stage_idx(s, bass.ds((i + 1) * (BS * BW) + s * G, G))
                                act.wait_ge(shifted, k + 1)
                                act.activation(weight[:], weight[:], ACT.Exp).then_inc(exped, 1)
                                if not last:
                                    stage_stay(b, bass.ds((i + 1) * (BS * BW) + b * BW, BW))
                                if not first:
                                    act.wait_ge(stored[b], i * 16)
                                act.activation(sums[:, b, :, WS3:WG], top[:, b, :, :].rearrange("p k j -> p j k"), ACT.Copy).then_inc(topped, 1)
                        turn(0, True, False)
                        with act.Fori(1, BTURNS - 1) as i:
                            turn(i, False, False)
                        turn(BTURNS - 1, False, True)

                    @block.vector
                    def _(dve):
                        line = Line(dve, dve_steps)
                        line.link(nc.vector.memset(stay[:, :, BW:BW + 1], LOW))
                        dve.wait_ge(got_start, 16)
                        dve.wait_ge(got_initial, 16 * (layer + 1))
                        for k in range(K3):
                            line.mark(nc.vector.tensor_tensor_scan(held[:, k, :], cont[:],
                                                                   at_start.rearrange("p (c f) -> p c f", f=K3)[:, :, k],
                                                                   initial[:, k:k + 1], ALU.mult, ALU.add))
                        dve.wait_ge(line.sem, line.n)
                        line.mark(nc.vector.memset(top[:, BS - 1, :, BW - 1:BW], LOW))
                        line.link(nc.vector.memset(sums[:, BS - 1, BW - 1, 0:WS3], 0.0))
                        base, per = line.n, 14

                        def block_of_columns(i, b, first):
                            k = i * BS + b
                            line.n = k * per + base
                            pb_ = (b - 1) % BS
                            rows_b = rows[:, b * NS:(b + 1) * NS, :, :].rearrange("p s j f -> p (s j) f")
                            for s in range(b * NS, (b + 1) * NS):
                                dve.wait_ge(got[s], i * (16 * G) + (g0[s] + 16 * G))
                            line.link(nc.vector.tensor_tensor(logit[:], rows_b[:, :, WS3:WG].rearrange("p j k -> p k j"),
                                                              held[:, :, bass.ds(k * BW, BW)], ALU.add))
                            line.link(nc.vector.scalar_tensor_tensor(out=logit[:], in0=logit[:], scalar=0.2, in1=logit[:],
                                                                     op0=ALU.mult, op1=ALU.max))
                            dve.wait_ge(stay_ready, k + 1)
                            if not first:
                                dve.wait_ge(topped, k - 1)
                            for n in range(K3):
                                line.mark(nc.vector.tensor_tensor_scan(top[:, b, n, :], stay[:, b, 0:BW], logit[:, n, :],
                                                                       top[:, pb_, n, BW - 1:BW], ALU.add, ALU.max))
                            dve.wait_ge(line.sem, line.n)
                            for n in range(K3):
                                line.mark(nc.vector.tensor_tensor_scan(top[:, b, n, ::-1], stay[:, b, 1:BW + 1][:, ::-1],
                                                                       top[:, b, n, ::-1], LOW, ALU.add, ALU.max))
                            dve.wait_ge(line.sem, line.n)
                            line.mark(nc.vector.tensor_tensor(weight[:, :, 0:BW], logit[:], top[:, b, :, :], ALU.subtract))
                            line.link(nc.vector.tensor_tensor(weight[:, :, BW:BW + 1], top[:, pb_, :, BW - 1:BW], top[:, b, :, 0:1], ALU.subtract))
                            nc.vector.tensor_scalar(weight[:, :, BW], weight[:, :, BW], 0.0, None, ALU.min).then_inc(shifted, 1)
                            dve.wait_ge(exped, k + 1)
                            line.mark(nc.vector.tensor_tensor(
                                before[:].rearrange("p (k d) -> p k d", k=K3), sums[:, pb_, BW - 1, 0:WS3].rearrange("p (k d) -> p k d", k=K3),
                                weight[:, :, BW:BW + 1].to_broadcast([P, K3, WH]), ALU.mult))
                            line.link(nc.vector.tensor_tensor(
                                heads_of(rows_b[:, :, 0:WS3]), heads_of(rows_b[:, :, 0:WS3]),
                                over_heads(weight[:, :, 0:BW].rearrange("p k j -> p j k"), K3, WH), ALU.mult))
                            if not first:
                                dve.wait_ge(stored[b], i * 16)
                            for j in range(BW):
                                if j:
                                    dve.wait_ge(summed, i * (BS * BW) + (b * BW + j))
                                nc.vector.scalar_tensor_tensor(
                                    out=sums[:, b, j, 0:WS3], in0=sums[:, b, j - 1, 0:WS3] if j else before[:],
                                    scalar=cont[:, bass.ds(k * BW + j, 1)], in1=rows_b[:, j, 0:WS3],
                                    op0=ALU.mult, op1=ALU.add).then_inc(summed, 1)
                            dve.wait_ge(summed, (k + 1) * BW)
                        for b in range(BS):
                            block_of_columns(0, b, True)
                        with dve.Fori(1, BTURNS) as i:
                            for b in range(BS):
                                block_of_columns(i, b, False)
                        dve.wait_ge(topped, BTURNS * BS)
                        nc.vector.tensor_copy(carry[:, 0:WG], sums[:, BS - 1, BW - 1, :])

                    @block.sync
                    def _(sp):
                        sp.dma_start(at_start, start_rows_d.rearrange("(p c) f -> p (c f)", c=C)).then_inc(got_start, 16)
                        view = s3_d.rearrange("(p c) f -> p c f", c=C)
                        with sp.Fori(0, BTURNS) as i:
                            for b in range(BS):
                                c0 = sp.snap((i * BS + b) * BW)
                                sp.wait_ge(summed, (i * BS + b + 1) * BW)
                                sp.sem_inc(sp_gate, 1)
                                sp.wait_ge(topped, i * BS + b + 1)
                                sp.sem_inc(sp_gate, 1)
                                sp.dma_start(view[:, bass.ds(c0, BW), :], sums[:, b, :, :]).then_inc(stored[b], 16)
                        for b in range(BS):
                            sp.wait_ge(stored[b], 16 * BTURNS)

        def gat_chain(name):
            HALF = WS3 // 2
            st = Stage(name)
            with st:
                pen_single = sb("pen_single", [P, P], F32, st)
                pen_first = sb("pen_first", [P, 1], F32, st)
                chained = sb("chained", [K3, P + 1], F32, st)
                ahead = sb("ahead", [P, 2, K3], F32, st)
                scale = sb("scale", [P, 2, K3], F32, st)
                keep = sb("keep", [P, WS3], F32, st)
                own = sb("own", [P, WS3], F32, st)
                keep_t = sb("keep_t", [HALF, P], F32, st)
                turned = sb("turned", [HALF, P + 1], F32, st)
                max_ps = pb("max_ps", [K3, P], st)
                ahead_ps = pb("ahead_ps", [P, 2, K3], st)
                keep_ps = pb("keep_ps", [HALF, P], st)
                own_ps = pb("own_ps", [HALF, P], st)
                back_ps = pb("back_ps", [P, HALF], st)
                dve_steps, pe_done, ready, exped = sem("dve_steps", st), sem("pe_done", st), sem("ready", st), sem("exped", st)
                with nc.Block() as block:
                    @block.tensor
                    def _(pe):
                        nc.tensor.transpose(max_ps[:], carry[:, WS3:WG], ident[:]).then_inc(pe_done, 1)
                        pe.wait_ge(ready, 1)
                        nc.tensor.transpose(ahead_ps[:, 0, :], chained[:, 0:P], ident[0:K3, 0:K3])
                        nc.tensor.transpose(ahead_ps[:, 1, :], chained[:, 1:P + 1], ident[0:K3, 0:K3]).then_inc(pe_done, 1)
                        pe.wait_ge(ready, 3)
                        for n in range(2):
                            if n:
                                pe.wait_ge(ready, 5)
                            cols = slice(n * HALF, (n + 1) * HALF)
                            nc.tensor.transpose(keep_ps[:], keep[:, cols], ident[:])
                            nc.tensor.transpose(own_ps[:], own[:, cols], ident[:]).then_inc(pe_done, 1)
                            pe.wait_ge(ready, 4 + 2 * n)
                            nc.tensor.transpose(back_ps[:], turned[:, 0:P], ident[0:HALF, 0:HALF]).then_inc(pe_done, 1)

                    @block.scalar
                    def _(act):
                        act.wait_ge(ready, 2)
                        act.activation(scale[:], scale[:], ACT.Exp).then_inc(exped, 1)

                    @block.vector
                    def _(dve):
                        line = Line(dve, dve_steps)
                        for tile, mask in ((pen_single[:], single_row[:]), (pen_first[:], in_first[:, C - 1:C])):
                            line.mark(nc.vector.tensor_scalar(tile, mask, -1.0, -LOW, ALU.add, ALU.mult))
                        line.link(nc.vector.memset(chained[:, 0:1], LOW))
                        dve.wait_ge(pe_done, 1)
                        nc.vector.tensor_tensor_scan(chained[:, 1:P + 1], pen_single[0:K3, :], max_ps[:], LOW,
                                                     ALU.add, ALU.max).then_inc(ready, 1)
                        dve.wait_ge(pe_done, 2)
                        line.link(nc.vector.tensor_copy(ahead[:], ahead_ps[:]))
                        line.mark(nc.vector.scalar_tensor_tensor(out=scale[:, 0, :], in0=ahead[:, 0, :], scalar=pen_first[:, 0:1],
                                                                 in1=ahead[:, 1, :], op0=ALU.add, op1=ALU.subtract))
                        line.link(nc.vector.tensor_tensor(scale[:, 1, :], carry[:, WS3:WG], ahead[:, 1, :], ALU.subtract))
                        nc.vector.tensor_scalar(scale[:], scale[:], 0.0, None, ALU.min).then_inc(ready, 1)
                        dve.wait_ge(exped, 1)

                        def wide(ap):
                            return ap.unsqueeze(2).to_broadcast([P, K3, WH])
                        line.mark(nc.vector.tensor_copy(keep[:].rearrange("p (k d) -> p k d", k=K3), wide(scale[:, 0, :])))
                        line.mark(nc.vector.tensor_copy(carry[:, WS3:WG], ahead[:, 0, :]))
                        nc.vector.tensor_tensor(own[:].rearrange("p (k d) -> p k d", k=K3),
                                                carry[:, 0:WS3].rearrange("p (k d) -> p k d", k=K3), wide(scale[:, 1, :]),
                                                ALU.mult).then_inc(ready, 1)
                        line.link(nc.vector.memset(turned[:, 0:1], 0.0))
                        for n in range(2):
                            dve.wait_ge(pe_done, 3 + 2 * n)
                            line.link(nc.vector.tensor_copy(keep_t[:], keep_ps[:]))
                            nc.vector.tensor_tensor_scan(turned[:, 1:P + 1], keep_t[:], own_ps[:], 0.0,
                                                         ALU.mult, ALU.add).then_inc(ready, 1)
                            dve.wait_ge(pe_done, 4 + 2 * n)
                            nc.vector.tensor_copy(carry[:, n * HALF:(n + 1) * HALF], back_ps[:]).then_inc(ready, 1)

        def gat_nodes(name, g, xw, selfs):
            def scratch(st):
                e = {"bias": sb("bias", [P, D], F32, st), "loaded": sem("loaded", st),
                     "logit_ready": sem("logit_ready", st), "exped": sem("exped", st)}
                for k in ("last", "earlier", "own"):
                    e[k] = sb(k, [P, GN, WS3], F32, st)
                e["scale"] = sb("scale", [P, GN, 3 * K3], F32, st)
                e["top"] = sb("top", [P, GN, K3], F32, st)

                def prepare(dve, line):
                    dve.wait_ge(e["loaded"], 16)
                e["prepare"] = prepare
                return e

            def consts(sp, e):
                sp.dma_start(e["bias"][:], g[3].rearrange("(a f) -> a f", a=1).to_broadcast([P, D])).then_inc(e["loaded"], 16)
                sp.wait_ge(e["loaded"], 16)

            def body(dve, line, k, total, reach, e):
                tiles = bass.ds(k * GN, GN)
                scale, top, last, earlier, own = e["scale"], e["top"], e["last"], e["earlier"], e["own"]

                def of_heads(ap):
                    return ap.unsqueeze(2).to_broadcast([P, GN, K3])

                line.mark(nc.vector.tensor_tensor(scale[:, :, 0:K3], total[:, :, WS3:WG], of_heads(low_without[:, tiles]), ALU.add))
                line.mark(nc.vector.tensor_tensor(scale[:, :, K3:2 * K3], reach[:, :, WS3:WG], of_heads(low_unreached[:, tiles]), ALU.add))
                line.link(nc.vector.tensor_copy(scale[:, :, 2 * K3:3 * K3], selfs[:, tiles, K3:2 * K3]))
                line.link(nc.vector.tensor_tensor(top[:], scale[:, :, 0:K3], scale[:, :, K3:2 * K3], ALU.max))
                line.link(nc.vector.tensor_tensor(top[:], top[:], scale[:, :, 2 * K3:3 * K3], ALU.max))
                nc.vector.tensor_tensor(scale[:].rearrange("p j (a k) -> p j a k", a=3), scale[:].rearrange("p j (a k) -> p j a k", a=3),
                                        top[:].unsqueeze(2).to_broadcast([P, GN, 3, K3]), ALU.subtract).then_inc(e["logit_ready"], 1)
                dve.wait_ge(e["exped"], k + 1)
                for n, (part, values) in enumerate(((last, total[:, :, 0:WS3]), (earlier, reach[:, :, 0:WS3]), (own, xw[:, tiles, :]))):
                    line.mark(nc.vector.tensor_tensor(heads_of(part[:]), heads_of(values),
                                                      over_heads(scale[:, :, n * K3:(n + 1) * K3], K3, WH), ALU.mult))
                dve.wait_ge(line.sem, line.n)
                line.link(nc.vector.tensor_tensor(last[:], last[:], earlier[:], ALU.add))
                line.link(nc.vector.tensor_tensor(last[:], last[:], own[:], ALU.add))
                line.link(nc.vector.reciprocal(top[:], heads_of(last[:])[:, :, :, D3]))
                features = own[:, :, 0:D].rearrange("p j (k d) -> p j k d", k=K3)
                line.link(nc.vector.tensor_tensor(features, heads_of(last[:])[:, :, :, 0:D3], over_heads(top[:], K3, D3), ALU.mult))
                line.link(nc.vector.tensor_tensor(h[:, tiles, :], own[:, :, 0:D], e["bias"][:].unsqueeze(1).to_broadcast([P, GN, D]), ALU.add))

            def act_body(act, k, first, e):
                act.wait_ge(e["logit_ready"], k + 1)
                act.activation(e["scale"][:], e["scale"][:], ACT.Exp).then_inc(e["exped"], 1)

            node_totals(name, s3_d, WG, WG, 0, 13, scratch, consts, body, act_body)

        def batch_norm_elu(name, g, last):
            st = Stage(name)
            with st:
                squares = sb("squares", [P, T, D], F32, st)
                part = sb("part", [P, D], F32, st)
                valid = sb("valid", [P, P], F32, st)
                mean = sb("mean", [P, D], F32, st)
                std = sb("std", [P, D], F32, st)
                gamma = sb("gamma", [P, D], F32, st)
                beta = sb("beta", [P, D], F32, st)
                eps = sb("eps", [P, 1], F32, st)
                real = sb("real", [P, 1], F32, st)
                tot_ps = pb("tot_ps", [P, D], st)
                loaded, part_ready, totalled, dve_steps = sem("loaded", st), sem("part_ready", st), sem("totalled", st), sem("dve_steps", st)
                std_ready, low_ready, exped = sem("std_ready", st), sem("low_ready", st), sem("exped", st)

                def all_tiles(ap):
                    return ap.unsqueeze(1).to_broadcast([P, T, D])

                with nc.Block() as block:
                    @block.sync
                    def _(sp):
                        for tile, src in ((gamma, g[4]), (beta, g[5])):
                            sp.dma_start(tile[:], src.rearrange("(a f) -> a f", a=1).to_broadcast([P, D])).then_inc(loaded, 16)
                        sp.wait_ge(loaded, 32)

                    @block.tensor
                    def _(pe):
                        for n in range(2):
                            pe.wait_ge(part_ready, n + 1)
                            nc.tensor.matmul(tot_ps[:], valid[:], part[:], start=True, stop=True).then_inc(totalled, 1)

                    @block.scalar
                    def _(act):
                        act.wait_ge(totalled, 2)
                        act.activation(std[:], tot_ps[:], ACT.Sqrt, bias=eps[:, 0:1], scale=1.0 / N).then_inc(std_ready, 1)
                        act.wait_ge(low_ready, 1)
                        act.activation(squares[:], squares[:], ACT.Exp).then_inc(exped, 1)

                    @block.vector
                    def _(dve):
                        line = Line(dve, dve_steps)
                        line.link(nc.vector.memset(eps[:], LN_EPS))
                        line.link(nc.vector.tensor_scalar(real[:], lane[:], float(PN), None, ALU.is_lt))
                        line.link(nc.vector.tensor_copy(valid[:], real[:].to_broadcast([P, P])))
                        nc.vector.tensor_reduce(part[:], h[:].rearrange("p t f -> p f t"), AX.X, ALU.add).then_inc(part_ready, 1)
                        dve.wait_ge(totalled, 1)
                        line.link(nc.vector.tensor_scalar(mean[:], tot_ps[:], 1.0 / N, None, ALU.mult))
                        line.link(nc.vector.tensor_tensor(h[:], h[:], all_tiles(mean[:]), ALU.subtract))
                        line.link(nc.vector.tensor_tensor(squares[:], h[:], h[:], ALU.mult))
                        nc.vector.tensor_reduce(part[:], squares[:].rearrange("p t f -> p f t"), AX.X, ALU.add).then_inc(part_ready, 1)
                        dve.wait_ge(std_ready, 1)
                        line.link(nc.vector.reciprocal(std[:], std[:]))
                        dve.wait_ge(loaded, 32)
                        line.link(nc.vector.tensor_tensor(std[:], std[:], gamma[:], ALU.mult))
                        line.link(nc.vector.tensor_tensor(h[:], h[:], all_tiles(std[:]), ALU.mult))
                        line.link(nc.vector.tensor_tensor(h[:], h[:], all_tiles(beta[:]), ALU.add))
                        nc.vector.tensor_scalar(squares[:], h[:], 0.0, None, ALU.min).then_inc(low_ready, 1)
                        line.link(nc.vector.tensor_scalar(h[:], h[:], 0.0, None, ALU.max))
                        dve.wait_ge(exped, 1)
                        line.link(nc.vector.scalar_tensor_tensor(out=h[:], in0=squares[:], scalar=-1.0, in1=h[:], op0=ALU.add, op1=ALU.add))
                        if last:
                            line.link(nc.vector.tensor_tensor(x[:], x[:], h[:], ALU.add))

        def finish():
            st = Stage("finish")
            with st:
                written = sem("written", st)
                with nc.Block() as block:
                    @block.sync
                    def _(sp):
                        ov = out.rearrange("(p t) f -> p t f", t=T)
                        sp.dma_start(ov[0:112], x[0:112, :, :]).then_inc(written, 16)
                        sp.dma_start(ov[112:PN], x[112:PN, :, :]).then_inc(written, 16)
                        sp.wait_ge(written, 32)

        setup()
        norm_relu("norm0", h0_d)
        gather_sum("sum0", h0_d, s0_d, True)
        chain_runs("chain0", [(0, D, False), (D, D, True)])
        layer0_nodes()
        norm_relu("norm1", h1_d)
        gather_sum("sum1", h1_d, s1_d, False)
        chain_runs("chain1", [(0, D, False)])
        layer1_nodes()
        norm_relu("norm2", None)
        relation_tables()
        with ExitStack() as keep:
            weights = sb("weights2", [P, K2, C], F32, keep)
            with ExitStack() as short:
                logits = sb("logits2", [P, K2, C], F32, short)
                relation_logits(logits)
                relation_softmax(logits, weights)
            weighted_sum("sum2", v_d, s2_d, weights, K2)
        chain_runs("chain2", [(0, D, False)])
        layer2_nodes()
        renew_semaphores()
        norm_relu("norm3", None)
        with ExitStack() as keep:
            xw = sb("xw", [P, T, WS3], F32, keep)
            selfs = sb("selfs", [P, T, 2 * K3], F32, keep)
            for n, g in enumerate(g3):
                if n:
                    renew_semaphores()
                gat_tables(f"tables3{n}", g, xw, selfs, n == 0)
                gat_sum(f"sum3{n}", n)
                gat_chain(f"chain3{n}")
                gat_nodes(f"nodes3{n}", g, xw, selfs)
                batch_norm_elu(f"bn3{n}", g, n == 1)
        finish()


_INS = ['x', 'src', 'dst', 'edge_type_5', 'L0_gnn_z_agg_hard', 'L1_gnn_W', 'L1_gnn_b', 'L2_gnn_W_Q', 'L2_gnn_W_K',
        'L2_gnn_W_V', 'L2_gnn_attn_bias', 'L2_gnn_out_proj_w', 'L2_gnn_out_proj_b', 'L2_gnn_ln_gamma',
        'L2_gnn_ln_beta', 'L3_gnn_W1', 'L3_gnn_a1_src', 'L3_gnn_a1_dst', 'L3_gnn_b1', 'L3_gnn_g1', 'L3_gnn_beta1',
        'L3_gnn_W2', 'L3_gnn_a2_src', 'L3_gnn_a2_dst', 'L3_gnn_b2', 'L3_gnn_g2', 'L3_gnn_beta2']


def kernel(**inputs):
    import numpy as _np
    import concourse.bacc as _bacc
    from concourse import mybir as _mybir
    from concourse.bass_utils import run_bass_kernel_spmd as _run

    nc = _bacc.Bacc("TRN2", target_bir_lowering=False, num_devices=1)
    arrays, args = {}, []
    for name in _INS:
        a = _np.ascontiguousarray(inputs[name])
        arrays[f"in_{name}_dram"] = a
        args.append(nc.dram_tensor(f"in_{name}_dram", a.shape, _mybir.dt.from_np(a.dtype), kind="ExternalInput").ap())
    result = nc.dram_tensor("out_0_dram", (N, D), _mybir.dt.float32, kind="ExternalOutput").ap()
    build(nc, *args[:15], [args[15:21], args[21:27]], result)
    r = _run(nc, [arrays], core_ids=[0])
    return r.results[0]["out_0_dram"]
```

```python
import concourse.bass as bass
from concourse import mybir
from contextlib import ExitStack

F32 = mybir.dt.float32
BF16 = mybir.dt.bfloat16
I32 = mybir.dt.int32
ALU = mybir.AluOpType
ACT = mybir.ActivationFunctionType
AX = mybir.AxisListType

P = 128
N = 6250
E = 106250
D = 128
T = N // 125
PN = N // T
NP = P * T
G = 8
NS = 4
C = -(-E // (P * G * NS)) * G * NS
EP = P * C
TURNS = C // (G * NS)
LAST = E - (P - 1) * C
GN = 5
NG = T // GN
FAR = 1 << 20
NEG = -1.0e9
LOW = -1.0e38
R = 5
K2 = 8
D2 = D // K2
K3 = 4
D3 = D // K3
LN_EPS = 1e-5
WH = D3 + 1
WS3 = K3 * WH
WG = WS3 + K3
BW = G * NS
BS = 2
BTURNS = C // (BW * BS)
assert BTURNS * BW * BS == C


class Line:

    def __init__(self, engine, sem):
        self.engine, self.sem, self.n = engine, sem, 0

    def mark(self, instruction):
        self.n = self.n + 1
        instruction.then_inc(self.sem, 1)
        return self.n

    def link(self, instruction):
        self.engine.wait_ge(self.sem, self.mark(instruction))


def over_heads(ap, heads, width):
    return ap.unsqueeze(3).to_broadcast([ap.shape[0], ap.shape[1], heads, width])


def build(nc, x_in, src_in, dst_in, type_in, z_in, w1_in, b1_in, wq_in, wk_in, wv_in, bias_in, ow_in, ob_in,
          lng_in, lnb_in, g3, out):
    ctx = ExitStack()
    with ctx:
        def dram(name, shape):
            return nc.dram_tensor(name, shape, F32, kind="Internal").ap()

        class Stage(ExitStack):
            def __init__(self, name):
                super().__init__()
                self.name = name + "_"
                stage_names.append(name)
                assert len(set(stage_names)) == len(stage_names)

        stage_names = []

        def getname(at):
            return at.name if isinstance(at, Stage) else ""

        def sb(name, shape, dt=F32, at=ctx):
            return at.enter_context(nc.sbuf_tensor(getname(at) + name, shape, dt))

        def pb(name, shape, at=ctx):
            free = 1
            for n in shape[1:]:
                free *= n
            bank = nc.PSUM_BANK_SIZE_BYTES // 4
            whole = at.enter_context(nc.psum_tensor(getname(at) + name, [shape[0], -(-free // bank) * bank], F32))
            view = whole[:, 0:free]
            return view if len(shape) == 2 else view.rearrange("p (a b) -> p a b", a=shape[1])

        def sem(name, at=ctx):
            return at.enter_context(nc.semaphore(getname(at) + name))

        dst_d = dram("dst_d", [P, C])
        start_d = dram("start_d", [NP + 1])
        run_d = dram("run_d", [NP + 1])
        h0_d = dram("h0_d", [NP, D])
        h1_d = dram("h1_d", [NP, D])
        s0_d = dram("s0_d", [EP, 2 * D])
        s1_d = dram("s1_d", [EP, D])
        kv_d = dram("kv_d", [NP * R, 2 * D])
        q_d = dram("q_d", [NP * R, D + K2])
        v_d = dram("v_d", [EP, D])
        s2_d = dram("s2_d", [EP, D])
        xw_d = dram("xw_d", [NP, WG])
        self_d = dram("self_d", [NP, 2 * K3])
        start_rows_d = dram("start_rows_d", [EP, K3])
        s3_d = dram("s3_d", [EP, WG])

        x = sb("x", [P, T, D])
        h = sb("h", [P, T, D])
        ident = sb("ident", [P, P])
        lane = sb("lane", [P, 1])
        src_i = sb("src_i", [P, C], I32)
        cont = sb("cont", [P, C])
        in_first = sb("in_first", [P, C])
        in_last = sb("in_last", [P, C])
        kv_i = sb("kv_i", [P, C], I32)
        q_i = sb("q_i", [P, C], I32)
        type_f = sb("type_f", [P, C])
        single_row = sb("single_row", [P, P])
        link_row = sb("link_row", [P, P])
        run_rows = sb("run_rows", [P, T + GN, P], BF16)
        end_i = sb("end_i", [P, T], I32)
        start_i = sb("start_i", [P, T], I32)
        dst0_i = sb("dst0_i", [P, 1], I32)
        has = sb("has", [P, T])
        low_without = sb("low_without", [P, T])
        low_unreached = sb("low_unreached", [P, T])
        rdeg = sb("rdeg", [P, T])
        carry = sb("carry", [P, 2 * D])

        gathered = [sem(f"gathered{s}") for s in range(BS * NS)]
        gathered_count = [0] * (BS * NS)

        def gathered_before(slots, dmas):
            before = list(gathered_count)
            for s in range(slots):
                gathered_count[s] += 16 * dmas
            return before

        initial_gathered = sem("initial_gathered")

        pool_gate, sp_gate, act_gate, dve_gate, pe_gate = (sem(f"{k}_gate") for k in ("pool", "sp", "act", "dve", "pe"))

        def renew_semaphores():
            nc.all_engine_barrier(sems_to_clear=range(pe_gate.num + 1, 256))

        def rows_of_edges(flat, first, count):
            return flat[first:first + count * C].rearrange("(p c) -> p c", c=C)

        def setup():
            st = Stage("setup")
            with st:
                dst_i = sb("dst_i", [P, C], I32, st)
                prev_i = sb("prev_i", [P, C], I32, st)
                next_i = sb("next_i", [P, 1], I32, st)
                type_i = sb("type_i", [P, C], I32, st)
                dst_f = sb("dst_f", [P, C], F32, st)
                prev_f = sb("prev_f", [P, C], F32, st)
                next_f = sb("next_f", [P, 1], F32, st)
                src_f = sb("src_f", [P, C], F32, st)
                tmp = sb("tmp", [P, C], F32, st)
                ids = sb("ids", [P, T], F32, st)
                wide = sb("wide", [P, GN, P], F32, st)
                below = sb("below", [P, GN, P], F32, st)
                first_row = sb("first_row", [P, P], F32, st)
                runs = sb("runs", [P, T], F32, st)
                run_i = sb("run_i", [P, T], I32, st)
                ids_slot = sb("ids_slot", [P, GN], F32, st)
                cnt_slot = sb("cnt_slot", [P, GN], F32, st)
                cnt = sb("cnt", [P, T], F32, st)
                start = sb("start", [P, T], F32, st)
                after = sb("after", [P, T], F32, st)
                run_after = sb("run_after", [P, T], F32, st)
                ends = sb("ends", [P, 2], F32, st)
                t0 = sb("t0", [P, T], F32, st)
                t1 = sb("t1", [P, T], F32, st)
                deg = sb("deg", [P, T], F32, st)
                run_sel = sb("run_sel", [P, T], F32, st)
                dst_rows = sb("dst_rows", [P, 2, GN, C], F32, st)
                idx_slot = sb("idx_slot", [P, 2, GN], I32, st)
                row_ps = pb("row_ps", [P, GN, P], st)

                cleared, loaded, iotas = sem("cleared", st), sem("loaded", st), sem("iotas", st)
                dst_saved, nodes_saved, nodes_back = (sem("dst_saved", st), sem("nodes_saved", st),
                                                      sem("nodes_back", st))
                dve_steps, wide_ready, rows_ready = sem("dve_steps", st), sem("wide_ready", st), sem("rows_ready", st)
                runs_ready, idx_ready, dst_ready = sem("runs_ready", st), sem("idx_ready", st), sem("dst_ready", st)
                starts_ready, rows_copied = sem("starts_ready", st), sem("rows_copied", st)
                got, g0 = gathered, gathered_before(2, GN * NG // 2)
                counted = sem("counted", st)

                with nc.Block() as block:
                    @block.sync
                    def _(sp):
                        sp.wait_ge(cleared, 6)
                        parts = [(0, 112), (112, P - 1)]
                        for tile, flat in ((dst_i, dst_in), (src_i, src_in), (type_i, type_in)):
                            for a, b in parts:
                                sp.dma_start(tile[a:b, :], rows_of_edges(flat, a * C, b - a)).then_inc(loaded, 16)
                            sp.dma_start(tile[P - 1:P, 0:LAST],
                                         flat[(P - 1) * C:E].rearrange("(a c) -> a c", a=1)).then_inc(loaded, 16)
                        for a, b in ((1, 113), (113, P - 1)):
                            sp.dma_start(prev_i[a:b, :], rows_of_edges(dst_in, a * C - 1, b - a)).then_inc(loaded, 16)
                        sp.dma_start(prev_i[P - 1:P, 0:LAST],
                                     dst_in[(P - 1) * C - 1:E - 1].rearrange("(a c) -> a c", a=1)).then_inc(loaded, 16)
                        sp.dma_start(prev_i[0:1, 1:C], dst_in[0:C - 1].rearrange("(a c) -> a c", a=1)).then_inc(loaded, 16)
                        sp.dma_start(next_i[0:P - 2, :], rows_of_edges(dst_in, C, P - 2)[:, 0:1],
                                     allow_slow_non_contiguous=True).then_inc(loaded, 16)
                        sp.dma_start(next_i[P - 2:P - 1, :],
                                     dst_in[(P - 1) * C:(P - 1) * C + 1].rearrange("(a c) -> a c", a=1)).then_inc(loaded, 16)
                        xv = x_in.rearrange("(p t) f -> p t f", t=T)
                        sp.dma_start(x[0:112, :, :], xv[0:112]).then_inc(loaded, 16)
                        sp.dma_start(x[112:PN, :, :], xv[112:PN]).then_inc(loaded, 16)
                        sp.wait_ge(dst_ready, 1)
                        sp.dma_start(dst_d, dst_f[:]).then_inc(dst_saved, 16)
                        sp.wait_ge(starts_ready, 1)
                        sp.dma_start(start_d[0:NP].rearrange("(p t) -> p t", t=T), start[:]).then_inc(nodes_saved, 16)
                        sp.dma_start(run_d[0:NP].rearrange("(p t) -> p t", t=T), runs[:]).then_inc(nodes_saved, 16)
                        sp.dma_start(start_d[NP:NP + 1].rearrange("(a c) -> a c", a=1), ends[0:1, 0:1]).then_inc(nodes_saved, 16)
                        sp.dma_start(run_d[NP:NP + 1].rearrange("(a c) -> a c", a=1), ends[0:1, 1:2]).then_inc(nodes_saved, 16)
                        sp.wait_ge(nodes_saved, 64)
                        sp.dma_start(after[:], start_d[1:NP + 1].rearrange("(p t) -> p t", t=T)).then_inc(nodes_back, 16)
                        sp.dma_start(run_after[:], run_d[1:NP + 1].rearrange("(p t) -> p t", t=T)).then_inc(nodes_back, 16)
                        sp.wait_ge(nodes_back, 32)

                    @block.gpsimd
                    def _(pool):
                        nc.gpsimd.memset(ident[:], 0.0).then_inc(iotas, 1)
                        pool.wait_ge(iotas, 1)
                        nc.gpsimd.affine_select(out=ident[:], in_=ident[:], compare_op=ALU.not_equal, fill=1.0,
                                                base=0, pattern=[[-1, P]], channel_multiplier=1).then_inc(iotas, 1)
                        nc.gpsimd.iota(lane[:], pattern=[[0, 1]], base=0, channel_multiplier=1,
                                       allow_small_or_imprecise_dtypes=True).then_inc(iotas, 1)
                        nc.gpsimd.iota(ids[:], pattern=[[1, T]], base=0, channel_multiplier=T,
                                       allow_small_or_imprecise_dtypes=True).then_inc(iotas, 1)
                        pool.wait_ge(dst_saved, 16)

                        def gathers(i, s):
                            pool.wait_ge(idx_ready, i * 2 + s + 1)
                            pool.sem_inc(pool_gate, 1)
                            for j in range(GN):
                                nc.gpsimd.indirect_dma_start(
                                    out=dst_rows[:, s, j, :], out_offset=None, in_=dst_d,
                                    in_offset=bass.IndirectOffsetOnAxis(ap=idx_slot[:, s, j:j + 1], axis=0)
                                ).then_inc(got[s], 16)
                        with pool.Fori(0, NG // 2) as i:
                            for s in range(2):
                                gathers(i, s)

                    @block.scalar
                    def _(act):
                        act.wait_ge(runs_ready, 1)
                        act.activation(idx_slot[:], run_i[:, 0:2 * GN].rearrange("p (s g) -> p s g", s=2),
                                       ACT.Copy).then_inc(idx_ready, 2)
                        with act.Fori(1, NG // 2) as i:
                            for s in range(2):
                                act.wait_ge(counted, (i - 1) * 2 + s + 1)
                                act.sem_inc(act_gate, 1)
                                act.activation(idx_slot[:, s, :], run_i[:, bass.ds((i * 2 + s) * GN, GN)],
                                               ACT.Copy).then_inc(idx_ready, 1)
                        with act.Fori(0, NG) as i:
                            act.wait_ge(rows_ready, i + 4)
                            act.sem_inc(act_gate, 1)
                            act.activation(run_rows[:, bass.ds(i * GN, GN), :], row_ps[:], ACT.Copy).then_inc(rows_copied, 1)

                    @block.tensor
                    def _(pe):
                        pe.wait_ge(iotas, 2)
                        for k in range(3):
                            pe.wait_ge(wide_ready, k + 1)
                            nc.tensor.transpose(row_ps[:, 0, :], wide[:, 0, :], ident[:]).then_inc(rows_ready, 1)
                        with pe.Fori(0, NG) as i:
                            pe.wait_ge(wide_ready, i + 4)
                            for j in range(GN):
                                ins = nc.tensor.transpose(row_ps[:, j, :], wide[:, j, :], ident[:])
                            ins.then_inc(rows_ready, 1)

                    @block.vector
                    def _(dve):
                        line = Line(dve, dve_steps)
                        for tile, value in ((dst_i, FAR), (src_i, 0), (type_i, 0), (prev_i, -1), (next_i, -2)):
                            nc.vector.memset(tile[:], value).then_inc(cleared, 1)
                        nc.vector.memset(x[:], 0.0).then_inc(cleared, 1)
                        line.link(nc.vector.memset(run_rows[:, T:T + GN, :], -1.0))
                        nc.vector.memset(ends[:, 0:1], float(E))
                        line.link(nc.vector.memset(ends[:, 1:2], float(P - 1)))
                        dve.wait_ge(loaded, 17 * 16)
                        nc.vector.tensor_copy(dst_f[:], dst_i[:]).then_inc(dst_ready, 1)
                        nc.vector.tensor_copy(src_f[:], src_i[:])
                        nc.vector.tensor_copy(type_f[:], type_i[:])
                        nc.vector.tensor_copy(next_f[:], next_i[:])
                        line.link(nc.vector.tensor_copy(prev_f[:], prev_i[:]))
                        nc.vector.tensor_tensor(cont[:], dst_f[:], prev_f[:], ALU.is_equal)
                        nc.vector.tensor_scalar(in_first[:], dst_f[:], prev_f[:, 0:1], None, ALU.is_equal)
                        nc.vector.tensor_scalar(in_last[:], dst_f[:], next_f[:, 0:1], None, ALU.is_equal)
                        line.link(nc.vector.scalar_tensor_tensor(out=tmp[:], in0=src_f[:], scalar=float(R), in1=type_f[:],
                                                                 op0=ALU.mult, op1=ALU.add))
                        line.link(nc.vector.tensor_copy(kv_i[:], tmp[:]))
                        line.link(nc.vector.tensor_scalar(tmp[:], dst_f[:], float(N - 1), float(R), ALU.min, ALU.mult))
                        line.link(nc.vector.tensor_tensor(tmp[:], tmp[:], type_f[:], ALU.add))
                        line.link(nc.vector.tensor_copy(q_i[:], tmp[:]))
                        line.link(nc.vector.tensor_scalar(tmp[:, 0:1], dst_f[:, 0:1], float(N - 1), None, ALU.min))
                        line.link(nc.vector.tensor_copy(dst0_i[:], tmp[:, 0:1]))

                        def spread(column):
                            nc.vector.tensor_copy(wide[:, 0, :], column.to_broadcast([P, P])).then_inc(wide_ready, 1)

                        spread(dst_f[:, 0:1])
                        dve.wait_ge(rows_ready, 1)
                        line.link(nc.vector.tensor_copy(first_row[:], row_ps[:, 0, :]))
                        line.link(nc.vector.tensor_tensor(tmp[:, 0:1], prev_f[:, 0:1], dst_f[:, C - 1:C], ALU.is_equal))
                        spread(tmp[:, 0:1])
                        dve.wait_ge(rows_ready, 2)
                        line.link(nc.vector.tensor_copy(single_row[:], row_ps[:, 0, :]))
                        line.link(nc.vector.tensor_tensor(tmp[:, 0:1], dst_f[:, 0:1], next_f[:, 0:1], ALU.is_equal))
                        spread(tmp[:, 0:1])
                        dve.wait_ge(rows_ready, 3)
                        line.link(nc.vector.tensor_copy(link_row[:], row_ps[:, 0, :]))

                        dve.wait_ge(iotas, 4)
                        base, per = line.n, 3
                        with dve.Fori(0, NG) as i:
                            line.n = i * per + base
                            line.link(nc.vector.tensor_copy(ids_slot[:], ids[:, bass.ds(i * GN, GN)]))
                            line.link(nc.vector.tensor_tensor(
                                below[:], first_row[:].unsqueeze(1).to_broadcast([P, GN, P]),
                                ids_slot[:].unsqueeze(2).to_broadcast([P, GN, P]), ALU.is_lt))
                            line.link(nc.vector.tensor_reduce(cnt_slot[:], below[:], AX.X, ALU.add))
                            nc.vector.tensor_copy(runs[:, bass.ds(i * GN, GN)], cnt_slot[:])
                        line.n = base + NG * per
                        line.link(nc.vector.memset(tmp[:, 0:1], 0.0))
                        line.link(nc.vector.tensor_scalar(runs[:], runs[:], -1.0, 0.0, ALU.add, ALU.max))
                        nc.vector.tensor_copy(run_i[:], runs[:]).then_inc(runs_ready, 1)

                        base, per = line.n, 2
                        with dve.Fori(0, NG // 2) as i:
                            line.n = i * (2 * per) + base
                            for s in range(2):
                                line.link(nc.vector.tensor_copy(ids_slot[:], ids[:, bass.ds((i * 2 + s) * GN, GN)]))
                                dve.wait_ge(got[s], i * (16 * GN) + (g0[s] + 16 * GN))
                                for j in range(GN):
                                    ins = nc.vector.tensor_scalar(dst_rows[:, s, j, :], dst_rows[:, s, j, :],
                                                                  ids_slot[:, j:j + 1], 0.0, ALU.is_lt, ALU.add,
                                                                  accum_out=cnt_slot[:, j:j + 1])
                                line.link(ins)
                                nc.vector.tensor_copy(cnt[:, bass.ds((i * 2 + s) * GN, GN)], cnt_slot[:]).then_inc(counted, 1)
                        line.n = base + NG * per
                        dve.wait_ge(counted, NG)
                        nc.vector.scalar_tensor_tensor(out=start[:], in0=runs[:], scalar=float(C), in1=cnt[:],
                                                       op0=ALU.mult, op1=ALU.add).then_inc(starts_ready, 1)
                        dve.wait_ge(nodes_back, 32)
                        line.link(nc.vector.tensor_tensor(deg[:], after[:], start[:], ALU.subtract))
                        line.link(nc.vector.tensor_scalar(has[:], deg[:], 0.0, None, ALU.is_gt))
                        line.link(nc.vector.tensor_scalar(low_without[:], has[:], -1.0, -LOW, ALU.add, ALU.mult))
                        line.link(nc.vector.tensor_scalar(deg[:], deg[:], 1.0, None, ALU.max))
                        line.link(nc.vector.reciprocal(rdeg[:], deg[:]))
                        line.link(nc.vector.tensor_scalar(t0[:], after[:], -1.0, 0.0, ALU.add, ALU.max))
                        line.link(nc.vector.tensor_copy(end_i[:], t0[:]))
                        line.link(nc.vector.tensor_scalar(t0[:], start[:], float(-FAR), None, ALU.add))
                        line.link(nc.vector.tensor_tensor(t0[:], t0[:], has[:], ALU.mult))
                        line.link(nc.vector.tensor_scalar(t0[:], t0[:], float(FAR), None, ALU.add))
                        line.link(nc.vector.tensor_copy(start_i[:], t0[:]))
                        line.link(nc.vector.tensor_scalar(t0[:], run_after[:], float(C), None, ALU.mult))
                        line.link(nc.vector.tensor_tensor(t0[:], start[:], t0[:], ALU.is_lt))
                        line.link(nc.vector.tensor_scalar(low_unreached[:], t0[:], -1.0, -LOW, ALU.add, ALU.mult))
                        line.link(nc.vector.tensor_scalar(t1[:], run_after[:], 1.0, None, ALU.add))
                        line.link(nc.vector.tensor_tensor(t1[:], t1[:], t0[:], ALU.mult))
                        line.link(nc.vector.tensor_scalar(run_sel[:], t1[:], -1.0, None, ALU.add))
                        nc.vector.tensor_copy(wide[:], run_sel[:, 0:GN].unsqueeze(2)
                                              .to_broadcast([P, GN, P])).then_inc(wide_ready, 1)
                        with dve.Fori(1, NG) as i:
                            dve.wait_ge(rows_copied, i)
                            nc.vector.tensor_copy(wide[:], run_sel[:, bass.ds(i * GN, GN)].unsqueeze(2)
                                                  .to_broadcast([P, GN, P])).then_inc(wide_ready, 1)

        def norm_relu(name, table):
            HALF = T // 2
            OWN = 10
            STEP = 5
            st = Stage(name)
            with st:
                stats = sb("stats", [P, T, 6], F32, st)
                half = sb("half", [P, T], F32, st)
                stats_done = sem("stats_done", st)
                rstd = sb("rstd", [P, T], F32, st)
                shift = sb("shift", [P, T], F32, st)
                eps = sb("eps", [P, 1], F32, st)
                dve_steps, var_ready, std_ready = sem("dve_steps", st), sem("var_ready", st), sem("std_ready", st)
                coef_ready, h_ready, h_rest = sem("coef_ready", st), sem("h_ready", st), sem("h_rest", st)
                scaled, saved = sem("scaled", st), sem("saved", st)

                def flat(tile, t):
                    return tile[:, t, :].rearrange("p a f -> p (a f)")

                with nc.Block() as block:
                    @block.vector
                    def _(dve):
                        line = Line(dve, dve_steps)
                        line.link(nc.vector.memset(eps[:], LN_EPS))
                        for n in range(2):
                            a, b = n * HALF, (n + 1) * HALF
                            with dve.Fori(a // STEP, b // STEP) as i:
                                for j in range(STEP):
                                    t = bass.ds(i * STEP + j, 1)
                                    nc.vector.bn_stats(flat(stats, t), flat(x, t)).then_inc(stats_done, 1)
                            dve.wait_ge(stats_done, b)
                            r, m, v = rstd[:, a:b], shift[:, a:b], half[:, a:b]
                            line.mark(nc.vector.tensor_tensor(m, stats[:, a:b, 1], stats[:, a:b, 4], ALU.add))
                            line.mark(nc.vector.tensor_tensor(v, stats[:, a:b, 2], stats[:, a:b, 5], ALU.add))
                            line.link(nc.vector.tensor_tensor(r, stats[:, a:b, 1], stats[:, a:b, 4], ALU.subtract))
                            line.link(nc.vector.scalar_tensor_tensor(out=r, in0=r, scalar=0.25, in1=r, op0=ALU.mult, op1=ALU.mult))
                            nc.vector.scalar_tensor_tensor(out=r, in0=v, scalar=1.0 / D, in1=r,
                                                           op0=ALU.mult, op1=ALU.add).then_inc(var_ready, 1)
                            dve.wait_ge(std_ready, n + 1)
                            line.link(nc.vector.reciprocal(r, r))
                            nc.vector.scalar_tensor_tensor(out=m, in0=m, scalar=-0.5, in1=r,
                                                           op0=ALU.mult, op1=ALU.mult).then_inc(coef_ready, 1)
                        dve.wait_ge(coef_ready, 2)
                        for t in range(T - OWN, T):
                            ins = nc.vector.tensor_scalar(h[:, t, :], x[:, t, :], rstd[:, t:t + 1], shift[:, t:t + 1], ALU.mult, ALU.add)
                        ins.then_inc(scaled, 1)
                        dve.wait_ge(scaled, 1)
                        nc.vector.tensor_scalar(h[:, T - OWN:T, :], h[:, T - OWN:T, :], 0.0, None, ALU.max).then_inc(h_rest, 1)

                    @block.scalar
                    def _(act):
                        for n, end in ((0, HALF), (1, T - OWN)):
                            act.wait_ge(var_ready, n + 1)
                            act.activation(rstd[:, n * HALF:(n + 1) * HALF], rstd[:, n * HALF:(n + 1) * HALF],
                                           ACT.Sqrt, bias=eps[:, 0:1]).then_inc(std_ready, 1)
                            act.wait_ge(coef_ready, n + 1)
                            with act.Fori(n * HALF // STEP, end // STEP) as i:
                                for j in range(STEP):
                                    t = bass.ds(i * STEP + j, 1)
                                    act.activation(flat(h, t), flat(x, t), ACT.Relu, bias=shift[:, t], scale=rstd[:, t]).then_inc(h_ready, 1)

                    @block.sync
                    def _(sp):
                        if table is not None:
                            view = table.rearrange("(p t) f -> p t f", t=T)
                            sp.wait_ge(h_ready, HALF)
                            sp.dma_start(view[:, 0:HALF, :], h[:, 0:HALF, :]).then_inc(saved, 16)
                            sp.wait_ge(h_ready, T - OWN)
                            sp.wait_ge(h_rest, 1)
                            sp.dma_start(view[:, HALF:T, :], h[:, HALF:T, :]).then_inc(saved, 16)
                            sp.wait_ge(saved, 32)

        def layer1_own(st):
            PAIR = T // (TURNS - 1)
            assert PAIR * (TURNS - 1) == T
            w, left, left_t = (sb(k, [P, D], F32, st) for k in ("own_w", "own_left", "own_left_t"))
            bias, ones = sb("own_bias", [1, D], F32, st), sb("own_ones", [1, P], F32, st)
            own = sb("own", [P, T, D], F32, st)
            turn_ps, lin_ps = pb("own_turn_ps", [P, D], st), pb("own_lin_ps", [P, D], st)
            loaded, copied, turned, evacuated, multiplied, owned, ones_ready = (
                sem(f"own_{k}", st) for k in ("loaded", "copied", "turned", "evacuated", "multiplied", "owned", "ones_ready"))

            def begin_sp(sp):
                sp.dma_start(w[:], w1_in[0:D, :]).then_inc(loaded, 16)
                sp.dma_start(bias[:], b1_in.rearrange("(a f) -> a f", a=1)).then_inc(loaded, 16)
                sp.wait_ge(loaded, 32)

            def begin_dve():
                nc.vector.memset(ones[:], 1.0).then_inc(ones_ready, 1)

            def act_tiles(act, i):
                for s in range(PAIR):
                    k = i * PAIR + (s - PAIR)
                    act.activation(left[:].unsqueeze(1), h[:, bass.ds(k, 1), :], ACT.Copy).then_inc(copied, 1)
                    act.wait_ge(turned, k + 1)
                    act.activation(left_t[:], turn_ps[:], ACT.Copy).then_inc(evacuated, 1)
                    act.wait_ge(multiplied, k + 1)
                    act.sem_inc(act_gate, 1)
                    act.activation(own[:, bass.ds(k, 1), :], lin_ps[:].unsqueeze(1), ACT.Copy).then_inc(owned, 1)

            def pe(pe):
                pe.wait_ge(loaded, 32)
                pe.wait_ge(ones_ready, 1)

                def tile(k, begin):
                    pe.wait_ge(copied, k + 1)
                    nc.tensor.transpose(turn_ps[:], left[:], ident[:]).then_inc(turned, 1)
                    pe.wait_ge(evacuated, k + 1)
                    if not begin:
                        pe.wait_ge(owned, k)
                    nc.tensor.matmul(lin_ps[:], ones[:], bias[:], start=True, stop=False)
                    nc.tensor.matmul(lin_ps[:], left_t[:], w[:], start=False, stop=True).then_inc(multiplied, 1)
                tile(0, True)
                with pe.Fori(1, T) as k:
                    tile(k, False)

            def end_dve(dve):
                dve.wait_ge(owned, T)
                nc.vector.tensor_tensor(x[:], x[:], own[:], ALU.add)
            return {"sp": begin_sp, "begin_dve": begin_dve, "act": act_tiles, "pe": pe, "dve": end_dve}

        def gather_sum(name, table, sums_d, with_max, own_half=None):
            W = 2 * D if with_max else D
            ops = 2 if with_max else 1
            st = Stage(name)
            with st:
                idx_slot = sb("idx_slot", [P, NS, G], I32, st)
                rows = sb("rows", [P, NS, G, D], F32, st)
                sums = sb("sums", [P, NS, G, W], F32, st)
                idx_ready, summed, cleared = sem("idx_ready", st), sem("summed", st), sem("cleared", st)
                got, g0 = gathered, gathered_before(NS, C // NS)
                stored = [sem(f"stored{s}", st) for s in range(NS)]
                beside = own_half(st) if own_half else None
                with nc.Block() as block:
                    if beside:
                        @block.tensor
                        def _(pe):
                            beside["pe"](pe)

                    @block.gpsimd
                    def _(pool):
                        def turn(i, first):
                            for s in range(NS):
                                pool.wait_ge(idx_ready, i * NS + s + 1)
                                if not first:
                                    pool.wait_ge(summed, (i * NS + s + 1 - NS) * (G * ops))
                                pool.sem_inc(pool_gate, 1)
                                for j in range(G):
                                    nc.gpsimd.indirect_dma_start(
                                        out=rows[:, s, j, :], out_offset=None, in_=table,
                                        in_offset=bass.IndirectOffsetOnAxis(ap=idx_slot[:, s, j:j + 1], axis=0)
                                    ).then_inc(got[s], 16)
                        turn(0, True)
                        with pool.Fori(1, TURNS) as i:
                            turn(i, False)

                    @block.scalar
                    def _(act):
                        act.activation(idx_slot[:], src_i[:, 0:NS * G].rearrange("p (s g) -> p s g", s=NS),
                                       ACT.Copy).then_inc(idx_ready, NS)
                        with act.Fori(1, TURNS) as i:
                            for s in range(NS):
                                act.wait_ge(got[s], i * (16 * G) + g0[s])
                                act.sem_inc(act_gate, 1)
                                act.activation(idx_slot[:, s, :], src_i[:, bass.ds((i * NS + s) * G, G)],
                                               ACT.Copy).then_inc(idx_ready, 1)
                            if beside:
                                beside["act"](act, i)

                    @block.vector
                    def _(dve):
                        nc.vector.memset(sums[:, NS - 1, G - 1, :], 0.0).then_inc(cleared, 1)
                        if beside:
                            beside["begin_dve"]()
                        dve.wait_ge(cleared, 1)

                        def turn(i, first):
                            for s in range(NS):
                                dve.wait_ge(got[s], i * (16 * G) + (g0[s] + 16 * G))
                                if not first:
                                    dve.wait_ge(stored[s], i * 16)
                                for j in range(G):
                                    ps, pj = (s, j - 1) if j else ((s - 1) % NS, G - 1)
                                    for m in range(ops):
                                        k = (s * G + j) * ops + m
                                        if not (first and k < ops):
                                            dve.wait_ge(summed, i * (NS * G * ops) + (k - ops + 1))
                                        nc.vector.scalar_tensor_tensor(
                                            out=sums[:, s, j, m * D:m * D + D], in0=sums[:, ps, pj, m * D:m * D + D],
                                            scalar=cont[:, bass.ds((i * NS + s) * G + j, 1)], in1=rows[:, s, j, :],
                                            op0=ALU.mult, op1=(ALU.add, ALU.max)[m]).then_inc(summed, 1)
                        turn(0, True)
                        with dve.Fori(1, TURNS) as i:
                            turn(i, False)
                        dve.wait_ge(summed, C * ops)
                        nc.vector.tensor_copy(carry[:, 0:W], sums[:, NS - 1, G - 1, :])
                        if beside:
                            beside["dve"](dve)

                    @block.sync
                    def _(sp):
                        if beside:
                            beside["sp"](sp)
                        view = sums_d.rearrange("(p c) f -> p c f", c=C)
                        with sp.Fori(0, TURNS) as i:
                            for s in range(NS):
                                c0 = sp.snap((i * NS + s) * G)
                                sp.wait_ge(summed, (i * NS + s + 1) * (G * ops))
                                sp.sem_inc(sp_gate, 1)
                                sp.dma_start(view[:, bass.ds(c0, G), :], sums[:, s, :, :]).then_inc(stored[s], 16)
                        for s in range(NS):
                            sp.wait_ge(stored[s], 16 * TURNS)

        def chain_runs(name, parts):
            st = Stage(name)
            with st:
                turned = sb("turned", [P, P + 1], F32, st)
                last_t = pb("last_t", [P, P], st)
                back_t = pb("back_t", [P, P], st)
                dve_steps, turned_ready, pe_done = sem("dve_steps", st), sem("turned_ready", st), sem("pe_done", st)
                with nc.Block() as block:
                    @block.tensor
                    def _(pe):
                        for n, (a, w, _m) in enumerate(parts):
                            if n:
                                pe.wait_ge(turned_ready, 2 * n)
                            nc.tensor.transpose(last_t[0:w, :], carry[:, a:a + w], ident[:]).then_inc(pe_done, 1)
                            pe.wait_ge(turned_ready, 2 * n + 1)
                            nc.tensor.transpose(back_t[:, 0:w], turned[0:w, 0:P], ident[0:w, 0:w]).then_inc(pe_done, 1)

                    @block.vector
                    def _(dve):
                        for n, (a, w, is_max) in enumerate(parts):
                            if not n:
                                nc.vector.memset(turned[:, 0:1], 0.0).then_inc(dve_steps, 1)
                                dve.wait_ge(dve_steps, 1)
                            dve.wait_ge(pe_done, 2 * n + 1)
                            nc.vector.tensor_tensor_scan(turned[0:w, 1:P + 1], single_row[0:w, :], last_t[0:w, :], 0.0,
                                                         ALU.mult, ALU.max if is_max else ALU.add).then_inc(turned_ready, 1)
                            dve.wait_ge(pe_done, 2 * n + 2)
                            nc.vector.tensor_copy(carry[:, a:a + w], back_t[:, 0:w]).then_inc(turned_ready, 1)

        def node_totals(name, sums_d, W, WC, pre, per_early, per_late, scratch, consts, early, late, act_body=None, pe_body=None,
                        pe_start=None, act_end=None):
            per = per_early + per_late
            st = Stage(name)
            with st:
                idx_slot = sb("idx_slot", [P, 2, GN], I32, st)
                totals = sb("totals", [P, 2, GN, W], F32, st)
                pick = sb("pick", [P, 2, GN, P], F32, st)
                reach = pb("reach", [P, GN, D if WC == D else 2 * D], st)
                idx_ready, picked, reached, taken = sem("idx_ready", st), sem("picked", st), sem("reached", st), sem("taken", st)
                got, g0 = gathered, gathered_before(2, GN * NG // 2)
                dve_steps = sem("dve_steps", st)
                extra = scratch(st)
                extra["taken"] = taken
                with nc.Block() as block:
                    @block.gpsimd
                    def _(pool):
                        with pool.Fori(0, NG // 2) as i:
                            for s in range(2):
                                pool.wait_ge(idx_ready, i * 2 + s + 1)
                                pool.sem_inc(pool_gate, 1)
                                for j in range(GN):
                                    nc.gpsimd.indirect_dma_start(
                                        out=totals[:, s, j, :], out_offset=None, in_=sums_d,
                                        in_offset=bass.IndirectOffsetOnAxis(ap=idx_slot[:, s, j:j + 1], axis=0)
                                    ).then_inc(got[s], 16)

                    @block.sync
                    def _(sp):
                        consts(sp, extra)

                    @block.scalar
                    def _(act):
                        act.activation(idx_slot[:], end_i[:, 0:2 * GN].rearrange("p (s g) -> p s g", s=2),
                                       ACT.Copy).then_inc(idx_ready, 2)

                        def group(k, s, first):
                            if act_body:
                                act_body(act, k, s, first, extra)

                        group(0, 0, True)
                        with act.Fori(1, NG // 2) as i:
                            for s in range(2):
                                act.wait_ge(taken, i * 2 + s - 1)
                                act.sem_inc(act_gate, 1)
                                act.activation(idx_slot[:, s, :], end_i[:, bass.ds((i * 2 + s) * GN, GN)],
                                               ACT.Copy).then_inc(idx_ready, 1)
                                group(i * 2 + s - 1, 1 - s, False)
                        group(NG - 1, 1, False)
                        if act_end:
                            act_end(act, extra)

                    @block.tensor
                    def _(pe):
                        if pe_start:
                            pe_start(pe, extra)

                        def fetch(k, s, first):
                            pe.wait_ge(picked, k + 1)
                            if not first:
                                pe.wait_ge(taken, k)
                            for j in range(GN):
                                ins = nc.tensor.matmul(reach[:, j, 0:WC], pick[:, s, j, :], carry[:, 0:WC], start=True, stop=True)
                            ins.then_inc(reached, 1)

                        def group(k, s):
                            fetch(k + 1, 1 - s, False)
                            if pe_body:
                                pe_body(pe, k, s, extra)
                        fetch(0, 0, True)
                        for s in range(2):
                            group(s, s)
                        with pe.Fori(1, NG // 2) as i:
                            for s in range(2):
                                group(i * 2 + s, s)

                    @block.vector
                    def _(dve):
                        line = Line(dve, dve_steps)
                        if "prepare" in extra:
                            extra["prepare"](dve, line)
                        assert line.n == pre

                        def choose(k, s):
                            nc.vector.tensor_scalar(pick[:, s, :, :], run_rows[:, bass.ds(k * GN, GN), :], lane[:, 0:1], None,
                                                    ALU.is_equal).then_inc(picked, 1)

                        def group(i, s, first):
                            k = i * 2 + s
                            dve.wait_ge(got[s], i * (16 * GN) + (g0[s] + 16 * GN))
                            dve.wait_ge(reached, k + 1)
                            line.n = pre if first else k * per + (pre - per_late)
                            early(dve, line, k, s, totals[:, s, :, :], reach, extra)
                            choose(k + 1, 1 - s)
                            if not first:
                                late(dve, line, k - 1, 1 - s, extra)
                        choose(0, 0)
                        for s in range(2):
                            group(0, s, s == 0)
                        with dve.Fori(1, NG // 2) as i:
                            for s in range(2):
                                group(i, s, False)
                        line.n = NG * per + (pre - per_late)
                        late(dve, line, NG - 1, 1, extra)

        def linear_scratch(st, e):
            e["left"] = sb("left", [P, 2, GN, D], F32, st)
            e["left_t"] = sb("left_t", [P, GN, D], F32, st)
            e["w"] = sb("w", [P, D], F32, st)
            e["turn_ps"] = pb("turn_ps", [P, GN, D], st)
            e["lin_ps"] = pb("lin_ps", [P, GN, D], st)
            for k in ("left_ready", "turned", "evacuated", "multiplied", "lin_taken", "loaded"):
                e[k] = sem(k, st)

        def linear_act(act, k, s, first, e):
            act.wait_ge(e["turned"], k + 1)
            if not first:
                act.wait_ge(e["multiplied"], k)
            act.activation(e["left_t"][:], e["turn_ps"][:], ACT.Copy).then_inc(e["evacuated"], 1)

        def linear_pe(pe, k, s, e):
            pe.wait_ge(e["left_ready"], k + 1)
            for j in range(GN):
                ins = nc.tensor.transpose(e["turn_ps"][:, j, :], e["left"][:, s, j, :], ident[:])
            ins.then_inc(e["turned"], 1)
            pe.wait_ge(e["evacuated"], k + 1)
            if not isinstance(k, int) or k:
                pe.wait_ge(e["lin_taken"], k)
            for j in range(GN):
                ins = nc.tensor.matmul(e["lin_ps"][:, j, :], e["left_t"][:, j, :], e["w"][:], start=True, stop=True)
            ins.then_inc(e["multiplied"], 1)

        def layer0_nodes():
            def scratch(st):
                e = {k: sb(k, [P, T], F32, st) for k in ("sum_w", "max_w")}
                e["z"] = sb("z", [P, 3], F32, st)
                e["a"] = sb("part_a", [P, 2, GN, D], F32, st)
                e["b"] = sb("part_b", [P, 2, GN, D], F32, st)
                e["loaded"] = sem("loaded", st)

                def prepare(dve, line):
                    z = e["z"]
                    dve.wait_ge(e["loaded"], 16)
                    line.link(nc.vector.tensor_scalar(e["sum_w"][:], rdeg[:], z[:, 1:2], z[:, 0:1], ALU.mult, ALU.add))
                    line.link(nc.vector.tensor_tensor(e["sum_w"][:], e["sum_w"][:], has[:], ALU.mult))
                    line.link(nc.vector.tensor_scalar(e["max_w"][:], has[:], z[:, 2:3], None, ALU.mult))
                e["prepare"] = prepare
                return e

            def consts(sp, e):
                sp.dma_start(e["z"][:], z_in.to_broadcast([P, 3])).then_inc(e["loaded"], 16)
                sp.wait_ge(e["loaded"], 16)

            def early(dve, line, k, s, total, reach, e):
                line.mark(nc.vector.tensor_tensor(e["a"][:, s, :, :], total[:, :, 0:D], reach[:, :, 0:D], ALU.add))
                nc.vector.tensor_tensor(e["b"][:, s, :, :], total[:, :, D:2 * D], reach[:, :, D:2 * D], ALU.max).then_inc(e["taken"], 1)

            def late(dve, line, k, s, e):
                tiles = bass.ds(k * GN, GN)
                a, b = e["a"][:, s, :, :], e["b"][:, s, :, :]
                dve.wait_ge(e["taken"], k + 1)
                line.mark(nc.vector.tensor_tensor(a, a, e["sum_w"][:, tiles].unsqueeze(2).to_broadcast([P, GN, D]), ALU.mult))
                line.link(nc.vector.tensor_tensor(b, b, e["max_w"][:, tiles].unsqueeze(2).to_broadcast([P, GN, D]), ALU.mult))
                line.link(nc.vector.tensor_tensor(a, a, b, ALU.add))
                line.link(nc.vector.tensor_tensor(x[:, tiles, :], x[:, tiles, :], a, ALU.add))

            node_totals("nodes0", s0_d, 2 * D, 2 * D, 3, 1, 4, scratch, consts, early, late)

        def layer1_nodes():
            def scratch(st):
                e = {}
                linear_scratch(st, e)
                e["mean_w"] = sb("mean_w", [P, T], F32, st)

                def prepare(dve, line):
                    line.link(nc.vector.tensor_tensor(e["mean_w"][:], rdeg[:], has[:], ALU.mult))
                e["prepare"] = prepare
                return e

            def consts(sp, e):
                sp.dma_start(e["w"][:], w1_in[D:2 * D, :]).then_inc(e["loaded"], 16)
                sp.wait_ge(e["loaded"], 16)

            def early(dve, line, k, s, total, reach, e):
                m = e["left"][:, s, :, :]
                nc.vector.tensor_tensor(m, total[:, :, 0:D], reach[:], ALU.add).then_inc(e["taken"], 1)
                dve.wait_ge(e["taken"], k + 1)
                nc.vector.tensor_tensor(m, m, e["mean_w"][:, bass.ds(k * GN, GN)].unsqueeze(2).to_broadcast([P, GN, D]),
                                        ALU.mult).then_inc(e["left_ready"], 1)

            def late(dve, line, k, s, e):
                tiles = bass.ds(k * GN, GN)
                dve.wait_ge(e["multiplied"], k + 1)
                nc.vector.tensor_tensor(x[:, tiles, :], x[:, tiles, :], e["lin_ps"][:], ALU.add).then_inc(e["lin_taken"], 1)

            def pe_start(pe, e):
                pe.wait_ge(e["loaded"], 16)

            node_totals("nodes1", s1_d, D, D, 1, 0, 0, scratch, consts, early, late, linear_act, linear_pe, pe_start)

        def relation_tables():
            BANK = 512
            KV = R * 2 * D
            st = Stage("tables2")
            with st:
                w = sb("w", [P, KV + R * D], F32, st)
                left = sb("left", [P, 2, D], F32, st)
                left_t = sb("left_t", [P, 2, D], F32, st)
                kv_slot = sb("kv_slot", [P, 2, KV], F32, st)
                q_slot = sb("q_slot", [P, 2, R, D + K2], F32, st)
                bias = sb("bias", [P, R, K2], F32, st)
                turn_ps = pb("turn_ps", [P, BANK], st)
                out_ps = pb("out_ps", [P, 4, BANK], st)
                loaded, copied, turned, evacuated = sem("loaded", st), sem("copied", st), sem("turned", st), sem("evacuated", st)
                multiplied, dve_out, act_out = sem("multiplied", st), sem("dve_out", st), sem("act_out", st)
                bias_in_place = sem("bias_in_place", st)
                saved = [sem(f"saved{s}", st) for s in range(2)]
                with nc.Block() as block:
                    @block.sync
                    def _(sp):
                        for r in range(R):
                            for a, src in ((r * 2 * D, wk_in), (r * 2 * D + D, wv_in), (KV + r * D, wq_in)):
                                sp.dma_start(w[:, a:a + D].rearrange("h (k d) -> h k d", k=K2),
                                             src[r].rearrange("k h d -> h k d")).then_inc(loaded, 16)
                        sp.dma_start(bias[:].rearrange("p r k -> p (r k)"),
                                     bias_in.rearrange("(a r) k -> a (r k)", a=1).to_broadcast([P, R * K2])).then_inc(loaded, 16)
                        kv_v = kv_d.rearrange("(p t r) w -> p t (r w)", t=T, r=R)
                        q_v = q_d.rearrange("(p t r) w -> p t (r w)", t=T, r=R)
                        with sp.Fori(0, T // 2) as i:
                            for s in range(2):
                                t = sp.snap(i * 2 + s)
                                sp.wait_ge(dve_out, i * 2 + s + 1)
                                sp.sem_inc(sp_gate, 1)
                                sp.wait_ge(act_out, i * 2 + s + 1)
                                sp.sem_inc(sp_gate, 1)
                                sp.dma_start(kv_v[:, bass.ds(t, 1), :], kv_slot[:, s:s + 1, :]).then_inc(saved[s], 16)
                                sp.dma_start(q_v[:, bass.ds(t, 1), :],
                                             q_slot[:, s:s + 1, :, :].rearrange("p a r w -> p a (r w)")).then_inc(saved[s], 16)
                        for s in range(2):
                            sp.wait_ge(saved[s], 32 * (T // 2))

                    @block.scalar
                    def _(act):
                        def prepare(k, s):
                            act.activation(left[:, s:s + 1, :], h[:, bass.ds(k, 1), :], ACT.Copy).then_inc(copied, 1)
                            act.wait_ge(turned, k + 1)
                            act.activation(left_t[:, s, :], turn_ps[:, 0:D], ACT.Copy).then_inc(evacuated, 1)

                        def take(i, s, first):
                            k = i * 2 + s
                            if not first:
                                act.wait_ge(saved[s], i * 32)
                            act.wait_ge(multiplied, k * 4 + 3)
                            act.activation(kv_slot[:, s, 2 * BANK:KV], out_ps[:, 2, 0:256], ACT.Copy)
                            act.activation(q_slot[:, s, 0:2, 0:D], out_ps[:, 2, 256:512].rearrange("p (r f) -> p r f", r=2), ACT.Copy)
                            act.wait_ge(multiplied, k * 4 + 4)
                            act.activation(q_slot[:, s, 2:5, 0:D], out_ps[:, 3, 0:384].rearrange("p (r f) -> p r f", r=3),
                                           ACT.Copy).then_inc(act_out, 1)

                        def turn(i, first, last):
                            for s in range(2):
                                if not (last and s):
                                    prepare(i * 2 + s + 1, 1 - s)
                                take(i, s, first)
                        prepare(0, 0)
                        turn(0, True, False)
                        with act.Fori(1, T // 2 - 1) as i:
                            turn(i, False, False)
                        turn(T // 2 - 1, False, True)

                    @block.tensor
                    def _(pe):
                        pe.wait_ge(loaded, 16 * (3 * R + 1))

                        def transpose(k, s, first):
                            pe.wait_ge(copied, k + 1)
                            if not first:
                                pe.wait_ge(evacuated, k)
                            nc.tensor.transpose(turn_ps[:, 0:D], left[:, s, :], ident[:]).then_inc(turned, 1)

                        def multiply(k, s, first):
                            for b in range(4):
                                if b == 0 and not first:
                                    pe.wait_ge(dve_out, k)
                                if b == 2 and not first:
                                    pe.wait_ge(act_out, k)
                                cols = min(BANK, KV + R * D - b * BANK)
                                nc.tensor.matmul(out_ps[:, b, 0:cols], left_t[:, s, :], w[:, b * BANK:b * BANK + cols],
                                                 start=True, stop=True).then_inc(multiplied, 1)
                        transpose(0, 0, True)

                        def turn(i, first, last):
                            for s in range(2):
                                k = i * 2 + s
                                if last and s:
                                    pe.wait_ge(evacuated, k + 1)
                                else:
                                    transpose(k + 1, 1 - s, False)
                                multiply(k, s, first and s == 0)
                        turn(0, True, False)
                        with pe.Fori(1, T // 2 - 1) as i:
                            turn(i, False, False)
                        turn(T // 2 - 1, False, True)

                    @block.vector
                    def _(dve):
                        dve.wait_ge(loaded, 16 * (3 * R + 1))
                        for s in range(2):
                            nc.vector.tensor_copy(q_slot[:, s, :, D:D + K2], bias[:]).then_inc(bias_in_place, 1)
                        dve.wait_ge(bias_in_place, 2)

                        def tile(i, s, first):
                            k = i * 2 + s
                            if not first:
                                dve.wait_ge(saved[s], i * 32)
                            dve.wait_ge(multiplied, k * 4 + 2)
                            nc.vector.tensor_copy(kv_slot[:, s, 0:2 * BANK], out_ps[:, 0:2, :].rearrange("p b f -> p (b f)")).then_inc(dve_out, 1)
                        for s in range(2):
                            tile(0, s, True)
                        with dve.Fori(1, T // 2) as i:
                            for s in range(2):
                                tile(i, s, False)

        def relation_logits(logits):
            st = Stage("logits2")
            with st:
                kv_idx = sb("kv_idx", [P, NS, G], I32, st)
                q_idx = sb("q_idx", [P, NS, G], I32, st)
                kv_rows = sb("kv_rows", [P, NS, G, 2 * D], F32, st)
                q_rows = sb("q_rows", [P, NS, G, D + K2], F32, st)
                prod = sb("prod", [P, 2, G, D], F32, st)
                dots = sb("dots", [P, 2, G, K2], F32, st)
                idx_ready, multiplied, reduced, scored = (sem("idx_ready", st), sem("multiplied", st), sem("reduced", st),
                                                          sem("scored", st))
                got, g0 = gathered, gathered_before(NS, 2 * C // NS)
                stored = [sem(f"stored{s}", st) for s in range(NS)]
                with nc.Block() as block:
                    @block.gpsimd
                    def _(pool):
                        def turn(i, first):
                            for s in range(NS):
                                pool.wait_ge(idx_ready, i * NS + s + 1)
                                if not first:
                                    pool.wait_ge(scored, i * NS + s + 1 - NS)
                                    pool.sem_inc(pool_gate, 1)
                                    pool.wait_ge(stored[s], i * 16)
                                pool.sem_inc(pool_gate, 1)
                                for j in range(G):
                                    nc.gpsimd.indirect_dma_start(
                                        out=kv_rows[:, s, j, :], out_offset=None, in_=kv_d,
                                        in_offset=bass.IndirectOffsetOnAxis(ap=kv_idx[:, s, j:j + 1], axis=0)).then_inc(got[s], 16)
                                    nc.gpsimd.indirect_dma_start(
                                        out=q_rows[:, s, j, :], out_offset=None, in_=q_d,
                                        in_offset=bass.IndirectOffsetOnAxis(ap=q_idx[:, s, j:j + 1], axis=0)).then_inc(got[s], 16)
                        turn(0, True)
                        with pool.Fori(1, TURNS) as i:
                            turn(i, False)

                    @block.scalar
                    def _(act):
                        act.activation(kv_idx[:], kv_i[:, 0:NS * G].rearrange("p (s g) -> p s g", s=NS), ACT.Copy)
                        act.activation(q_idx[:], q_i[:, 0:NS * G].rearrange("p (s g) -> p s g", s=NS), ACT.Copy).then_inc(idx_ready, NS)
                        with act.Fori(1, TURNS) as i:
                            for s in range(NS):
                                act.wait_ge(got[s], i * (32 * G) + g0[s])
                                act.sem_inc(act_gate, 1)
                                cols = bass.ds((i * NS + s) * G, G)
                                act.activation(kv_idx[:, s, :], kv_i[:, cols], ACT.Copy)
                                act.activation(q_idx[:, s, :], q_i[:, cols], ACT.Copy).then_inc(idx_ready, 1)

                    @block.vector
                    def _(dve):
                        with dve.Fori(0, TURNS) as i:
                            for s in range(NS):
                                k = i * NS + s
                                dve.wait_ge(got[s], i * (32 * G) + (g0[s] + 32 * G))
                                nc.vector.tensor_tensor(prod[:, s % 2, :, :], kv_rows[:, s, :, 0:D], q_rows[:, s, :, 0:D],
                                                        ALU.mult).then_inc(multiplied, 1)
                                dve.wait_ge(multiplied, k + 1)
                                nc.vector.tensor_reduce(dots[:, s % 2, :, :].rearrange("p j k -> p (j k)"),
                                                        prod[:, s % 2, :, :].rearrange("p j (k d) -> p (j k) d", k=K2),
                                                        AX.X, ALU.add).then_inc(reduced, 1)
                                dve.wait_ge(reduced, k + 1)
                                nc.vector.scalar_tensor_tensor(
                                    out=logits[:, :, bass.ds(k * G, G)].rearrange("p k j -> p j k"), in0=dots[:, s % 2, :, :],
                                    scalar=1.0 / float(D2) ** 0.5, in1=q_rows[:, s, :, D:D + K2], op0=ALU.mult,
                                    op1=ALU.add).then_inc(scored, 1)

                    @block.sync
                    def _(sp):
                        view = v_d.rearrange("(p c) f -> p c f", c=C)
                        with sp.Fori(0, TURNS) as i:
                            for s in range(NS):
                                c0 = sp.snap((i * NS + s) * G)
                                sp.wait_ge(got[s], i * (32 * G) + (g0[s] + 32 * G))
                                sp.sem_inc(sp_gate, 1)
                                sp.dma_start(view[:, bass.ds(c0, G), :], kv_rows[:, s, :, D:2 * D]).then_inc(stored[s], 16)
                        for s in range(NS):
                            sp.wait_ge(stored[s], 16 * TURNS)

        def relation_softmax(logits, weights):
            n = K2
            st = Stage("softmax2")
            with st:
                lanes = sb("lanes", [P, n, C], F32, st)
                stay = sb("stay", [P, C + 1], F32, st)
                pen_first = sb("pen_first", [P, C], F32, st)
                pen_last = sb("pen_last", [P, C], F32, st)
                pen_single = sb("pen_single", [P, P], F32, st)
                pen_link = sb("pen_link", [P, P], F32, st)
                ends = sb("ends", [P, 2, n], F32, st)
                left = sb("left", [n, P + 1], F32, st)
                right = sb("right", [n, P + 1], F32, st)
                reach = sb("reach", [P, 2, n], F32, st)
                mask = sb("mask", [P, C], F32, st)
                rel = sb("rel", [P, 2], F32, st)
                own = pb("own", [P, C], st)
                ends_ps = pb("ends_ps", [P, 2, P], st)
                reach_ps = pb("reach_ps", [P, 2, n], st)
                dve_steps, pool_steps, masked, merged = (sem("dve_steps", st), sem("pool_steps", st), sem("masked", st),
                                                         sem("merged", st))
                dve_turns, pe_turns = sem("dve_turns", st), sem("pe_turns", st)
                shifted, exped = sem("shifted", st), sem("exped", st)

                with nc.Block() as block:
                    @block.gpsimd
                    def _(pool):
                        line = Line(pool, pool_steps)
                        for phase, op in enumerate((ALU.add, ALU.mult)):
                            line.link(nc.gpsimd.memset(rel[:, 0:1], -1.0))
                            base, per = line.n, 2 + (phase == 0)
                            with pool.Fori(0, R) as r:
                                line.n = r * per + base
                                pool.wait_ge(masked, (r + phase * R) * n + 1)
                                pool.sem_inc(pool_gate, 1)
                                line.link(nc.gpsimd.tensor_scalar(rel[:, 0:1], rel[:, 0:1], 1.0, None, ALU.add))
                                pool.sem_inc(pool_gate, 1)
                                line.link(nc.gpsimd.tensor_scalar(mask[:], type_f[:], rel[:, 0:1], 1.0 if phase else -LOW,
                                                                  ALU.is_equal, ALU.mult))
                                pool.sem_inc(pool_gate, 1)
                                if not phase:
                                    line.link(nc.gpsimd.tensor_scalar(mask[:], mask[:], LOW, None, ALU.add))
                                    pool.sem_inc(pool_gate, 1)
                                for k in range(n):
                                    if phase:
                                        pool.wait_ge(exped, k + 1)
                                    pool.wait_ge(merged, (r + phase * R) * n + (k + 1))
                                    pool.sem_inc(pool_gate, 1)
                                    nc.gpsimd.tensor_tensor(lanes[:, k, :], logits[:, k, :], mask[:], op).then_inc(masked, 1)
                            line.n = base + R * per

                    @block.tensor
                    def _(pe):
                        with pe.Fori(0, 2 * R) as i:
                            pe.wait_ge(dve_turns, i * 2 + 1)
                            nc.tensor.transpose(ends_ps[0:n, 0, :], ends[:, 0, :], ident[:])
                            nc.tensor.transpose(ends_ps[0:n, 1, :], ends[:, 1, :], ident[:]).then_inc(pe_turns, 1)
                            pe.wait_ge(dve_turns, i * 2 + 2)
                            pe.sem_inc(pe_gate, 1)
                            nc.tensor.transpose(reach_ps[:, 0, 0:n], left[0:n, 0:P], ident[0:n, 0:n])
                            nc.tensor.transpose(reach_ps[:, 1, 0:n], right[0:n, 1:P + 1], ident[0:n, 0:n]).then_inc(pe_turns, 1)

                    @block.scalar
                    def _(act):
                        for k in range(n):
                            act.wait_ge(shifted, k + 1)
                            act.activation(logits[:, k, :], logits[:, k, :], ACT.Exp, scale=-1.0).then_inc(exped, 1)

                    @block.vector
                    def _(dve):
                        line = Line(dve, dve_steps)
                        for tile, m in ((stay[:, 0:C], cont), (pen_first[:], in_first), (pen_last[:], in_last),
                                        (pen_single[:], single_row), (pen_link[:], link_row)):
                            line.mark(nc.vector.tensor_scalar(tile, m[:], -1.0, -LOW, ALU.add, ALU.mult))
                        line.mark(nc.vector.memset(stay[:, C:C + 1], LOW))
                        line.link(nc.vector.memset(weights[:], 0.0))
                        nc.vector.memset(own[:], 0.0).then_inc(merged, n)
                        dve.wait_ge(merged, n)
                        nc.vector.memset(lanes[:, 0, 0:1], 0.0).then_inc(masked, 1)
                        for phase in range(2):
                            is_max = phase == 0
                            least = LOW if is_max else 0.0
                            hold, op = (stay[:, 0:C], ALU.max) if is_max else (cont[:], ALU.add)
                            keep = ALU.add if is_max else ALU.mult
                            first, last = (pen_first, pen_last) if is_max else (in_first, in_last)
                            single, link = (pen_single, pen_link) if is_max else (single_row, link_row)
                            line.link(nc.vector.memset(rel[:, 1:2], -1.0))
                            base, per = line.n, 2 + 2 * n + 5 + 2 * n
                            with dve.Fori(0, R) as r:
                                line.n = r * per + base
                                line.link(nc.vector.tensor_scalar(rel[:, 1:2], rel[:, 1:2], 1.0, None, ALU.add))
                                line.mark(nc.vector.tensor_scalar(own[:], type_f[:], rel[:, 1:2], None, ALU.is_equal))
                                for k in range(n):
                                    dve.wait_ge(masked, (r + phase * R) * n + (k + 2))
                                    line.mark(nc.vector.tensor_tensor_scan(lanes[:, k, :], hold, lanes[:, k, :], least, keep, op))
                                dve.wait_ge(line.sem, line.n)
                                line.link(nc.vector.tensor_copy(ends[:, 0, :], lanes[:, :, C - 1]))
                                for k in range(n):
                                    line.mark(nc.vector.tensor_tensor_scan(lanes[:, k, ::-1], stay[:, 1:C + 1][:, ::-1],
                                                                           lanes[:, k, ::-1], least, ALU.add, ALU.max))
                                dve.wait_ge(line.sem, line.n)
                                nc.vector.tensor_copy(ends[:, 1, :], lanes[:, :, 0]).then_inc(dve_turns, 1)
                                line.mark(nc.vector.memset(left[:, 0:1], least))
                                line.link(nc.vector.memset(right[:, P:P + 1], least))
                                dve.wait_ge(pe_turns, (r + phase * R) * 2 + 1)
                                line.link(nc.vector.tensor_tensor_scan(left[0:n, 1:P + 1], single[0:n, :], ends_ps[0:n, 0, :],
                                                                       least, keep, op))
                                nc.vector.tensor_tensor_scan(right[0:n, 0:P][:, ::-1], link[0:n, ::-1], ends_ps[0:n, 1, ::-1],
                                                             least, keep, op).then_inc(dve_turns, 1)
                                dve.wait_ge(pe_turns, (r + phase * R) * 2 + 2)
                                line.link(nc.vector.tensor_copy(reach[:], reach_ps[:, :, 0:n]))
                                done = {}
                                for m in range(n + 2):
                                    if m >= 2:
                                        dve.wait_ge(line.sem, done[1, m - 2])
                                        if m > n:
                                            dve.sem_inc(dve_gate, 1)
                                    for side, edge, k in ((0, first, m), (1, last, m - 1)):
                                        if 0 <= k < n:
                                            if side:
                                                dve.wait_ge(line.sem, done[0, k])
                                            done[side, k] = line.mark(nc.vector.scalar_tensor_tensor(
                                                out=lanes[:, k, :], in0=edge[:], scalar=reach[:, side, k:k + 1],
                                                in1=lanes[:, k, :], op0=keep, op1=op))
                                    if m >= 2:
                                        k = m - 2
                                        nc.vector.copy_predicated(weights[:, k, :], own[:].bitcast(I32), lanes[:, k, :]).then_inc(merged, 1)
                                dve.wait_ge(merged, (r + phase * R) * n + 2 * n)
                            line.n = base + R * per
                            for k in range(n if is_max else 0):
                                nc.vector.scalar_tensor_tensor(out=logits[:, k, :], in0=weights[:, k, :], scalar=NEG, in1=logits[:, k, :],
                                                               op0=ALU.max, op1=ALU.subtract).then_inc(shifted, 1)
                        line.link(nc.vector.tensor_scalar(weights[:], weights[:], 1e-12, None, ALU.add))
                        line.link(nc.vector.reciprocal(weights[:], weights[:]))
                        line.link(nc.vector.tensor_tensor(weights[:], weights[:], logits[:], ALU.mult))

        def weighted_sum(name, rows_d, sums_d, weights, heads):
            BL, NR, NL = C // 32, 3, 2
            BLOCKS = C // BL
            PER = NR * NL
            turns, rest = BLOCKS // PER, BLOCKS % PER
            SPLIT = 5
            st = Stage(name)
            with st:
                rows = sb("rows", [P, NR, BL, D], F32, st)
                lanes = sb("lanes", [P, NL, D, BL], F32, st)
                factor = sb("factor", [P, NL, D, BL], F32, st)
                cleared, multiplied, joined, begun, summed, turned, staged = (
                    sem(k, st) for k in ("cleared", "multiplied", "joined", "begun", "summed", "turned", "staged"))
                got = [sem(f"got{r}", st) for r in range(NR)]
                stored = [sem(f"stored{r}", st) for r in range(NR)]

                def blocks(engine, block, peel):
                    for j in range(PER if peel else 0):
                        block(j, j, j // NR)
                    with engine.Fori(1 if peel else 0, turns) as i:
                        for j in range(PER):
                            block(i * PER + j, j, i * NL + j // NR)
                    for j in range(rest):
                        block(turns * PER + j, j, turns * NL + j // NR)

                def times_weights(engine, k, r, l, a, b):
                    f = slice(a * (D // heads), b * (D // heads))
                    w = weights[:, a:b, bass.ds(k * BL, BL)]
                    return engine.tensor_tensor(
                        lanes[:, l, f, :].rearrange("p (k d) j -> p k d j", k=b - a),
                        rows[:, r, :, f].rearrange("p j (k d) -> p k d j", k=b - a),
                        w.unsqueeze(2).to_broadcast([P, b - a, D // heads, BL]), ALU.mult)

                with nc.Block() as block:
                    @block.sync
                    def _(sp):
                        view = rows_d.rearrange("(p c) f -> p c f", c=C)

                        def load(k, j, uses):
                            r = j % NR
                            peeled = isinstance(k, int)
                            c0 = k * BL if peeled else sp.snap(k * BL)
                            if not (peeled and k < NR):
                                sp.wait_ge(stored[r], uses * 16)
                                sp.sem_inc(sp_gate, 1)
                            sp.dma_start(rows[:, r, :, :], view[:, bass.ds(c0, BL), :]).then_inc(got[r], 16)
                        blocks(sp, load, True)

                    @block.gpsimd
                    def _(pool):
                        pool.wait_ge(cleared, 1)

                        def multiply(k, j, uses):
                            r, l = j % NR, j % NL
                            peeled = isinstance(k, int)
                            pool.wait_ge(got[r], uses * 16 + 16)
                            pool.sem_inc(pool_gate, 1)
                            if not (peeled and k < 2):
                                pool.wait_ge(turned, k - 1)
                                pool.sem_inc(pool_gate, 1)
                            if not (peeled and k < 1):
                                pool.wait_ge(begun, k)
                                pool.sem_inc(pool_gate, 1)
                            times_weights(nc.gpsimd, k, r, l, SPLIT, heads).then_inc(joined, 1)
                        blocks(pool, multiply, True)

                    @block.vector
                    def _(dve):
                        nc.vector.memset(lanes[:, NL - 1, :, BL - 1:BL], 0.0)
                        nc.vector.memset(factor[:, :, :, 0:1], 0.0).then_inc(cleared, 1)
                        dve.wait_ge(cleared, 1)

                        def recur(k, j, uses):
                            r, l = j % NR, j % NL
                            dve.wait_ge(got[r], uses * 16 + 16)
                            if not (isinstance(k, int) and k < 2):
                                dve.wait_ge(turned, k - 1)
                            times_weights(nc.vector, k, r, l, 0, SPLIT).then_inc(multiplied, 1)
                            dve.wait_ge(multiplied, k + 1)
                            dve.wait_ge(joined, k + 1)
                            nc.vector.scalar_tensor_tensor(
                                out=lanes[:, l, :, 0], in0=lanes[:, 1 - l, :, BL - 1], scalar=cont[:, bass.ds(k * BL, 1)],
                                in1=lanes[:, l, :, 0], op0=ALU.mult, op1=ALU.add).then_inc(begun, 1)
                            dve.wait_ge(begun, k + 1)
                            dve.wait_ge(staged, k + 1)
                            flat = lanes[:, l, :, :].rearrange("p f j -> p (f j)")
                            nc.vector.tensor_tensor_scan(flat, factor[:, l, :, :].rearrange("p f j -> p (f j)"), flat, 0.0,
                                                         ALU.mult, ALU.add).then_inc(summed, 1)
                            dve.wait_ge(summed, k + 1)
                        blocks(dve, recur, True)
                        nc.vector.tensor_copy(carry[:, 0:D], lanes[:, (BLOCKS - 1) % NL, :, BL - 1])

                    @block.scalar
                    def _(act):
                        view = sums_d.rearrange("(p c) f -> p c f", c=C)
                        act.wait_ge(cleared, 1)

                        def stage(k, l):
                            act.activation(factor[:, l, :, 1:BL], cont[:, bass.ds(k * BL + 1, BL - 1)].unsqueeze(1)
                                           .to_broadcast([P, D, BL - 1]), ACT.Copy).then_inc(staged, 1)

                        def turn_back(k, j, uses):
                            r, l = j % NR, j % NL
                            act.wait_ge(summed, k + 1)
                            act.activation(rows[:, r, :, :], lanes[:, l, :, :].rearrange("p f j -> p j f"), ACT.Copy).then_inc(turned, 1)
                            if not isinstance(k, int) or k + NL < BLOCKS:
                                stage(k + NL, l)
                            act.wait_ge(turned, k + 1)
                            act.dma_start(view[:, bass.ds(k * BL, BL), :], rows[:, r, :, :]).then_inc(stored[r], 16)
                        for l in range(NL):
                            stage(l, l)
                        blocks(act, turn_back, False)
                        for r in range(NR):
                            act.wait_ge(stored[r], 16 * len(range(r, BLOCKS, NR)))

        def layer2_nodes():
            def scratch(st):
                e = {}
                linear_scratch(st, e)
                for k in ("bias", "gamma", "beta", "wo"):
                    e[k] = sb(k, [P, D], F32, st)
                e["stats"] = sb("stats", [P, GN, 6], F32, st)
                for k in ("mean", "dev", "std"):
                    e[k] = sb(k, [P, GN], F32, st)
                e["eps"] = sb("eps", [P, 1], F32, st)
                for k in ("w_turned", "w_ready", "var_ready", "std_ready"):
                    e[k] = sem(k, st)

                def prepare(dve, line):
                    line.link(nc.vector.memset(e["eps"][:], LN_EPS))
                    dve.wait_ge(e["w_turned"], 1)
                    nc.vector.tensor_copy(e["w"][:], e["lin_ps"][:, 0, :]).then_inc(e["w_ready"], 1)
                e["prepare"] = prepare
                return e

            def consts(sp, e):
                sp.dma_start(e["wo"][:], ow_in).then_inc(e["loaded"], 16)
                for k, src in (("bias", ob_in), ("gamma", lng_in), ("beta", lnb_in)):
                    sp.dma_start(e[k][:], src.rearrange("(a f) -> a f", a=1).to_broadcast([P, D])).then_inc(e["loaded"], 16)
                sp.wait_ge(e["loaded"], 64)

            def early(dve, line, k, s, total, reach, e):
                m = e["left"][:, s, :, :]
                nc.vector.tensor_tensor(m, total[:, :, 0:D], reach[:], ALU.add).then_inc(e["taken"], 1)
                dve.wait_ge(e["taken"], k + 1)
                nc.vector.tensor_tensor(m, m, has[:, bass.ds(k * GN, GN)].unsqueeze(2).to_broadcast([P, GN, D]),
                                        ALU.mult).then_inc(e["left_ready"], 1)

            def late(dve, line, k, s, e):
                tiles = bass.ds(k * GN, GN)
                m = e["left"][:, s, :, :]

                def tiled(ap):
                    return ap.unsqueeze(2).to_broadcast([P, GN, D])

                def rowed(ap):
                    return ap.unsqueeze(1).to_broadcast([P, GN, D])

                dve.wait_ge(e["multiplied"], k + 1)
                nc.vector.tensor_tensor(m, e["lin_ps"][:], rowed(e["bias"][:]), ALU.add).then_inc(e["lin_taken"], 1)
                dve.wait_ge(e["lin_taken"], k + 1)
                line.link(nc.vector.tensor_tensor(m, m, h[:, tiles, :], ALU.add))
                for j in range(GN):
                    line.mark(nc.vector.bn_stats(e["stats"][:, j, :], e["left"][:, s, j, :]))
                dve.wait_ge(line.sem, line.n)
                stats = e["stats"]
                line.link(nc.vector.tensor_tensor(e["mean"][:], stats[:, :, 1], stats[:, :, 4], ALU.add))
                line.link(nc.vector.tensor_scalar(e["mean"][:], e["mean"][:], 0.5, None, ALU.mult))
                line.link(nc.vector.tensor_tensor(e["dev"][:], stats[:, :, 1], stats[:, :, 4], ALU.subtract))
                line.link(nc.vector.scalar_tensor_tensor(out=e["dev"][:], in0=e["dev"][:], scalar=0.25, in1=e["dev"][:],
                                                         op0=ALU.mult, op1=ALU.mult))
                line.link(nc.vector.tensor_tensor(e["std"][:], stats[:, :, 2], stats[:, :, 5], ALU.add))
                nc.vector.scalar_tensor_tensor(out=e["dev"][:], in0=e["std"][:], scalar=1.0 / D, in1=e["dev"][:],
                                               op0=ALU.mult, op1=ALU.add).then_inc(e["var_ready"], 1)
                line.link(nc.vector.tensor_tensor(m, m, tiled(e["mean"][:]), ALU.subtract))
                dve.wait_ge(e["std_ready"], k + 1)
                line.link(nc.vector.reciprocal(e["std"][:], e["std"][:]))
                line.link(nc.vector.tensor_tensor(m, m, tiled(e["std"][:]), ALU.mult))
                line.link(nc.vector.tensor_tensor(m, m, rowed(e["gamma"][:]), ALU.mult))
                line.link(nc.vector.tensor_tensor(m, m, rowed(e["beta"][:]), ALU.add))
                line.link(nc.vector.tensor_tensor(x[:, tiles, :], x[:, tiles, :], m, ALU.add))

            def root(act, e, k):
                act.wait_ge(e["var_ready"], k + 1)
                act.activation(e["std"][:], e["dev"][:], ACT.Sqrt, bias=e["eps"][:, 0:1]).then_inc(e["std_ready"], 1)

            def act_body(act, k, s, first, e):
                linear_act(act, k, s, first, e)
                if not first:
                    root(act, e, k - 1)

            def pe_start(pe, e):
                pe.wait_ge(e["loaded"], 64)
                nc.tensor.transpose(e["lin_ps"][:, 0, :], e["wo"][:], ident[:]).then_inc(e["w_turned"], 1)
                pe.wait_ge(e["w_ready"], 1)

            node_totals("nodes2", s2_d, D, D, 1, 0, 1 + 5 + 5 + 6, scratch, consts, early, late, act_body, linear_pe, pe_start,
                        lambda act, e: root(act, e, NG - 1))

        def heads_of(ap):
            return ap.rearrange("p j (k d) -> p j k d", k=K3)

        def gat_tables(name, g, xw, selfs, first):
            w_in, a_src_in, a_dst_in = g[0], g[1], g[2]
            st = Stage(name)
            with st:
                w = sb("w", [P, D], F32, st)
                a_src = sb("a_src", [P, D], F32, st)
                a_dst = sb("a_dst", [P, D], F32, st)
                left = sb("left", [P, 2, GN, D], F32, st)
                left_t = sb("left_t", [P, 2, GN, D], F32, st)
                made = sb("made", [P, 2, GN, WG], F32, st)
                prod = sb("prod", [P, 2, GN, D], F32, st)
                zeros = sb("zeros", [P, C, K3], F32, st) if first else None
                start_slot = sb("start_slot", [P, 2, GN], I32, st)
                pair = sb("pair", [P, 2, GN, 2 * K3], F32, st)
                turn_ps = pb("turn_ps", [P, GN, D], st)
                lin_ps = [pb(f"lin_ps{s}", [P, GN, D], st) for s in range(2)]
                loaded, copied, turned, evacuated = sem("loaded", st), sem("copied", st), sem("turned", st), sem("evacuated", st)
                multiplied, made_ready, dve_steps = sem("multiplied", st), sem("made_ready", st), sem("dve_steps", st)
                zeroed, zeros_out, staged, selfs_saved = sem("zeroed", st), sem("zeros_out", st), sem("staged", st), sem("selfs_saved", st)
                saved = [sem(f"saved{s}", st) for s in range(2)]
                put, g0 = gathered, gathered_before(2, GN * NG // 2)
                per = 7
                with nc.Block() as block:
                    @block.sync
                    def _(sp):
                        sp.dma_start(w[:], w_in).then_inc(loaded, 16)
                        for tile, src in ((a_src, a_src_in), (a_dst, a_dst_in)):
                            sp.dma_start(tile[:], src.rearrange("(a k) d -> a (k d)", a=1).to_broadcast([P, D])).then_inc(loaded, 16)
                        if first:
                            sp.wait_ge(zeroed, 1)
                            sp.dma_start(start_rows_d.rearrange("(p c) f -> p (c f)", c=C),
                                         zeros[:].rearrange("p c f -> p (c f)")).then_inc(zeros_out, 16)
                            sp.wait_ge(zeros_out, 16)
                        view = xw_d.rearrange("(p t) f -> p t f", t=T)
                        with sp.Fori(0, NG // 2) as i:
                            for s in range(2):
                                t0 = sp.snap((i * 2 + s) * GN)
                                sp.wait_ge(made_ready, i * 2 + s + 1)
                                sp.sem_inc(sp_gate, 1)
                                sp.dma_start(view[:, bass.ds(t0, GN), :], made[:, s, :, :]).then_inc(saved[s], 16)
                        sp.wait_ge(made_ready, NG)
                        sp.dma_start(self_d.rearrange("(p t) f -> p t f", t=T), selfs[:]).then_inc(selfs_saved, 16)
                        for s in range(2):
                            sp.wait_ge(saved[s], 16 * (NG // 2))
                        sp.wait_ge(selfs_saved, 16)

                    @block.scalar
                    def _(act):
                        def copy(k, s):
                            act.activation(left[:, s, :, :], h[:, bass.ds(k * GN, GN), :], ACT.Copy).then_inc(copied, 1)

                        def turn(i, first, last):
                            for s in range(2):
                                k = i * 2 + s
                                if not (last and s):
                                    copy(k + 1, 1 - s)
                                if not first:
                                    act.wait_ge(put[s], i * (16 * GN) + g0[s])
                                    act.sem_inc(act_gate, 1)
                                act.activation(start_slot[:, s, :], start_i[:, bass.ds(k * GN, GN)], ACT.Copy).then_inc(staged, 1)
                                act.wait_ge(turned, k + 1)
                                if not first:
                                    act.wait_ge(multiplied, k - 1)
                                act.activation(left_t[:, s, :, :], turn_ps[:], ACT.Copy).then_inc(evacuated, 1)
                        copy(0, 0)
                        turn(0, True, False)
                        with act.Fori(1, NG // 2 - 1) as i:
                            turn(i, False, False)
                        turn(NG // 2 - 1, False, True)

                    @block.gpsimd
                    def _(pool):
                        if first:
                            pool.wait_ge(zeros_out, 16)
                        with pool.Fori(0, NG // 2) as i:
                            for s in range(2):
                                pool.wait_ge(staged, i * 2 + s + 1)
                                pool.sem_inc(pool_gate, 1)
                                pool.wait_ge(made_ready, i * 2 + s + 1)
                                pool.sem_inc(pool_gate, 1)
                                for j in range(GN):
                                    nc.gpsimd.indirect_dma_start(
                                        out=start_rows_d, in_=pair[:, s, j, 0:K3], in_offset=None,
                                        out_offset=bass.IndirectOffsetOnAxis(ap=start_slot[:, s, j:j + 1], axis=0),
                                        bounds_check=EP - 1, oob_is_err=False).then_inc(put[s], 16)
                        for s in range(2):
                            pool.wait_ge(put[s], g0[s] + 16 * GN * (NG // 2))

                    @block.tensor
                    def _(pe):
                        pe.wait_ge(loaded, 48)

                        def transpose(k, s, first):
                            pe.wait_ge(copied, k + 1)
                            if not first:
                                pe.wait_ge(evacuated, k)
                            for j in range(GN):
                                ins = nc.tensor.transpose(turn_ps[:, j, :], left[:, s, j, :], ident[:])
                            ins.then_inc(turned, 1)

                        def turn(i, first, last):
                            for s in range(2):
                                k = i * 2 + s
                                if last and s:
                                    pe.wait_ge(evacuated, k + 1)
                                else:
                                    transpose(k + 1, 1 - s, False)
                                if not first:
                                    pe.wait_ge(made_ready, k - 1)
                                for j in range(GN):
                                    ins = nc.tensor.matmul(lin_ps[s][:, j, :], left_t[:, s, j, :], w[:], start=True, stop=True)
                                ins.then_inc(multiplied, 1)
                        transpose(0, 0, True)
                        turn(0, True, False)
                        with pe.Fori(1, NG // 2 - 1) as i:
                            turn(i, False, False)
                        turn(NG // 2 - 1, False, True)

                    @block.vector
                    def _(dve):
                        line = Line(dve, dve_steps)
                        if first:
                            nc.vector.memset(zeros[:], 0.0).then_inc(zeroed, 1)
                        line.link(nc.vector.memset(made[:], 1.0))
                        base = line.n
                        dve.wait_ge(loaded, 48)

                        def group(i, s, begin):
                            k = i * 2 + s
                            tiles = bass.ds(k * GN, GN)
                            m = heads_of(made[:, s, :, 0:WS3])[:, :, :, 0:D3]
                            line.n = k * per + base
                            if not begin:
                                dve.wait_ge(saved[s], i * 16)
                                dve.wait_ge(put[s], i * (16 * GN) + g0[s])
                            dve.wait_ge(multiplied, k + 1)
                            line.mark(nc.vector.tensor_copy(m, lin_ps[s][:].rearrange("p j (k d) -> p j k d", k=K3)))
                            for n, a in ((0, a_src), (1, a_dst)):
                                line.mark(nc.vector.tensor_tensor(prod[:, n, :, :], lin_ps[s][:], a[:].unsqueeze(1).to_broadcast([P, GN, D]), ALU.mult))
                            dve.wait_ge(line.sem, line.n)
                            for n, o in ((0, made[:, s, :, WS3:WG]), (1, pair[:, s, :, 0:K3])):
                                line.mark(nc.vector.tensor_reduce(o, prod[:, n, :, :].rearrange("p j (k d) -> p j k d", k=K3), AX.X, ALU.add))
                            dve.wait_ge(line.sem, line.n)
                            nc.vector.tensor_copy(xw[:, tiles, :], made[:, s, :, 0:WS3])
                            own = pair[:, s, :, K3:2 * K3]
                            line.link(nc.vector.tensor_tensor(own, made[:, s, :, WS3:WG], pair[:, s, :, 0:K3], ALU.add))
                            line.link(nc.vector.scalar_tensor_tensor(out=own, in0=own, scalar=0.2, in1=own, op0=ALU.mult, op1=ALU.max))
                            nc.vector.tensor_copy(selfs[:, tiles, :], pair[:, s, :, :]).then_inc(made_ready, 1)
                        for s in range(2):
                            group(0, s, True)
                        with dve.Fori(1, NG // 2) as i:
                            for s in range(2):
                                group(i, s, False)

        def gat_sum(name, layer):
            st = Stage(name)
            with st:
                idx_slot = sb("idx_slot", [P, BS * NS, G], I32, st)
                rows = sb("rows", [P, BS * NS, G, WG], F32, st)
                sums = sb("sums", [P, BS, BW, WG], F32, st)
                held = sb("held", [P, K3, C], F32, st)
                initial = sb("initial", [P, 2 * K3], F32, st)
                stay = sb("stay", [P, BS, BW + 1], F32, st)
                logit = sb("logit", [P, K3, BW], F32, st)
                top = sb("top", [P, BS, K3, BW], F32, st)
                weight = sb("weight", [P, K3, BW + 1], F32, st)
                before = sb("before", [P, WS3], F32, st)
                got_start, got_initial = sem("got_start", st), initial_gathered
                got, g0 = gathered, gathered_before(BS * NS, C // (BS * NS))
                idx_ready, stay_ready, dve_steps = sem("idx_ready", st), sem("stay_ready", st), sem("dve_steps", st)
                shifted, exped, topped, summed = sem("shifted", st), sem("exped", st), sem("topped", st), sem("summed", st)
                stored = [sem(f"stored{b}", st) for b in range(BS)]
                at_start = sums[:].rearrange("p b c f -> p (b c f)")[:, 0:C * K3]
                with nc.Block() as block:
                    @block.gpsimd
                    def _(pool):
                        nc.gpsimd.indirect_dma_start(out=initial[:], out_offset=None, in_=self_d,
                                                     in_offset=bass.IndirectOffsetOnAxis(ap=dst0_i[:], axis=0)).then_inc(got_initial, 16)

                        def turn(i, first):
                            for s in range(BS * NS):
                                pool.wait_ge(idx_ready, (i * BS + s // NS) * NS + (s % NS + 1))
                                if not first:
                                    pool.sem_inc(pool_gate, 1)
                                    pool.wait_ge(summed, i * (BS * BW) + ((s + 1) * G - BS * BW))
                                pool.sem_inc(pool_gate, 1)
                                for j in range(G):
                                    nc.gpsimd.indirect_dma_start(
                                        out=rows[:, s, j, :], out_offset=None, in_=xw_d,
                                        in_offset=bass.IndirectOffsetOnAxis(ap=idx_slot[:, s, j:j + 1], axis=0)).then_inc(got[s], 16)
                        turn(0, True)
                        with pool.Fori(1, BTURNS) as i:
                            turn(i, False)

                    @block.scalar
                    def _(act):
                        def stage_stay(b, cols):
                            act.activation(stay[:, b, 0:BW], cont[:, cols], ACT.Copy, bias=LOW, scale=-LOW).then_inc(stay_ready, 1)

                        def stage_idx(s, cols):
                            act.activation(idx_slot[:, s, :], src_i[:, cols], ACT.Copy).then_inc(idx_ready, 1)

                        for s in range(BS * NS):
                            stage_idx(s, slice(s * G, (s + 1) * G))
                        for b in range(BS):
                            stage_stay(b, slice(b * BW, (b + 1) * BW))

                        def turn(i, first, last):
                            for b in range(BS):
                                k = i * BS + b
                                if not last:
                                    for s in range(b * NS, (b + 1) * NS):
                                        act.wait_ge(got[s], i * (16 * G) + (g0[s] + 16 * G))
                                        act.sem_inc(act_gate, 1)
                                        stage_idx(s, bass.ds((i + 1) * (BS * BW) + s * G, G))
                                act.wait_ge(shifted, k + 1)
                                act.activation(weight[:], weight[:], ACT.Exp).then_inc(exped, 1)
                                if not last:
                                    stage_stay(b, bass.ds((i + 1) * (BS * BW) + b * BW, BW))
                                if not first:
                                    act.wait_ge(stored[b], i * 16)
                                act.activation(sums[:, b, :, WS3:WG], top[:, b, :, :].rearrange("p k j -> p j k"), ACT.Copy).then_inc(topped, 1)
                        turn(0, True, False)
                        with act.Fori(1, BTURNS - 1) as i:
                            turn(i, False, False)
                        turn(BTURNS - 1, False, True)

                    @block.vector
                    def _(dve):
                        line = Line(dve, dve_steps)
                        line.link(nc.vector.memset(stay[:, :, BW:BW + 1], LOW))
                        dve.wait_ge(got_start, 16)
                        dve.wait_ge(got_initial, 16 * (layer + 1))
                        for k in range(K3):
                            line.mark(nc.vector.tensor_tensor_scan(held[:, k, :], cont[:],
                                                                   at_start.rearrange("p (c f) -> p c f", f=K3)[:, :, k],
                                                                   initial[:, k:k + 1], ALU.mult, ALU.add))
                        dve.wait_ge(line.sem, line.n)
                        line.mark(nc.vector.memset(top[:, BS - 1, :, BW - 1:BW], LOW))
                        line.link(nc.vector.memset(sums[:, BS - 1, BW - 1, 0:WS3], 0.0))
                        base, per = line.n, 14

                        def block_of_columns(i, b, first):
                            k = i * BS + b
                            line.n = k * per + base
                            pb_ = (b - 1) % BS
                            rows_b = rows[:, b * NS:(b + 1) * NS, :, :].rearrange("p s j f -> p (s j) f")
                            for s in range(b * NS, (b + 1) * NS):
                                dve.wait_ge(got[s], i * (16 * G) + (g0[s] + 16 * G))
                            line.link(nc.vector.tensor_tensor(logit[:], rows_b[:, :, WS3:WG].rearrange("p j k -> p k j"),
                                                              held[:, :, bass.ds(k * BW, BW)], ALU.add))
                            line.link(nc.vector.scalar_tensor_tensor(out=logit[:], in0=logit[:], scalar=0.2, in1=logit[:],
                                                                     op0=ALU.mult, op1=ALU.max))
                            dve.wait_ge(stay_ready, k + 1)
                            if not first:
                                dve.wait_ge(topped, k - 1)
                            for n in range(K3):
                                line.mark(nc.vector.tensor_tensor_scan(top[:, b, n, :], stay[:, b, 0:BW], logit[:, n, :],
                                                                       top[:, pb_, n, BW - 1:BW], ALU.add, ALU.max))
                            dve.wait_ge(line.sem, line.n)
                            for n in range(K3):
                                line.mark(nc.vector.tensor_tensor_scan(top[:, b, n, ::-1], stay[:, b, 1:BW + 1][:, ::-1],
                                                                       top[:, b, n, ::-1], LOW, ALU.add, ALU.max))
                            dve.wait_ge(line.sem, line.n)
                            line.mark(nc.vector.tensor_tensor(weight[:, :, 0:BW], logit[:], top[:, b, :, :], ALU.subtract))
                            line.link(nc.vector.tensor_tensor(weight[:, :, BW:BW + 1], top[:, pb_, :, BW - 1:BW], top[:, b, :, 0:1], ALU.subtract))
                            nc.vector.tensor_scalar(weight[:, :, BW], weight[:, :, BW], 0.0, None, ALU.min).then_inc(shifted, 1)
                            dve.wait_ge(exped, k + 1)
                            line.mark(nc.vector.tensor_tensor(
                                before[:].rearrange("p (k d) -> p k d", k=K3), sums[:, pb_, BW - 1, 0:WS3].rearrange("p (k d) -> p k d", k=K3),
                                weight[:, :, BW:BW + 1].to_broadcast([P, K3, WH]), ALU.mult))
                            line.link(nc.vector.tensor_tensor(
                                heads_of(rows_b[:, :, 0:WS3]), heads_of(rows_b[:, :, 0:WS3]),
                                over_heads(weight[:, :, 0:BW].rearrange("p k j -> p j k"), K3, WH), ALU.mult))
                            if not first:
                                dve.wait_ge(stored[b], i * 16)
                            for j in range(BW):
                                if j:
                                    dve.wait_ge(summed, i * (BS * BW) + (b * BW + j))
                                nc.vector.scalar_tensor_tensor(
                                    out=sums[:, b, j, 0:WS3], in0=sums[:, b, j - 1, 0:WS3] if j else before[:],
                                    scalar=cont[:, bass.ds(k * BW + j, 1)], in1=rows_b[:, j, 0:WS3],
                                    op0=ALU.mult, op1=ALU.add).then_inc(summed, 1)
                            dve.wait_ge(summed, (k + 1) * BW)
                        for b in range(BS):
                            block_of_columns(0, b, True)
                        with dve.Fori(1, BTURNS) as i:
                            for b in range(BS):
                                block_of_columns(i, b, False)
                        dve.wait_ge(topped, BTURNS * BS)
                        nc.vector.tensor_copy(carry[:, 0:WG], sums[:, BS - 1, BW - 1, :])

                    @block.sync
                    def _(sp):
                        sp.dma_start(at_start, start_rows_d.rearrange("(p c) f -> p (c f)", c=C)).then_inc(got_start, 16)
                        view = s3_d.rearrange("(p c) f -> p c f", c=C)
                        with sp.Fori(0, BTURNS) as i:
                            for b in range(BS):
                                c0 = sp.snap((i * BS + b) * BW)
                                sp.wait_ge(summed, (i * BS + b + 1) * BW)
                                sp.sem_inc(sp_gate, 1)
                                sp.wait_ge(topped, i * BS + b + 1)
                                sp.sem_inc(sp_gate, 1)
                                sp.dma_start(view[:, bass.ds(c0, BW), :], sums[:, b, :, :]).then_inc(stored[b], 16)
                        for b in range(BS):
                            sp.wait_ge(stored[b], 16 * BTURNS)

        def gat_chain(name):
            HALF = WS3 // 2
            st = Stage(name)
            with st:
                pen_single = sb("pen_single", [P, P], F32, st)
                pen_first = sb("pen_first", [P, 1], F32, st)
                chained = sb("chained", [K3, P + 1], F32, st)
                ahead = sb("ahead", [P, 2, K3], F32, st)
                scale = sb("scale", [P, 2, K3], F32, st)
                keep = sb("keep", [P, WS3], F32, st)
                own = sb("own", [P, WS3], F32, st)
                keep_t = sb("keep_t", [HALF, P], F32, st)
                turned = sb("turned", [HALF, P + 1], F32, st)
                max_ps = pb("max_ps", [K3, P], st)
                ahead_ps = pb("ahead_ps", [P, 2, K3], st)
                keep_ps = pb("keep_ps", [HALF, P], st)
                own_ps = pb("own_ps", [HALF, P], st)
                back_ps = pb("back_ps", [P, HALF], st)
                dve_steps, pe_done, ready, exped = sem("dve_steps", st), sem("pe_done", st), sem("ready", st), sem("exped", st)
                with nc.Block() as block:
                    @block.tensor
                    def _(pe):
                        nc.tensor.transpose(max_ps[:], carry[:, WS3:WG], ident[:]).then_inc(pe_done, 1)
                        pe.wait_ge(ready, 1)
                        nc.tensor.transpose(ahead_ps[:, 0, :], chained[:, 0:P], ident[0:K3, 0:K3])
                        nc.tensor.transpose(ahead_ps[:, 1, :], chained[:, 1:P + 1], ident[0:K3, 0:K3]).then_inc(pe_done, 1)
                        pe.wait_ge(ready, 3)
                        for n in range(2):
                            if n:
                                pe.wait_ge(ready, 5)
                            cols = slice(n * HALF, (n + 1) * HALF)
                            nc.tensor.transpose(keep_ps[:], keep[:, cols], ident[:])
                            nc.tensor.transpose(own_ps[:], own[:, cols], ident[:]).then_inc(pe_done, 1)
                            pe.wait_ge(ready, 4 + 2 * n)
                            nc.tensor.transpose(back_ps[:], turned[:, 0:P], ident[0:HALF, 0:HALF]).then_inc(pe_done, 1)

                    @block.scalar
                    def _(act):
                        act.wait_ge(ready, 2)
                        act.activation(scale[:], scale[:], ACT.Exp).then_inc(exped, 1)

                    @block.vector
                    def _(dve):
                        line = Line(dve, dve_steps)
                        for tile, mask in ((pen_single[:], single_row[:]), (pen_first[:], in_first[:, C - 1:C])):
                            line.mark(nc.vector.tensor_scalar(tile, mask, -1.0, -LOW, ALU.add, ALU.mult))
                        line.link(nc.vector.memset(chained[:, 0:1], LOW))
                        dve.wait_ge(pe_done, 1)
                        nc.vector.tensor_tensor_scan(chained[:, 1:P + 1], pen_single[0:K3, :], max_ps[:], LOW,
                                                     ALU.add, ALU.max).then_inc(ready, 1)
                        dve.wait_ge(pe_done, 2)
                        line.link(nc.vector.tensor_copy(ahead[:], ahead_ps[:]))
                        line.mark(nc.vector.scalar_tensor_tensor(out=scale[:, 0, :], in0=ahead[:, 0, :], scalar=pen_first[:, 0:1],
                                                                 in1=ahead[:, 1, :], op0=ALU.add, op1=ALU.subtract))
                        line.link(nc.vector.tensor_tensor(scale[:, 1, :], carry[:, WS3:WG], ahead[:, 1, :], ALU.subtract))
                        nc.vector.tensor_scalar(scale[:], scale[:], 0.0, None, ALU.min).then_inc(ready, 1)
                        dve.wait_ge(exped, 1)

                        def wide(ap):
                            return ap.unsqueeze(2).to_broadcast([P, K3, WH])
                        line.mark(nc.vector.tensor_copy(keep[:].rearrange("p (k d) -> p k d", k=K3), wide(scale[:, 0, :])))
                        line.mark(nc.vector.tensor_copy(carry[:, WS3:WG], ahead[:, 0, :]))
                        nc.vector.tensor_tensor(own[:].rearrange("p (k d) -> p k d", k=K3),
                                                carry[:, 0:WS3].rearrange("p (k d) -> p k d", k=K3), wide(scale[:, 1, :]),
                                                ALU.mult).then_inc(ready, 1)
                        line.link(nc.vector.memset(turned[:, 0:1], 0.0))
                        for n in range(2):
                            dve.wait_ge(pe_done, 3 + 2 * n)
                            line.link(nc.vector.tensor_copy(keep_t[:], keep_ps[:]))
                            nc.vector.tensor_tensor_scan(turned[:, 1:P + 1], keep_t[:], own_ps[:], 0.0,
                                                         ALU.mult, ALU.add).then_inc(ready, 1)
                            dve.wait_ge(pe_done, 4 + 2 * n)
                            nc.vector.tensor_copy(carry[:, n * HALF:(n + 1) * HALF], back_ps[:]).then_inc(ready, 1)

        def gat_nodes(name, g, xw, selfs):
            def scratch(st):
                e = {"bias": sb("bias", [P, D], F32, st), "loaded": sem("loaded", st),
                     "logit_ready": sem("logit_ready", st), "exped": sem("exped", st)}
                for k in ("last", "earlier"):
                    e[k] = sb(k, [P, 2, GN, WS3], F32, st)
                e["own"] = sb("own", [P, GN, WS3], F32, st)
                e["scale"] = sb("scale", [P, 2, GN, 3 * K3], F32, st)
                e["top"] = sb("top", [P, 2, GN, K3], F32, st)

                def prepare(dve, line):
                    dve.wait_ge(e["loaded"], 16)
                e["prepare"] = prepare
                return e

            def consts(sp, e):
                sp.dma_start(e["bias"][:], g[3].rearrange("(a f) -> a f", a=1).to_broadcast([P, D])).then_inc(e["loaded"], 16)
                sp.wait_ge(e["loaded"], 16)

            def of_heads(ap):
                return ap.unsqueeze(2).to_broadcast([P, GN, K3])

            def early(dve, line, k, s, total, reach, e):
                tiles = bass.ds(k * GN, GN)
                scale, top = e["scale"][:, s, :, :], e["top"][:, s, :, :]
                line.mark(nc.vector.tensor_tensor(scale[:, :, 0:K3], total[:, :, WS3:WG], of_heads(low_without[:, tiles]), ALU.add))
                line.mark(nc.vector.tensor_tensor(scale[:, :, K3:2 * K3], reach[:, :, WS3:WG], of_heads(low_unreached[:, tiles]), ALU.add))
                line.link(nc.vector.tensor_copy(scale[:, :, 2 * K3:3 * K3], selfs[:, tiles, K3:2 * K3]))
                line.link(nc.vector.tensor_tensor(top, scale[:, :, 0:K3], scale[:, :, K3:2 * K3], ALU.max))
                line.link(nc.vector.tensor_tensor(top, top, scale[:, :, 2 * K3:3 * K3], ALU.max))
                nc.vector.tensor_tensor(scale.rearrange("p j (a k) -> p j a k", a=3), scale.rearrange("p j (a k) -> p j a k", a=3),
                                        top.unsqueeze(2).to_broadcast([P, GN, 3, K3]), ALU.subtract).then_inc(e["logit_ready"], 1)
                nc.vector.tensor_copy(e["last"][:, s, :, :], total[:, :, 0:WS3])
                nc.vector.tensor_copy(e["earlier"][:, s, :, :], reach[:, :, 0:WS3]).then_inc(e["taken"], 1)

            def late(dve, line, k, s, e):
                tiles = bass.ds(k * GN, GN)
                scale, top = e["scale"][:, s, :, :], e["top"][:, s, :, :]
                last, earlier, own = e["last"][:, s, :, :], e["earlier"][:, s, :, :], e["own"]
                dve.wait_ge(e["taken"], k + 1)
                dve.wait_ge(e["exped"], k + 1)
                for n, (part, values) in enumerate(((last, last), (earlier, earlier), (own[:], xw[:, tiles, :]))):
                    line.mark(nc.vector.tensor_tensor(heads_of(part), heads_of(values),
                                                      over_heads(scale[:, :, n * K3:(n + 1) * K3], K3, WH), ALU.mult))
                dve.wait_ge(line.sem, line.n)
                line.link(nc.vector.tensor_tensor(last, last, earlier, ALU.add))
                line.link(nc.vector.tensor_tensor(last, last, own[:], ALU.add))
                line.link(nc.vector.reciprocal(top, heads_of(last)[:, :, :, D3]))
                features = own[:, :, 0:D].rearrange("p j (k d) -> p j k d", k=K3)
                line.link(nc.vector.tensor_tensor(features, heads_of(last)[:, :, :, 0:D3], over_heads(top, K3, D3), ALU.mult))
                line.link(nc.vector.tensor_tensor(h[:, tiles, :], own[:, :, 0:D], e["bias"][:].unsqueeze(1).to_broadcast([P, GN, D]), ALU.add))

            def act_body(act, k, s, first, e):
                act.wait_ge(e["logit_ready"], k + 1)
                act.activation(e["scale"][:, s, :, :], e["scale"][:, s, :, :], ACT.Exp).then_inc(e["exped"], 1)

            node_totals(name, s3_d, WG, WG, 0, 5, 8, scratch, consts, early, late, act_body)

        def batch_norm_elu(name, g, last):
            st = Stage(name)
            with st:
                squares = sb("squares", [P, T, D], F32, st)
                part = sb("part", [P, D], F32, st)
                valid = sb("valid", [P, P], F32, st)
                mean = sb("mean", [P, D], F32, st)
                std = sb("std", [P, D], F32, st)
                gamma = sb("gamma", [P, D], F32, st)
                beta = sb("beta", [P, D], F32, st)
                eps = sb("eps", [P, 1], F32, st)
                real = sb("real", [P, 1], F32, st)
                tot_ps = pb("tot_ps", [P, D], st)
                loaded, part_ready, totalled, dve_steps = sem("loaded", st), sem("part_ready", st), sem("totalled", st), sem("dve_steps", st)
                std_ready, low_ready, exped = sem("std_ready", st), sem("low_ready", st), sem("exped", st)

                def all_tiles(ap):
                    return ap.unsqueeze(1).to_broadcast([P, T, D])

                with nc.Block() as block:
                    @block.sync
                    def _(sp):
                        for tile, src in ((gamma, g[4]), (beta, g[5])):
                            sp.dma_start(tile[:], src.rearrange("(a f) -> a f", a=1).to_broadcast([P, D])).then_inc(loaded, 16)
                        sp.wait_ge(loaded, 32)

                    @block.tensor
                    def _(pe):
                        for n in range(2):
                            pe.wait_ge(part_ready, n + 1)
                            nc.tensor.matmul(tot_ps[:], valid[:], part[:], start=True, stop=True).then_inc(totalled, 1)

                    @block.scalar
                    def _(act):
                        act.wait_ge(totalled, 2)
                        act.activation(std[:], tot_ps[:], ACT.Sqrt, bias=eps[:, 0:1], scale=1.0 / N).then_inc(std_ready, 1)
                        act.wait_ge(low_ready, 1)
                        act.activation(squares[:], squares[:], ACT.Exp).then_inc(exped, 1)

                    @block.vector
                    def _(dve):
                        line = Line(dve, dve_steps)
                        line.link(nc.vector.memset(eps[:], LN_EPS))
                        line.link(nc.vector.tensor_scalar(real[:], lane[:], float(PN), None, ALU.is_lt))
                        line.link(nc.vector.tensor_copy(valid[:], real[:].to_broadcast([P, P])))
                        nc.vector.tensor_reduce(part[:], h[:].rearrange("p t f -> p f t"), AX.X, ALU.add).then_inc(part_ready, 1)
                        dve.wait_ge(totalled, 1)
                        line.link(nc.vector.tensor_scalar(mean[:], tot_ps[:], 1.0 / N, None, ALU.mult))
                        line.link(nc.vector.tensor_tensor(h[:], h[:], all_tiles(mean[:]), ALU.subtract))
                        line.link(nc.vector.tensor_tensor(squares[:], h[:], h[:], ALU.mult))
                        nc.vector.tensor_reduce(part[:], squares[:].rearrange("p t f -> p f t"), AX.X, ALU.add).then_inc(part_ready, 1)
                        dve.wait_ge(std_ready, 1)
                        line.link(nc.vector.reciprocal(std[:], std[:]))
                        dve.wait_ge(loaded, 32)
                        line.link(nc.vector.tensor_tensor(std[:], std[:], gamma[:], ALU.mult))
                        line.link(nc.vector.tensor_tensor(h[:], h[:], all_tiles(std[:]), ALU.mult))
                        line.link(nc.vector.tensor_tensor(h[:], h[:], all_tiles(beta[:]), ALU.add))
                        nc.vector.tensor_scalar(squares[:], h[:], 0.0, None, ALU.min).then_inc(low_ready, 1)
                        line.link(nc.vector.tensor_scalar(h[:], h[:], 0.0, None, ALU.max))
                        dve.wait_ge(exped, 1)
                        line.link(nc.vector.scalar_tensor_tensor(out=h[:], in0=squares[:], scalar=-1.0, in1=h[:], op0=ALU.add, op1=ALU.add))
                        if last:
                            line.link(nc.vector.tensor_tensor(x[:], x[:], h[:], ALU.add))

        def finish():
            st = Stage("finish")
            with st:
                written = sem("written", st)
                with nc.Block() as block:
                    @block.sync
                    def _(sp):
                        ov = out.rearrange("(p t) f -> p t f", t=T)
                        sp.dma_start(ov[0:112], x[0:112, :, :]).then_inc(written, 16)
                        sp.dma_start(ov[112:PN], x[112:PN, :, :]).then_inc(written, 16)
                        sp.wait_ge(written, 32)

        setup()
        norm_relu("norm0", h0_d)
        gather_sum("sum0", h0_d, s0_d, True)
        chain_runs("chain0", [(0, D, False), (D, D, True)])
        layer0_nodes()
        norm_relu("norm1", h1_d)
        gather_sum("sum1", h1_d, s1_d, False, layer1_own)
        chain_runs("chain1", [(0, D, False)])
        layer1_nodes()
        norm_relu("norm2", None)
        relation_tables()
        with ExitStack() as keep:
            weights = sb("weights2", [P, K2, C], F32, keep)
            with ExitStack() as short:
                logits = sb("logits2", [P, K2, C], F32, short)
                relation_logits(logits)
                relation_softmax(logits, weights)
            weighted_sum("sum2", v_d, s2_d, weights, K2)
        chain_runs("chain2", [(0, D, False)])
        layer2_nodes()
        renew_semaphores()
        norm_relu("norm3", None)
        with ExitStack() as keep:
            xw = sb("xw", [P, T, WS3], F32, keep)
            selfs = sb("selfs", [P, T, 2 * K3], F32, keep)
            for n, g in enumerate(g3):
                if n:
                    renew_semaphores()
                gat_tables(f"tables3{n}", g, xw, selfs, n == 0)
                gat_sum(f"sum3{n}", n)
                gat_chain(f"chain3{n}")
                gat_nodes(f"nodes3{n}", g, xw, selfs)
                batch_norm_elu(f"bn3{n}", g, n == 1)
        finish()


_INS = ['x', 'src', 'dst', 'edge_type_5', 'L0_gnn_z_agg_hard', 'L1_gnn_W', 'L1_gnn_b', 'L2_gnn_W_Q', 'L2_gnn_W_K',
        'L2_gnn_W_V', 'L2_gnn_attn_bias', 'L2_gnn_out_proj_w', 'L2_gnn_out_proj_b', 'L2_gnn_ln_gamma',
        'L2_gnn_ln_beta', 'L3_gnn_W1', 'L3_gnn_a1_src', 'L3_gnn_a1_dst', 'L3_gnn_b1', 'L3_gnn_g1', 'L3_gnn_beta1',
        'L3_gnn_W2', 'L3_gnn_a2_src', 'L3_gnn_a2_dst', 'L3_gnn_b2', 'L3_gnn_g2', 'L3_gnn_beta2']


def kernel(**inputs):
    import numpy as _np
    import concourse.bacc as _bacc
    from concourse import mybir as _mybir
    from concourse.bass_utils import run_bass_kernel_spmd as _run

    nc = _bacc.Bacc("TRN2", target_bir_lowering=False, num_devices=1)
    arrays, args = {}, []
    for name in _INS:
        a = _np.ascontiguousarray(inputs[name])
        arrays[f"in_{name}_dram"] = a
        args.append(nc.dram_tensor(f"in_{name}_dram", a.shape, _mybir.dt.from_np(a.dtype), kind="ExternalInput").ap())
    result = nc.dram_tensor("out_0_dram", (N, D), _mybir.dt.float32, kind="ExternalOutput").ap()
    build(nc, *args[:15], [args[15:21], args[21:27]], result)
    r = _run(nc, [arrays], core_ids=[0])
    return r.results[0]["out_0_dram"]
```
